# Optimizing a Trainium2 kernel written in Bass

```python
import numpy as np
import jax
import jax.numpy as jnp

def _softmax(x, axis=-1):
    return jax.nn.softmax(x, axis=axis)

def _gelu(x):
    return jax.nn.gelu(x, approximate=True)

def _silu(x):
    return jax.nn.silu(x)

def _sigmoid(x):
    return jax.nn.sigmoid(x)

def _layernorm(x, axis=-1, eps=1e-05):
    m = jnp.mean(x, axis=axis, keepdims=True)
    v = jnp.var(x, axis=axis, keepdims=True)
    return (x - m) / jnp.sqrt(v + eps)

def _scatter_add(tgt, idx, src, axis=0):
    return tgt.at[idx].add(src)

def _segment_sum(src, seg, n):
    return jax.ops.segment_sum(src, seg, n)
kernel_name = 'mk_gps_d2_gnn_r32_20c6ea'

def setup_inputs(seed: int=0):
    np.random.seed(seed)
    _w = jnp.asarray

    def _rec_inputs():
        import jax
        import jax.numpy as jnp
        _gk = jax.random.key(seed)
        x = -0.0003713 + 1 * jax.random.normal(jax.random.fold_in(_gk, 1), (3125, 256), jnp.float32)
        src = jax.random.randint(jax.random.fold_in(_gk, 2), (50000,), 0, 3125, jnp.int32)
        dst = jnp.minimum((3125 * jax.random.uniform(jax.random.fold_in(_gk, 3), (50000,)) ** 2.0).astype(jnp.int32), 99999)
        _o = jnp.argsort(dst, stable=True)
        src = src[_o]
        dst = dst[_o]
        return (x, src, dst)
    x, src, dst = _rec_inputs()

    def _L0_gnn_setup():
        import jax, jax.numpy as jnp
        import numpy as np
        N_NODES = 50000
        N_EDGES = 25000
        D_IN = 256
        D_HID = 256
        D_OUT = 256

        def _sage_conv(x, src, dst, Wl, bl, Wr, num_nodes):
            msg = x[src]
            agg = jax.ops.segment_sum(msg, dst, num_segments=num_nodes)
            deg = jax.ops.segment_sum(jnp.ones((src.shape[0],), x.dtype), dst, num_segments=num_nodes)
            mean = agg / jnp.maximum(deg, 1.0)[:, None]
            return jnp.einsum('nd,od->no', mean, Wl) + bl + jnp.einsum('nd,od->no', x, Wr)
        key = jax.random.key(seed)
        ks = jax.random.split(key, 12)
        x = jax.random.normal(ks[0], (N_NODES, D_IN), dtype=jnp.float32)
        edge_index = jax.random.randint(ks[1], (2, N_EDGES), 0, N_NODES, dtype=jnp.int32)

        def lin(k, dout, din):
            return jax.random.normal(k, (dout, din), dtype=jnp.float32) * (1.0 / np.sqrt(din))
        return {'x': x, 'edge_index': edge_index, 'W1l': lin(ks[2], D_HID, D_IN), 'b1l': jnp.zeros((D_HID,), jnp.float32), 'W1r': lin(ks[3], D_HID, D_IN), 'W2l': lin(ks[4], D_HID, D_HID), 'b2l': jnp.zeros((D_HID,), jnp.float32), 'W2r': lin(ks[5], D_HID, D_HID), 'W3l': lin(ks[6], D_OUT, D_HID), 'b3l': jnp.zeros((D_OUT,), jnp.float32), 'W3r': lin(ks[7], D_OUT, D_HID)}
    _L0_gnn_all = _L0_gnn_setup()
    _L0_gnn_in = {k: v for k, v in _L0_gnn_all.items() if k in ('W1l', 'b1l', 'W1r', 'W2l', 'b2l', 'W2r', 'W3l', 'b3l', 'W3r')}
    del _L0_gnn_all

    def _L0_mix_setup():
        import jax, jax.numpy as jnp
        import numpy as np
        HEADS = 8
        DIM_HEAD = 32
        SCALE = DIM_HEAD ** (-0.5)
        EPS = 1e-05

        def _layernorm_gamma(x, gamma):
            mu = jnp.mean(x, axis=-1, keepdims=True)
            var = jnp.var(x, axis=-1, keepdims=True)
            return (x - mu) * jax.lax.rsqrt(var + EPS) * gamma
        key = jax.random.key(seed)
        k1, k2, k3 = jax.random.split(key, 3)
        B, N, D = (8, 512, 256)
        hidden = HEADS * DIM_HEAD
        x = jax.random.normal(k1, (B, N, D), dtype=jnp.float32)
        Wqkv = jax.random.normal(k2, (D, 3 * hidden), dtype=jnp.float32) * D ** (-0.5)
        Wout = jax.random.normal(k3, (hidden, D), dtype=jnp.float32) * hidden ** (-0.5)
        gamma = jnp.ones((D,), dtype=jnp.float32)
        return {'x': x, 'Wqkv': Wqkv, 'Wout': Wout, 'gamma': gamma}
    _L0_mix_all = _L0_mix_setup()
    _L0_mix_in = {k: v for k, v in _L0_mix_all.items() if k in ('Wqkv', 'Wout', 'gamma')}
    del _L0_mix_all

    def _L0_ffn_setup():
        import jax, jax.numpy as jnp
        import numpy as np
        B, S, D = (8, 128, 256)
        H = 4 * D
        CAPACITY = 0.5
        key = jax.random.key(seed)
        ks = jax.random.split(key, 6)
        x = jax.random.normal(ks[0], (B, S, D), dtype=jnp.float32)
        attention_mask = jnp.zeros((B, 1, 1, S), dtype=jnp.float32)
        wr = jax.random.normal(ks[1], (D, 1), dtype=jnp.float32) * 0.02
        br = jnp.zeros((1,), dtype=jnp.float32)
        w1 = jax.random.normal(ks[2], (D, H), dtype=jnp.float32) * 0.02
        b1 = jnp.zeros((H,), dtype=jnp.float32)
        w2 = jax.random.normal(ks[3], (H, D), dtype=jnp.float32) * 0.02
        b2 = jnp.zeros((D,), dtype=jnp.float32)
        return {'x': x, 'attention_mask': attention_mask, 'wr': wr, 'br': br, 'w1': w1, 'b1': b1, 'w2': w2, 'b2': b2}
    _L0_ffn_all = _L0_ffn_setup()
    _L0_ffn_in = {k: v for k, v in _L0_ffn_all.items() if k in ('attention_mask', 'wr', 'br', 'w1', 'b1', 'w2', 'b2')}
    del _L0_ffn_all

    def _L1_gnn_setup():
        import jax, jax.numpy as jnp
        import numpy as np
        N = 50000
        E = 25000
        IN_DIM = 256
        HID = 64
        HEADS = 4
        NEG_SLOPE = 0.2

        def _gat_forward(x, edge_index, W, att_src, att_dst, bias):
            n = x.shape[0]
            h = (x @ W).reshape(n, HEADS, HID)
            a_src = jnp.einsum('nhf,hf->nh', h, att_src)
            a_dst = jnp.einsum('nhf,hf->nh', h, att_dst)
            loop = jnp.arange(n, dtype=edge_index.dtype)
            src = jnp.concatenate([edge_index[0], loop])
            dst = jnp.concatenate([edge_index[1], loop])
            e = jax.nn.leaky_relu(a_src[src] + a_dst[dst], NEG_SLOPE)
            m = jax.ops.segment_max(e, dst, num_segments=n)
            num = jnp.exp(e - m[dst])
            denom = jax.ops.segment_sum(num, dst, num_segments=n)
            alpha = num / denom[dst]
            msg = alpha[:, :, None] * h[src]
            out = jax.ops.segment_sum(msg, dst, num_segments=n)
            out = out.reshape(n, HEADS * HID) + bias
            return jax.nn.relu(out)
        key = jax.random.key(seed)
        k1, k2, k3, k4, k5, k6 = jax.random.split(key, 6)
        x = jax.random.normal(k1, (N, IN_DIM), dtype=jnp.float32)
        edge_index = jax.random.randint(k2, (2, E), 0, N, dtype=jnp.int64)
        W = jax.random.normal(k3, (IN_DIM, HEADS * HID), dtype=jnp.float32) / np.sqrt(IN_DIM)
        att_src = jax.random.normal(k4, (HEADS, HID), dtype=jnp.float32) / np.sqrt(HID)
        att_dst = jax.random.normal(k5, (HEADS, HID), dtype=jnp.float32) / np.sqrt(HID)
        bias = jnp.zeros((HEADS * HID,), dtype=jnp.float32)
        return {'x': x, 'edge_index': edge_index, 'W': W, 'att_src': att_src, 'att_dst': att_dst, 'bias': bias}
    _L1_gnn_all = _L1_gnn_setup()
    _L1_gnn_in = {k: v for k, v in _L1_gnn_all.items() if k in ('W', 'att_src', 'att_dst', 'bias')}
    del _L1_gnn_all

    def _L1_mix_setup():
        import jax, jax.numpy as jnp
        import numpy as np
        MIDC = 256
        HEADS = 8
        HEADC = MIDC // HEADS
        EPS = 1e-05

        def _ln(x, gamma, beta):
            mu = jnp.mean(x, axis=-1, keepdims=True)
            var = jnp.var(x, axis=-1, keepdims=True)
            return (x - mu) * jax.lax.rsqrt(var + EPS) * gamma + beta
        key = jax.random.key(seed)
        ks = jax.random.split(key, 8)
        B, HW, C = (8, 128, MIDC)
        s = 1.0 / np.sqrt(C)
        return {'x': jax.random.normal(ks[0], (B, HW, C), jnp.float32), 'w_qkv': jax.random.normal(ks[1], (C, 3 * C), jnp.float32) * s, 'b_qkv': jnp.zeros((3 * C,), jnp.float32), 'kln_g': jnp.ones((HEADC,), jnp.float32), 'kln_b': jnp.zeros((HEADC,), jnp.float32), 'vln_g': jnp.ones((HEADC,), jnp.float32), 'vln_b': jnp.zeros((HEADC,), jnp.float32), 'w1': jax.random.normal(ks[2], (C, C), jnp.float32) * s, 'b1': jnp.zeros((C,), jnp.float32), 'w2': jax.random.normal(ks[3], (C, C), jnp.float32) * s, 'b2': jnp.zeros((C,), jnp.float32)}
    _L1_mix_all = _L1_mix_setup()
    _L1_mix_in = {k: v for k, v in _L1_mix_all.items() if k in ('w_qkv', 'b_qkv', 'kln_g', 'kln_b', 'vln_g', 'vln_b', 'w1', 'b1', 'w2', 'b2')}
    del _L1_mix_all

    def _L1_ffn_setup():
        import jax, jax.numpy as jnp
        import numpy as np
        B, A = (128, 8)
        IN, OUT = (256, 256)
        SH1, SH2 = (256, 128)
        EH1, EH2 = (128, 64)
        E, TOPK = (4, 2)

        def _shared_mlp(x, W1, b1, W2, b2, W3, b3):
            h = jax.nn.relu(x @ W1 + b1)
            h = jax.nn.relu(h @ W2 + b2)
            return h @ W3 + b3

        def _experts_mlp(x, eW1, eb1, eW2, eb2, eW3, eb3):
            h = jax.nn.relu(jnp.einsum('baf,efh->ebah', x, eW1) + eb1[:, None, None, :])
            h = jax.nn.relu(jnp.einsum('ebah,ehg->ebag', h, eW2) + eb2[:, None, None, :])
            o = jnp.einsum('ebag,ego->ebao', h, eW3) + eb3[:, None, None, :]
            return jnp.moveaxis(o, 0, -1)
        key = jax.random.key(seed)
        ks = jax.random.split(key, 16)
        s = 0.05
        return {'x': jax.random.normal(ks[0], (B, A, IN), jnp.float32), 'sW1': jax.random.normal(ks[1], (IN, SH1), jnp.float32) * s, 'sb1': jnp.zeros((SH1,), jnp.float32), 'sW2': jax.random.normal(ks[2], (SH1, SH2), jnp.float32) * s, 'sb2': jnp.zeros((SH2,), jnp.float32), 'sW3': jax.random.normal(ks[3], (SH2, OUT), jnp.float32) * s, 'sb3': jnp.zeros((OUT,), jnp.float32), 'eW1': jax.random.normal(ks[4], (E, IN, EH1), jnp.float32) * s, 'eb1': jnp.zeros((E, EH1), jnp.float32), 'eW2': jax.random.normal(ks[5], (E, EH1, EH2), jnp.float32) * s, 'eb2': jnp.zeros((E, EH2), jnp.float32), 'eW3': jax.random.normal(ks[6], (E, EH2, OUT), jnp.float32) * s, 'eb3': jnp.zeros((E, OUT), jnp.float32), 'gW': jax.random.normal(ks[7], (IN, E), jnp.float32) * s, 'gb': jnp.zeros((E,), jnp.float32)}
    _L1_ffn_all = _L1_ffn_setup()
    _L1_ffn_in = {k: v for k, v in _L1_ffn_all.items() if k in ('sW1', 'sb1', 'sW2', 'sb2', 'sW3', 'sb3', 'eW1', 'eb1', 'eW2', 'eb2', 'eW3', 'eb3', 'gW', 'gb')}
    del _L1_ffn_all
    return {'x': x, 'src': src, 'dst': dst, 'L0_gnn_W1l': _L0_gnn_in['W1l'], 'L0_gnn_b1l': _L0_gnn_in['b1l'], 'L0_gnn_W1r': _L0_gnn_in['W1r'], 'L0_gnn_W2l': _L0_gnn_in['W2l'], 'L0_gnn_b2l': _L0_gnn_in['b2l'], 'L0_gnn_W2r': _L0_gnn_in['W2r'], 'L0_gnn_W3l': _L0_gnn_in['W3l'], 'L0_gnn_b3l': _L0_gnn_in['b3l'], 'L0_gnn_W3r': _L0_gnn_in['W3r'], 'L0_mix_Wqkv': _L0_mix_in['Wqkv'], 'L0_mix_Wout': _L0_mix_in['Wout'], 'L0_mix_gamma': _L0_mix_in['gamma'], 'L0_ffn_attention_mask': _L0_ffn_in['attention_mask'], 'L0_ffn_wr': _L0_ffn_in['wr'], 'L0_ffn_br': _L0_ffn_in['br'], 'L0_ffn_w1': _L0_ffn_in['w1'], 'L0_ffn_b1': _L0_ffn_in['b1'], 'L0_ffn_w2': _L0_ffn_in['w2'], 'L0_ffn_b2': _L0_ffn_in['b2'], 'L1_gnn_W': _L1_gnn_in['W'], 'L1_gnn_att_src': _L1_gnn_in['att_src'], 'L1_gnn_att_dst': _L1_gnn_in['att_dst'], 'L1_gnn_bias': _L1_gnn_in['bias'], 'L1_mix_w_qkv': _L1_mix_in['w_qkv'], 'L1_mix_b_qkv': _L1_mix_in['b_qkv'], 'L1_mix_kln_g': _L1_mix_in['kln_g'], 'L1_mix_kln_b': _L1_mix_in['kln_b'], 'L1_mix_vln_g': _L1_mix_in['vln_g'], 'L1_mix_vln_b': _L1_mix_in['vln_b'], 'L1_mix_w1': _L1_mix_in['w1'], 'L1_mix_b1': _L1_mix_in['b1'], 'L1_mix_w2': _L1_mix_in['w2'], 'L1_mix_b2': _L1_mix_in['b2'], 'L1_ffn_sW1': _L1_ffn_in['sW1'], 'L1_ffn_sb1': _L1_ffn_in['sb1'], 'L1_ffn_sW2': _L1_ffn_in['sW2'], 'L1_ffn_sb2': _L1_ffn_in['sb2'], 'L1_ffn_sW3': _L1_ffn_in['sW3'], 'L1_ffn_sb3': _L1_ffn_in['sb3'], 'L1_ffn_eW1': _L1_ffn_in['eW1'], 'L1_ffn_eb1': _L1_ffn_in['eb1'], 'L1_ffn_eW2': _L1_ffn_in['eW2'], 'L1_ffn_eb2': _L1_ffn_in['eb2'], 'L1_ffn_eW3': _L1_ffn_in['eW3'], 'L1_ffn_eb3': _L1_ffn_in['eb3'], 'L1_ffn_gW': _L1_ffn_in['gW'], 'L1_ffn_gb': _L1_ffn_in['gb']}

def reference(x, src, dst, L0_gnn_W1l, L0_gnn_b1l, L0_gnn_W1r, L0_gnn_W2l, L0_gnn_b2l, L0_gnn_W2r, L0_gnn_W3l, L0_gnn_b3l, L0_gnn_W3r, L0_mix_Wqkv, L0_mix_Wout, L0_mix_gamma, L0_ffn_attention_mask, L0_ffn_wr, L0_ffn_br, L0_ffn_w1, L0_ffn_b1, L0_ffn_w2, L0_ffn_b2, L1_gnn_W, L1_gnn_att_src, L1_gnn_att_dst, L1_gnn_bias, L1_mix_w_qkv, L1_mix_b_qkv, L1_mix_kln_g, L1_mix_kln_b, L1_mix_vln_g, L1_mix_vln_b, L1_mix_w1, L1_mix_b1, L1_mix_w2, L1_mix_b2, L1_ffn_sW1, L1_ffn_sb1, L1_ffn_sW2, L1_ffn_sb2, L1_ffn_sW3, L1_ffn_sb3, L1_ffn_eW1, L1_ffn_eb1, L1_ffn_eW2, L1_ffn_eb2, L1_ffn_eW3, L1_ffn_eb3, L1_ffn_gW, L1_ffn_gb):
    import jax
    import jax.numpy as jnp

    def _L0_gnn_ref(x, edge_index, W1l, b1l, W1r, W2l, b2l, W2r, W3l, b3l, W3r):
        import jax, jax.numpy as jnp
        import numpy as np
        N_NODES = 50000
        N_EDGES = 25000
        D_IN = 256
        D_HID = 256
        D_OUT = 256

        def _sage_conv(x, src, dst, Wl, bl, Wr, num_nodes):
            msg = x[src]
            agg = jax.ops.segment_sum(msg, dst, num_segments=num_nodes)
            deg = jax.ops.segment_sum(jnp.ones((src.shape[0],), x.dtype), dst, num_segments=num_nodes)
            mean = agg / jnp.maximum(deg, 1.0)[:, None]
            return jnp.einsum('nd,od->no', mean, Wl) + bl + jnp.einsum('nd,od->no', x, Wr)
        src, dst = (edge_index[0], edge_index[1])
        n = x.shape[0]
        h = _sage_conv(x, src, dst, W1l, b1l, W1r, n)
        h = jax.nn.relu(h)
        h = _sage_conv(h, src, dst, W2l, b2l, W2r, n)
        h = jax.nn.relu(h)
        h = _sage_conv(h, src, dst, W3l, b3l, W3r, n)
        return h

    def _L0_mix_ref(x, Wqkv, Wout, gamma):
        import jax, jax.numpy as jnp
        import numpy as np
        HEADS = 8
        DIM_HEAD = 32
        SCALE = DIM_HEAD ** (-0.5)
        EPS = 1e-05

        def _layernorm_gamma(x, gamma):
            mu = jnp.mean(x, axis=-1, keepdims=True)
            var = jnp.var(x, axis=-1, keepdims=True)
            return (x - mu) * jax.lax.rsqrt(var + EPS) * gamma
        B, N, D = x.shape
        qkv = x @ Wqkv
        q, k, v = jnp.split(qkv, 3, axis=-1)

        def to_heads(t):
            return t.reshape(B, N, HEADS, DIM_HEAD).transpose(0, 2, 1, 3)
        q, k, v = map(to_heads, (q, k, v))
        q = jax.nn.softmax(q, axis=-1) * SCALE
        k = jax.nn.softmax(k, axis=2)
        context = jnp.einsum('bhnd,bhne->bhde', k, v)
        out = jnp.einsum('bhde,bhnd->bhne', context, q)
        out = out.transpose(0, 2, 1, 3).reshape(B, N, HEADS * DIM_HEAD)
        out = out @ Wout
        return _layernorm_gamma(out, gamma)

    def _L0_ffn_ref(x, attention_mask, wr, br, w1, b1, w2, b2):
        import jax, jax.numpy as jnp
        import numpy as np
        B, S, D = (8, 128, 256)
        H = 4 * D
        CAPACITY = 0.5
        b, s, d = x.shape
        weights = (jnp.einsum('bsd,do->bso', x, wr) + br)[..., 0]
        k = max(1, int(CAPACITY * s))
        kk = k - 1 if k > 1 else 1
        _, idx = jax.lax.top_k(weights, k)
        sel_idx = idx[:, :kk]
        sel = jnp.take_along_axis(x, sel_idx[:, :, None], axis=1)
        h = jax.nn.gelu(jnp.einsum('bkd,dh->bkh', sel, w1) + b1)
        y = jnp.einsum('bkh,hd->bkd', h, w2) + b2
        w_sel = jnp.take_along_axis(weights, sel_idx, axis=1)
        y = y * w_sel[..., None]
        batch_idx = jnp.arange(b)[:, None]
        processed = jnp.zeros_like(x).at[batch_idx, sel_idx].set(y)
        return processed + x

    def _L1_gnn_ref(x, edge_index, W, att_src, att_dst, bias):
        import jax, jax.numpy as jnp
        import numpy as np
        N = 50000
        E = 25000
        IN_DIM = 256
        HID = 64
        HEADS = 4
        NEG_SLOPE = 0.2

        def _gat_forward(x, edge_index, W, att_src, att_dst, bias):
            n = x.shape[0]
            h = (x @ W).reshape(n, HEADS, HID)
            a_src = jnp.einsum('nhf,hf->nh', h, att_src)
            a_dst = jnp.einsum('nhf,hf->nh', h, att_dst)
            loop = jnp.arange(n, dtype=edge_index.dtype)
            src = jnp.concatenate([edge_index[0], loop])
            dst = jnp.concatenate([edge_index[1], loop])
            e = jax.nn.leaky_relu(a_src[src] + a_dst[dst], NEG_SLOPE)
            m = jax.ops.segment_max(e, dst, num_segments=n)
            num = jnp.exp(e - m[dst])
            denom = jax.ops.segment_sum(num, dst, num_segments=n)
            alpha = num / denom[dst]
            msg = alpha[:, :, None] * h[src]
            out = jax.ops.segment_sum(msg, dst, num_segments=n)
            out = out.reshape(n, HEADS * HID) + bias
            return jax.nn.relu(out)
        return _gat_forward(x, edge_index, W, att_src, att_dst, bias)

    def _L1_mix_ref(x, w_qkv, b_qkv, kln_g, kln_b, vln_g, vln_b, w1, b1, w2, b2):
        import jax, jax.numpy as jnp
        import numpy as np
        MIDC = 256
        HEADS = 8
        HEADC = MIDC // HEADS
        EPS = 1e-05

        def _ln(x, gamma, beta):
            mu = jnp.mean(x, axis=-1, keepdims=True)
            var = jnp.var(x, axis=-1, keepdims=True)
            return (x - mu) * jax.lax.rsqrt(var + EPS) * gamma + beta
        B, HW, C = x.shape
        bias = x
        qkv = (x @ w_qkv + b_qkv).reshape(B, HW, HEADS, 3 * HEADC)
        qkv = qkv.transpose(0, 2, 1, 3)
        q, k, v = jnp.split(qkv, 3, axis=-1)
        k = _ln(k, kln_g, kln_b)
        v = _ln(v, vln_g, vln_b)
        kv = jnp.einsum('bhnd,bhne->bhde', k, v) / HW
        out = jnp.einsum('bhnd,bhde->bhne', q, kv)
        out = out.transpose(0, 2, 1, 3).reshape(B, HW, C)
        ret = out + bias
        h = jax.nn.gelu(ret @ w1 + b1, approximate=False)
        return h @ w2 + b2 + bias

    def _L1_ffn_ref(x, sW1, sb1, sW2, sb2, sW3, sb3, eW1, eb1, eW2, eb2, eW3, eb3, gW, gb):
        import jax, jax.numpy as jnp
        import numpy as np
        B, A = (128, 8)
        IN, OUT = (256, 256)
        SH1, SH2 = (256, 128)
        EH1, EH2 = (128, 64)
        E, TOPK = (4, 2)

        def _shared_mlp(x, W1, b1, W2, b2, W3, b3):
            h = jax.nn.relu(x @ W1 + b1)
            h = jax.nn.relu(h @ W2 + b2)
            return h @ W3 + b3

        def _experts_mlp(x, eW1, eb1, eW2, eb2, eW3, eb3):
            h = jax.nn.relu(jnp.einsum('baf,efh->ebah', x, eW1) + eb1[:, None, None, :])
            h = jax.nn.relu(jnp.einsum('ebah,ehg->ebag', h, eW2) + eb2[:, None, None, :])
            o = jnp.einsum('ebag,ego->ebao', h, eW3) + eb3[:, None, None, :]
            return jnp.moveaxis(o, 0, -1)
        all_out = _experts_mlp(x, eW1, eb1, eW2, eb2, eW3, eb3)
        shared = _shared_mlp(x, sW1, sb1, sW2, sb2, sW3, sb3)
        gates = jax.nn.softmax(x @ gW + gb, axis=-1)
        topv, topi = jax.lax.top_k(gates, TOPK)
        topw = jax.nn.softmax(topv, axis=-1)
        sel = jnp.take_along_axis(all_out, topi[:, :, None, :], axis=-1)
        gated = jnp.sum(sel * topw[:, :, None, :], axis=-1)
        return shared + gated
    edge_index = jnp.stack([src, dst])
    xn = _layernorm(x, axis=-1)
    x = x + _L0_gnn_ref(xn, edge_index, L0_gnn_W1l, L0_gnn_b1l, L0_gnn_W1r, L0_gnn_W2l, L0_gnn_b2l, L0_gnn_W2r, L0_gnn_W3l, L0_gnn_b3l, L0_gnn_W3r) + _L0_mix_ref(xn[None], L0_mix_Wqkv, L0_mix_Wout, L0_mix_gamma)[0]
    x = x + _L0_ffn_ref(_layernorm(x, axis=-1)[None], L0_ffn_attention_mask, L0_ffn_wr, L0_ffn_br, L0_ffn_w1, L0_ffn_b1, L0_ffn_w2, L0_ffn_b2)[0]
    xn = _layernorm(x, axis=-1)
    x = x + _L1_gnn_ref(xn, edge_index, L1_gnn_W, L1_gnn_att_src, L1_gnn_att_dst, L1_gnn_bias) + _L1_mix_ref(xn[None], L1_mix_w_qkv, L1_mix_b_qkv, L1_mix_kln_g, L1_mix_kln_b, L1_mix_vln_g, L1_mix_vln_b, L1_mix_w1, L1_mix_b1, L1_mix_w2, L1_mix_b2)[0]
    x = x + _L1_ffn_ref(_layernorm(x, axis=-1)[None], L1_ffn_sW1, L1_ffn_sb1, L1_ffn_sW2, L1_ffn_sb2, L1_ffn_sW3, L1_ffn_sb3, L1_ffn_eW1, L1_ffn_eb1, L1_ffn_eW2, L1_ffn_eb2, L1_ffn_eW3, L1_ffn_eb3, L1_ffn_gW, L1_ffn_gb)[0]
    return x

_drawn_inputs = setup_inputs


def setup_inputs(seed=0):
    import zlib

    import numpy as np

    out = dict(_drawn_inputs(seed))
    spreads = {'L0_gnn_b1l': (0.0, 0.1),
     'L0_gnn_b2l': (0.0, 0.1),
     'L0_gnn_b3l': (0.0, 0.1),
     'L0_mix_gamma': (1.0, 0.2),
     'L0_ffn_b1': (0.0, 0.8),
     'L0_ffn_b2': (0.0, 0.8),
     'L1_gnn_bias': (0.0, 0.484),
     'L1_mix_b_qkv': (0.0, 0.1),
     'L1_mix_kln_g': (1.0, 0.2),
     'L1_mix_kln_b': (0.0, 0.1),
     'L1_mix_vln_g': (1.0, 0.2),
     'L1_mix_vln_b': (0.0, 0.1),
     'L1_mix_b1': (0.0, 0.423),
     'L1_mix_b2': (0.0, 0.337),
     'L1_ffn_sb1': (0.0, 2.0),
     'L1_ffn_sb2': (0.0, 2.0),
     'L1_ffn_sb3': (0.0, 0.946),
     'L1_ffn_eb1': (0.0, 0.8),
     'L1_ffn_eb2': (0.0, 0.8),
     'L1_ffn_eb3': (0.0, 0.486),
     'L1_ffn_gb': (0.0, 0.8)}
    factors = {'L0_ffn_wr': 5.686,
     'L0_ffn_w1': 8.0,
     'L0_ffn_w2': 8.0,
     'L1_gnn_att_src': 2.99,
     'L1_gnn_att_dst': 6.535,
     'L1_ffn_eW1': 5.51,
     'L1_ffn_eW2': 5.041,
     'L1_ffn_eW3': 3.981,
     'L1_ffn_gW': 3.946,
     'L1_ffn_sW1': 4.885,
     'L1_ffn_sW2': 3.337}
    for name, (base, spread) in spreads.items():
        noise = np.random.default_rng([zlib.crc32(name.encode()), seed]).standard_normal(out[name].shape)
        drawn = base * np.exp(spread * noise) if base else spread * noise
        out[name] = jnp.asarray(drawn.astype(out[name].dtype))
    for name, factor in factors.items():
        out[name] = (out[name] * factor).astype(out[name].dtype)
    return out
```

```python
from contextlib import ExitStack

import concourse.bass as bass
from concourse import mybir

F32 = mybir.dt.float32
I32 = mybir.dt.int32
ALU = mybir.AluOpType
ACT = mybir.ActivationFunctionType
AX = mybir.AxisListType

N, D, E = 3125, 256, 50000
P = 125
NB = N // P
KC = D // 128
ET = 128
NT = -(-E // ET)
U = 4
NG = -(-NT // U)
GS = 16
RG = GS // U
LAG = 4
GW = 260
EPS = 1e-5
H1 = 4 * D
HC = H1 // 128
TB = 4
TOK = TB * P
CHOSEN = max(1, N // 2) - 1
ds = bass.ds


def build(nc, I, out):
    with ExitStack() as ctx:
        def sb(name, shape, dt=F32):
            return ctx.enter_context(nc.sbuf_tensor(name, shape, dt))

        def sem(name):
            return ctx.enter_context(nc.semaphore(name))

        bigk = sb("bigk", [128, NB * D])
        bigv = sb("bigv", [128, NB * D])
        bigx = sb("bigx", [128, NB * D])
        bigq = sb("bigq", [128, NB * D])
        ho = sb("ho", [128, D])
        iota = sb("iota", [128, N])
        G = sb("G", [128, GS, GW])
        oh = sb("oh", [128, U, P])
        ident = sb("ident", [128, 128])
        eps = sb("eps", [128, 1])
        ones = sb("ones", [1, P])
        zrow = sb("zrow", [1, 512], mybir.dt.bfloat16)
        idx = sb("idx", [128, NG * U], I32)
        idxc = sb("idxc", [128, 16], I32)
        dstf = sb("dstf", [128, NG * U])
        qrun = sb("qrun", [1, 2, NB], I32)
        st = sb("st", [128, 2, D])
        rT = sb("rT", [128, 2, KC * 128])
        st6 = sb("st6", [128, NB, 6])
        mv = sb("mv", [128, NB, 3])
        rdeg = sb("rdeg", [128, 2])
        gamma = sb("gamma", [P, D])
        rm = sb("rm", [P, D])
        kmb = sb("kmb", [P, D])
        kmx = sb("kmx", [128, KC])
        dg = sb("dg", [128, KC, 128])
        ones128 = sb("ones128", [128, P])
        bdm = sb("bdm", [128, 128])
        qst = sb("qst", [P, 3, 8])
        qsm = sb("qsm", [P, D])
        ek = sb("ek", [P, D])
        dn = sb("dn", [128, KC])
        bd = sb("bd", [128, KC, 128])
        bdT = sb("bdT", [128, KC, 128])
        qT = sb("qT", [128, KC * P])
        ty = sb("ty", [P, D])
        xs = sb("xs", [P, D])
        x1s = sb("x1s", [P, D])
        xls = sb("xls", [P, D])
        lst = sb("lst", [P, 2, 10])
        wr = sb("wr", [128, KC])
        wrr = sb("wrr", [128, KC, P])
        br = sb("br", [P, 1])
        b1c = sb("b1c", [128, HC])
        b2r = sb("b2r", [1, D])
        wcol = sb("wcol", [P, NB])
        cnt = sb("cnt", [P, NB, 4])
        sel = sb("sel", [P, NB])
        tril = sb("tril", [P, P])
        triu = sb("triu", [P, P])
        bl = sb("bl", [1, 3, D])
        wh = sb("wh", [128, U, GW])
        ohT = sb("ohT", [P, U * ET])
        ez = sb("ez", [128, U, 4])
        rs8 = sb("rs8", [P, 8])
        wA = sb("wA", [128, 11 * KC * D])
        wB = sb("wB", [128, 2 * KC * H1])
        B = [ctx.enter_context(nc.psum_tensor(f"B{k}", [128, 512], F32)) for k in range(8)]
        psS, psH, psM, psO = B[0:4]
        psQK, psV = B[4], B[5]
        psC, psA = B[6], B[7]
        psT, psX = B[1], B[2]

        tab = [nc.dram_tensor(f"tab{k}", [N, D], F32, kind="Internal").ap() for k in range(3)]
        gtab = nc.dram_tensor("gtab", [N, GW], F32, kind="Internal").ap()
        tabb = [t.rearrange("(b p) d -> p b d", p=P) for t in tab]

        by_block = [t[0:P, :].rearrange("p (b d) -> p b d", b=NB) for t in (bigk, bigv, bigx, bigq)]
        k_all, v_all, x1_all, q_all = by_block
        xin, h = q_all, x1_all
        xlT = bigk[:, 0:KC * N].rearrange("p (c n) -> p c n", c=KC)

        def blk(t, b):
            return t[:, ds(b, 1), :].rearrange("p a d -> p (a d)")

        wrow = bigv[0:P, 0:N]
        yw = q_all
        hT = G[:, :, :].rearrange("p s d -> p (s d)")[:, 0:HC * TOK].rearrange("p (m n) -> p m n", m=HC)
        junk = bigv[0:P, N:2 * N]
        junk2 = bigv[0:P, 2 * N:2 * N + P]

        def part(buf, at, *shape):
            n = 1
            for k in shape:
                n *= k
            v = buf[:, at:at + n]
            names = "abc"[:len(shape)]
            return v.rearrange(f"p ({' '.join(names)}) -> p {' '.join(names)}", **dict(zip(names, shape)))
        W1 = KC * D
        WlT, WrT = part(wA, 0, 3, KC, D), part(wA, 3 * W1, 3, KC, D)
        Wqkv = part(wA, 6 * W1, KC, 3 * D)
        Wout = part(wA, 9 * W1, KC, D)
        Mx = part(wA, 10 * W1, KC, D)
        w1, w2 = part(wB, 0, KC, H1), part(wB, KC * H1, HC, D)

        Wg = part(wA, 0, KC, D + 8)
        at = KC * (D + 8)
        Wkv = part(wA, at, KC, 2 * D)
        at += 2 * W1
        Wq, WqT, WqpT, m1, m2, Wpp, WgT = [part(wA, at + k * W1, KC, D) for k in range(7)]
        at += 7 * W1
        A8 = part(wA, at, KC, 8)
        bqc, bqp, b1m, bpp = [part(wA, at + 16 + KC * k, KC) for k in range(4)]
        cmean = wA[:, at + 24:at + 56]
        gbk = bigv[0:P, 0:4 * D].rearrange("p (a d) -> p a d", a=2)
        kvn = bigv[0:P, 1024:1536]
        sq = bigv[0:P, 1536:2048]
        hs = bigv[0:P, 2048:2048 + D + 8]
        gbias = bigv[0:P, 2320:2320 + D]
        bkv = bigv[0:1, 2576:2576 + 2 * D]
        bq = bigv[0:1, 3088:3088 + D]
        b2m = bigv[0:1, 3344:3344 + D]
        b3 = bigv[0:1, 3600:3600 + 5 * D]
        asd = bigv[0:P, 4880:4880 + 8 * NB].rearrange("p (b h) -> p b h", b=NB)
        tab8 = bigv[0:P, 5080:5080 + 8 * NB].rearrange("p (b h) -> p b h", b=NB)
        wself = bigv[0:P, 5280:5280 + 4 * NB].rearrange("p (b h) -> p b h", b=NB)
        ss = bigv[0:P, 5380:5412]
        mx4 = bigv[0:P, 5412:5416]
        kx = bigv[0:4, 5416:5417]
        dg4 = bigv[0:4, 5420:5424]
        bmean = bigv[0:1, 5424:5440]
        gbr = bigv[0:1, 5440:5444]
        gl, gx, gr2, ga, gp = [bigv[0:P, 5444 + k * 4 * NB:5444 + (k + 1) * 4 * NB].rearrange("p (b h) -> p b h", b=NB) for k in range(5)]
        g1 = bigv[0:P, 5944:5944 + NB].rearrange("p (b h) -> p b h", b=NB)
        at = 0
        def take(*shape):
            nonlocal at
            n = 1
            for k in shape:
                n *= k
            at += n
            return part(wB, at - n, *shape)
        sW1, sW2, sW3 = take(KC, D), take(KC, 128), take(1, D)
        eW1, eW2, eW3 = take(4, KC, 128), take(4, 64), take(4, D)
        gW, sb1, sb2, eb1, eb2 = take(KC, 4), take(KC), take(1), take(4), take(4)
        gT = bigq[:, 0:KC * TOK].rearrange("p (m n) -> p m n", m=KC)
        ffh = [bigq[:, k * TOK:(k + 1) * TOK] for k in range(11)]

        rows = bigk[:, 0:2 * 4 * ET].rearrange("p (a c e) -> p a c e", a=2, c=4)
        rowsi = bigk[:, 1024:2048].bitcast(I32).rearrange("p (a c e) -> p a c e", a=2, c=4)
        red = bigk[:, 2048:2048 + 40]
        redi = bigk[:, 2096:2104].bitcast(I32)
        wst = bigv[:, 3200:3200 + 6 * KC * D].rearrange("p (m c d) -> p m c d", m=6, c=KC)

        s_edges = sem("s_edges")
        s_x = [sem(f"s_xin{g}") for g in range(5)]
        s_w = sem("s_w")
        s_id = sem("s_id")
        s_pad = sem("s_pad")
        s_row = sem("s_row")
        s_et = sem("s_et")
        s_ev = sem("s_ev")
        s_wt = sem("s_wt")
        s_wv = sem("s_wv")
        s_red = sem("s_red")
        s_rt = sem("s_rt")
        s_tb = sem("s_tb")
        s_qe = sem("s_qe")
        s_st = sem("s_st")
        s_mv = sem("s_mv")
        s_rs = sem("s_rs")
        s_sd = sem("s_sd")
        s_lnd = sem("s_lnd")
        s_tab0 = sem("s_tab0")
        s_cnt = sem("s_cnt")
        L4 = range(3)
        s_gath = [[sem(f"s_gath{k}_{u}") for u in range(LAG)] for k in range(4)]
        s_ic = [sem(f"s_ic{k}") for k in range(4)]
        s_landed = [sem(f"s_landed{k}") for k in range(4)]
        s_free = [sem(f"s_free{k}") for k in range(4)]
        s_oh = [sem(f"s_oh{k}") for k in range(4)]
        s_mm = [sem(f"s_mm{k}") for k in range(4)]
        s_sum = sem("s_sum")
        s_mean = sem("s_mean")
        s_gat = sem("s_gat")
        s_hin = sem("s_hin")
        s_hT = sem("s_hT")
        s_he = sem("s_he")
        s_mT = sem("s_mT")
        s_me = sem("s_me")
        s_omm = sem("s_omm")
        s_ho = sem("s_ho")
        s_hfree = sem("s_hfree")
        s_sto = sem("s_sto")
        s_mixw = sem("s_mixw")
        s_gdone = sem("s_gdone")
        s_out = sem("s_out")
        s_fw = sem("s_fw")
        s_wc = sem("s_wc")
        s_rank = sem("s_rank")
        s_ge = sem("s_ge")
        s_st2 = sem("s_st2")
        s_yw = sem("s_yw")
        s_st1 = sem("s_st1")
        s_w4 = sem("s_w4")
        s_w5 = sem("s_w5")
        s_w6 = sem("s_w6")
        s_a8 = sem("s_a8")
        s_x2 = sem("s_x2")
        s_x2sd = sem("s_x2sd")
        s_x2T = sem("s_x2T")
        s_x2Te = sem("s_x2Te")
        s_hkv = sem("s_hkv")
        s_hs = sem("s_hs")
        s_kvsd = sem("s_kvsd")
        s_hsa = sem("s_hsa")
        s_kvg = sem("s_kvg")
        s_kva = sem("s_kva")
        s_gst = sem("s_gst")
        s_pt = sem("s_pt")
        s_pv = sem("s_pv")
        s_kvd = sem("s_kvd")
        s_k4 = sem("s_k4")
        s_k4p = sem("s_k4p")
        s_k4x = sem("s_k4x")
        s_p1 = sem("s_p1")
        s_p1e = sem("s_p1e")
        s_p2 = sem("s_p2")
        s_p2x = sem("s_p2x")
        s_ohT = sem("s_ohT")
        s_ohTe = sem("s_ohTe")
        s_psx = sem("s_psx")
        s_z = sem("s_z")
        s_ew = sem("s_ew")
        s_m = sem("s_m")
        s_msd = sem("s_msd")
        s_mxT = sem("s_mxT")
        s_mxTe = sem("s_mxTe")
        s_mg = sem("s_mg")
        s_mge = sem("s_mge")
        s_gx = sem("s_gx")
        s_gxe = sem("s_gxe")
        s_e1 = sem("s_e1")
        s_e2 = sem("s_e2")
        s_tm = sem("s_tm")
        s_acc = sem("s_acc")
        s_mix0 = sem("s_mix0")
        s_qkv = sem("s_qkv")
        s_kvc = sem("s_kvc")
        s_qx = sem("s_qx")
        s_km = sem("s_km")
        s_kmT = sem("s_kmT")
        s_kmB = sem("s_kmB")
        s_ek = sem("s_ek")
        s_ekx = sem("s_ekx")
        s_ctx = sem("s_ctx")
        s_bd = sem("s_bd")
        s_bdp = sem("s_bdp")
        s_xs = sem("s_xs")
        s_qs = sem("s_qs")
        s_qT = sem("s_qT")
        s_qTe = sem("s_qTe")
        s_omx = sem("s_omx")
        s_ln = sem("s_ln")
        s_lna = sem("s_lna")
        s_xlT = sem("s_xlT")
        s_xlTe = sem("s_xlTe")
        s_rw = sem("s_rw")
        s_wrow = sem("s_wrow")
        s_wrr = sem("s_wrr")

        block = ctx.enter_context(nc.Block())
        full = E // ET // 128
        rest = E // ET - full * 128
        tail = E - (E // ET) * ET
        chunk_rows = [128] * full + [rest + 1]

        def group_range(eng, b):
            return [eng.value_load(qrun[0:1, k, ds(b, 1)], min_val=k, max_val=NB * NG) for k in range(2)]

        def ring(q, u):
            return ds(q % RG * U + u, 1)

        @block.sync
        def _(sp):
            sp.wait_ge(s_pad, 2)
            for a, e in enumerate((I["src"], I["dst"])):
                sp.dma_start(rowsi[:, a, 0:full, :], e[0:full * 128 * ET].rearrange("(c p e) -> p c e", p=128, e=ET)).then_inc(s_edges, 16)
                sp.dma_start(rowsi[0:rest, a, full, :], e[full * 128 * ET:(E // ET) * ET].rearrange("(p e) -> p e", e=ET)).then_inc(s_edges, 16)
                sp.dma_start(rowsi[rest:rest + 1, a, full, 0:tail], e[(E // ET) * ET:E].rearrange("(p e) -> p e", p=1)).then_inc(s_edges, 16)
            for g in range(5):
                sp.dma_start(xin[0:P, 5 * g:5 * g + 5, :], I["x"].rearrange("(b p) d -> p b d", p=P)[:, 5 * g:5 * g + 5, :]).then_inc(s_x[g], 16)
            for k in range(3):
                sp.dma_start(wst[:, k, :, :], I[f"L0_gnn_W{k+1}l"].rearrange("(c p) d -> p c d", p=128)).then_inc(s_w, 16)
                sp.dma_start(wst[:, 3 + k, :, :], I[f"L0_gnn_W{k+1}r"].rearrange("(c p) d -> p c d", p=128)).then_inc(s_w, 16)
                sp.dma_start(bl[:, k, :], I[f"L0_gnn_b{k+1}l"].rearrange("(a d) -> a d", a=1)).then_inc(s_w, 16)
            sp.dma_start(Wqkv[:, :, :], I["L0_mix_Wqkv"].rearrange("(c p) d -> p c d", p=128)).then_inc(s_mixw, 16)
            sp.dma_start(Wout[:, :, :], I["L0_mix_Wout"].rearrange("(c p) d -> p c d", p=128)).then_inc(s_mixw, 16)
            sp.dma_start(gamma[:, :], I["L0_mix_gamma"].rearrange("(a d) -> a d", a=1).broadcast_to((P, D))).then_inc(s_mixw, 16)
            sp.dma_start(wr[:, :], I["L0_ffn_wr"].rearrange("(c p) o -> p (c o)", p=128), allow_slow_non_contiguous=True).then_inc(s_mixw, 16)
            sp.dma_start(br[:, :], I["L0_ffn_br"].rearrange("(a d) -> a d", a=1).broadcast_to((P, 1))).then_inc(s_mixw, 16)
            sp.dma_start(w1[:, :, :], I["L0_ffn_w1"].rearrange("(c p) d -> p c d", p=128)).then_inc(s_fw, 16)
            sp.dma_start(w2[:, :, :], I["L0_ffn_w2"].rearrange("(c p) d -> p c d", p=128)).then_inc(s_fw, 16)
            sp.dma_start(b1c[:, :], I["L0_ffn_b1"].rearrange("(c p) -> p c", p=128), allow_slow_non_contiguous=True).then_inc(s_fw, 16)
            sp.dma_start(b2r[:, :], I["L0_ffn_b2"].rearrange("(a d) -> a d", a=1)).then_inc(s_fw, 16)
            for g in range(5):
                sp.wait_ge(s_lnd, 5 * g + 5)
                sp.dma_start(tabb[0][:, 5 * g:5 * g + 5, :], h[0:P, 5 * g:5 * g + 5, :]).then_inc(s_tab0, 16)
            for L in L4:
                if L == 0:
                    sp.wait_ge(s_tab0, 5 * 16)
                else:
                    sp.wait_ge(s_sto, L * NB * 16)
                with sp.Fori(0, NB) as b:
                    sp.wait_ge(s_hT, L * NB + b + 1)
                    sp.dma_start(st[0:P, 0, :], tab[L][ds(b * P, P), :]).then_inc(s_hin, 16)
                    if L < 2:
                        sp.wait_ge(s_ho, L * NB + b + 2)
                        sp.dma_start(tab[L + 1][ds(b * P, P), :], ho[0:P, :]).then_inc(s_sto, 16)
                        sp.wait_ge(s_sto, (L * NB + b + 1) * 16)
                        sp.sem_inc(s_hfree, 1)
                    else:
                        sp.wait_ge(s_ln, b * 12 + 1)
                        sp.dma_start(xs[:, :], I["x"][ds(b * P, P), :]).then_inc(s_xs, 16)
            row = lambda t: t.rearrange("(a d) -> a d", a=1)
            sp.wait_ge(s_rw, NB)
            sp.wait_ge(s_a8, 1)
            sp.dma_start(Wg[:, :, 0:D], I["L1_gnn_W"].rearrange("(c p) d -> p c d", p=128)).then_inc(s_w4, 16)
            for a, w in enumerate((I["L1_gnn_att_src"], I["L1_gnn_att_dst"])):
                for k in range(4):
                    lo = 64 * (k % 2)
                    sp.dma_start(A8[lo:lo + 64, k // 2, 4 * a + k:4 * a + k + 1], w[k:k + 1, :].rearrange("a f -> f a"), allow_slow_non_contiguous=True).then_inc(s_w4, 16)
            wq = I["L1_mix_w_qkv"].rearrange("(c p) (h t e) -> c t p h e", p=128, t=3, e=32)
            for c in range(KC):
                for t in range(3):
                    to = Wq[:, c, :] if t == 0 else Wkv[:, c, (t - 1) * D:t * D]
                    sp.dma_start(to.rearrange("p (h e) -> p h e", h=8), wq[c, t]).then_inc(s_w4, 16)
            sp.dma_start(m1[:, :, :], I["L1_mix_w1"].rearrange("(c p) d -> p c d", p=128)).then_inc(s_w4, 16)
            sp.dma_start(m2[:, :, :], I["L1_mix_w2"].rearrange("(c p) d -> p c d", p=128)).then_inc(s_w4, 16)
            sp.dma_start(b1m[:, :], I["L1_mix_b1"].rearrange("(c p) -> p c", p=128), allow_slow_non_contiguous=True).then_inc(s_w4, 16)
            sp.wait_ge(s_rank, 4 * NB)
            for a, n in enumerate(("g", "b")):
                for k, t in enumerate(("kln", "vln")):
                    sp.dma_start(gbk[:, a, k * D:(k + 1) * D].rearrange("p (h e) -> p h e", h=8),
                                 I[f"L1_mix_{t}_{n}"].rearrange("(a b e) -> a b e", a=1, b=1).broadcast_to((P, 8, 32))).then_inc(s_w5, 16)
            bs = I["L1_mix_b_qkv"].rearrange("(a h t e) -> t a h e", a=1, t=3, e=32)
            for t in range(3):
                to = bq if t == 0 else bkv[:, (t - 1) * D:t * D]
                sp.dma_start(to.rearrange("p (h e) -> p h e", h=8), bs[t]).then_inc(s_w5, 16)
            sp.dma_start(gbias, row(I["L1_gnn_bias"]).broadcast_to((P, D))).then_inc(s_w5, 16)
            sp.dma_start(b2m, row(I["L1_mix_b2"])).then_inc(s_w5, 16)
            sp.dma_start(b3[:, 0:D], row(I["L1_ffn_sb3"])).then_inc(s_w5, 16)
            sp.dma_start(b3[:, D:5 * D], I["L1_ffn_eb3"].rearrange("(a e) d -> a (e d)", a=1)).then_inc(s_w5, 16)
            sp.dma_start(gbr, row(I["L1_ffn_gb"])).then_inc(s_w5, 16)
            sp.wait_ge(s_st2, NB // TB + 1)
            sp.dma_start(sW1, I["L1_ffn_sW1"].rearrange("(c p) d -> p c d", p=128)).then_inc(s_w6, 16)
            sp.dma_start(sW2, I["L1_ffn_sW2"].rearrange("(c p) d -> p c d", p=128)).then_inc(s_w6, 16)
            sp.dma_start(sW3[:, 0, :], I["L1_ffn_sW3"]).then_inc(s_w6, 16)
            for k in range(4):
                sp.dma_start(eW1[:, k, :, :], I["L1_ffn_eW1"][k].rearrange("(c p) d -> p c d", p=128)).then_inc(s_w6, 16)
            sp.dma_start(eW2, I["L1_ffn_eW2"].rearrange("k p d -> p k d")).then_inc(s_w6, 16)
            sp.dma_start(eW3[0:64, :, :], I["L1_ffn_eW3"].rearrange("k p d -> p k d")).then_inc(s_w6, 16)
            sp.dma_start(gW, I["L1_ffn_gW"].rearrange("(c p) d -> p c d", p=128), allow_slow_non_contiguous=True).then_inc(s_w6, 16)
            sp.dma_start(sb1, I["L1_ffn_sb1"].rearrange("(c p) -> p c", p=128), allow_slow_non_contiguous=True).then_inc(s_w6, 16)
            sp.dma_start(sb2, I["L1_ffn_sb2"].rearrange("(p c) -> p c", c=1), allow_slow_non_contiguous=True).then_inc(s_w6, 16)
            sp.dma_start(eb1, I["L1_ffn_eb1"].rearrange("k p -> p k"), allow_slow_non_contiguous=True).then_inc(s_w6, 16)
            sp.dma_start(eb2[0:64, :], I["L1_ffn_eb2"].rearrange("k p -> p k"), allow_slow_non_contiguous=True).then_inc(s_w6, 16)
            with sp.Fori(0, NB) as b:
                sp.wait_ge(s_hs, b + 1)
                sp.dma_start(gtab[ds(b * P, P), :], hs[:, 0:GW]).then_inc(s_gst, 16)
                sp.wait_ge(s_gst, (b + 1) * 16)
                sp.sem_inc(s_hfree, 1)
            sp.wait_ge(s_gst, NB * 16)
            with sp.Fori(0, NB) as b:
                sp.wait_ge(s_gat, b * 7 + 1)
                sp.dma_start(st[0:P, 0, :], gtab[ds(b * P, P), 0:D]).then_inc(s_hin, 16)
            with sp.Fori(0, NB) as b:
                sp.wait_ge(s_acc, b * 5 + 6)
                sp.dma_start(out[ds(b * P, P), :], blk(x1_all, b)).then_inc(s_out, 16)
            sp.wait_ge(s_out, NB * 16)

        @block.gpsimd
        def _(pool):
            pool.memset(ident[:, :], 1.0).then_inc(s_id, 1)
            pool.memset(G[:, :, D:GW], 1.0).then_inc(s_id, 1)
            pool.memset(idx[:, :], 0).then_inc(s_id, 1)
            pool.iota(bigv[:, 0:N].bitcast(I32), pattern=[[1, N]], base=0, channel_multiplier=0).then_inc(s_id, 1)
            pool.wait_ge(s_id, 4)
            pool.affine_select(out=ident[:, :], in_=ident[:, :], compare_op=ALU.is_equal, fill=0.0,
                               base=0, pattern=[[-1, 128]], channel_multiplier=1).then_inc(s_id, 1)
            pool.memset(ones[:, :], 1.0).then_inc(s_id, 1)
            pool.memset(eps[:, :], EPS).then_inc(s_id, 1)
            pool.memset(zrow[:, :], 0.0).then_inc(s_id, 1)
            pool.memset(ones128[:, :], 1.0).then_inc(s_id, 1)
            pool.memset(bdm[:, :], 0.0).then_inc(s_id, 1)
            pool.wait_ge(s_id, 10)
            for q in range(4):
                pool.memset(bdm[32 * q:32 * q + 32, 32 * q:32 * q + 32], 1.0).then_inc(s_id, 1)
            pool.wait_ge(s_id, 14)
            pool.memset(tril[:, :], 1.0).then_inc(s_id, 1)
            pool.memset(triu[:, :], 1.0).then_inc(s_id, 1)
            pool.wait_ge(s_id, 16)
            pool.affine_select(out=tril[:, :], in_=tril[:, :], compare_op=ALU.is_gt, fill=0.0,
                               base=0, pattern=[[-1, P]], channel_multiplier=1).then_inc(s_id, 1)
            pool.affine_select(out=triu[:, :], in_=triu[:, :], compare_op=ALU.is_gt, fill=0.0,
                               base=0, pattern=[[1, P]], channel_multiplier=-1).then_inc(s_id, 1)
            pool.wait_ge(s_qe, 2)
            for L in range(4):
                if L == 3:
                    pool.wait_ge(s_w5, 12 * 16)
                    with pool.Fori(0, NB) as b:
                        pool.wait_ge(s_x2, b * 9 + 9)
                        pool.tensor_tensor(kvn, kvn, gbk[:, 0, :], ALU.mult).then_inc(s_kvg, 1)
                        pool.wait_ge(s_kvg, b * 2 + 1)
                        pool.tensor_tensor(kvn, kvn, gbk[:, 1, :], ALU.add).then_inc(s_kvg, 1)
                if L == 0:
                    pool.wait_ge(s_tab0, 5 * 16)
                elif L == 3:
                    pool.wait_ge(s_gst, NB * 16)
                else:
                    pool.wait_ge(s_sto, L * NB * 16)
                groups = pool.value_load(qrun[0:1, 1, NB - 1:NB], min_val=1, max_val=NB * NG)

                def gathers(q, slot):
                    pool.tensor_copy(idxc[:, slot:slot + U], idx[:, ds(q % NG * U, U)]).then_inc(s_ic[L], 1)
                    pool.wait_ge(s_ic[L], q + 1)
                    pool.wait_ge(s_free[L], q + 1)
                    for u in range(U):
                        if not isinstance(q, int):
                            pool.wait_ge(s_gath[L][u], q * 16)
                            pool.sem_inc(s_landed[L], 1)
                        pool.indirect_dma_start(out=G[:, slot + u, 0:D if L < 3 else GW], out_offset=None, in_=tab[L][:, :] if L < 3 else gtab[:, :],
                                                in_offset=bass.IndirectOffsetOnAxis(ap=idxc[:, slot + u:slot + u + 1], axis=0)).then_inc(s_gath[L][u], 16)

                gathers(0, 0)
                with pool.Fori(1, groups, RG) as q:
                    for k in range(RG):
                        gathers(q + k, (k + 1) % RG * U)
                for u in range(LAG):
                    pool.wait_ge(s_gath[L][u], ((groups + (RG - 2)) // RG * RG + 1) * 16)
                    pool.sem_inc(s_landed[L], 1)
                pool.sem_inc(s_gdone, 1)

        @block.vector
        def _(dve):
            dve.memset(rowsi[:, 0, :, :], 0).then_inc(s_pad, 1)
            dve.memset(rowsi[:, 1, :, :], N).then_inc(s_pad, 1)
            dve.wait_ge(s_id, 4)
            dve.tensor_copy(iota[:, :], bigv[:, 0:N].bitcast(I32)).then_inc(s_cnt, 1)
            dve.memset(dstf[:, :], float(N)).then_inc(s_cnt, 1)
            dve.wait_ge(s_edges, 96)
            dve.tensor_copy(rows[:, :, :, :], rowsi[:, :, :, :]).then_inc(s_row, 1)
            dve.wait_ge(s_row, 1)
            c1 = red[:, 0:4]
            c2 = red[:, 4:8]
            dve.tensor_reduce(c1, rows[:, 1, :, :], AX.X, ALU.min).then_inc(s_red, 1)
            dve.tensor_scalar(bigk[:, 4096:4096 + 512].rearrange("p (c e) -> p c e", c=4), rows[:, 1, :, :], float(N - 1), None, ALU.min).then_inc(s_red, 1)
            dve.wait_ge(s_red, 2)
            dve.tensor_reduce(c2, bigk[:, 4096:4096 + 512].rearrange("p (c e) -> p c e", c=4), AX.X, ALU.max).then_inc(s_red, 1)
            dve.wait_ge(s_red, 3)
            dve.tensor_scalar(red[:, 16:24], red[:, 0:8], 0.5, 1.0 / P, ALU.add, ALU.mult).then_inc(s_red, 1)
            dve.wait_ge(s_red, 4)
            dve.tensor_copy(redi, red[:, 16:24]).then_inc(s_red, 1)
            dve.wait_ge(s_red, 5)
            dve.tensor_copy(red[:, 24:32], redi).then_inc(s_red, 1)
            dve.wait_ge(s_red, 6)
            dve.tensor_tensor(red[:, 32:40], red[:, 24:32], red[:, 16:24], ALU.is_gt).then_inc(s_red, 1)
            dve.wait_ge(s_red, 7)
            dve.tensor_tensor(red[:, 8:16], red[:, 24:32], red[:, 32:40], ALU.subtract).then_inc(s_red, 1)
            for c in range(4):
                for a in range(2):
                    k = 2 * c + a
                    dve.wait_ge(s_et, k + 1)
                    src_ps = B[k % 4][:, 0:chunk_rows[c]]
                    dst_sb = (idx if a == 0 else dstf)[:, 128 * c:128 * c + chunk_rows[c]]
                    dve.tensor_copy(dst_sb, src_ps).then_inc(s_ev, 1)
            gr = bigk[0:1, 3000:3000 + 4 * NG]
            gmin, gmax, gt = gr[:, 0:NG], gr[:, NG:2 * NG], gr[:, 2 * NG:3 * NG]
            fl = bigk[0:1, 3400:3404]
            qs, qg = bigk[0:1, 3410:3410 + NB], bigk[0:1, 3440:3440 + NB]
            le = bigk[0:1, 3470:3470 + NB * NG].rearrange("p (b g) -> p b g", b=NB)
            dve.wait_ge(s_rt, 8)
            dve.tensor_reduce(gmin, B[4][0:1, 0:NG * U].rearrange("p (g u) -> p g u", u=U), AX.X, ALU.min).then_inc(s_tb, 1)
            dve.tensor_reduce(gmax, B[5][0:1, 0:NG * U].rearrange("p (g u) -> p g u", u=U), AX.X, ALU.max).then_inc(s_tb, 1)
            dve.wait_ge(s_tb, 2)
            dve.tensor_tensor(gt[:, 0:NG - 1], gmin[:, 1:NG], gmax[:, 0:NG - 1], ALU.is_lt).then_inc(s_tb, 1)
            dve.wait_ge(s_tb, 3)
            dve.tensor_reduce(fl[:, 0:1], gt[:, 0:NG - 1], AX.X, ALU.max).then_inc(s_tb, 1)
            dve.tensor_tensor(le, gmin.rearrange("p (b g) -> p b g", b=1).broadcast_to((1, NB, NG)), iota[0:1, 0:NB].rearrange("p (b g) -> p b g", g=1).broadcast_to((1, NB, NG)), ALU.is_le).then_inc(s_tb, 1)
            dve.wait_ge(s_tb, 5)
            dve.tensor_reduce(qs, le, AX.X, ALU.add).then_inc(s_tb, 1)
            dve.tensor_scalar(qg, iota[0:1, 0:NB], float(NG - 1), float(NG), ALU.mult, ALU.add).then_inc(s_tb, 1)
            dve.wait_ge(s_tb, 7)
            dve.tensor_scalar(qs, qs, 1.0, None, ALU.max).then_inc(s_tb, 1)
            dve.wait_ge(s_tb, 8)
            dve.tensor_tensor(qg, qg, qs, ALU.subtract).then_inc(s_tb, 1)
            dve.wait_ge(s_tb, 9)
            dve.scalar_tensor_tensor(out=qs, in0=qg, scalar=fl[:, 0:1], in1=qs, op0=ALU.mult, op1=ALU.add).then_inc(s_tb, 1)
            dve.memset(qrun[:, 0, 0:1], 0).then_inc(s_tb, 1)
            dve.wait_ge(s_tb, 11)
            dve.tensor_copy(qrun[:, 1, :], qs).then_inc(s_qe, 1)
            dve.tensor_scalar(qg[:, 0:NB - 1], qs[:, 0:NB - 1], -1.0, None, ALU.add).then_inc(s_tb, 1)
            dve.wait_ge(s_tb, 12)
            dve.tensor_copy(qrun[:, 0, 1:NB], qg[:, 0:NB - 1]).then_inc(s_qe, 1)

            for g in range(5):
                dve.wait_ge(s_x[g], 16)
                for b in range(5 * g, 5 * g + 5):
                    dve.bn_stats(st6[0:P, b, :], xin[0:P, b, :]).then_inc(s_st, 1)
                for b in range(5 * g, 5 * g + 5):
                    dve.wait_ge(s_st, b + 1)
                    dve.bn_aggr(mv[0:P, b, 0:2], st6[0:P, b, :]).then_inc(s_mv, 1)
            for g in range(5):
                dve.wait_ge(s_sd, g + 1)
                dve.reciprocal(mv[0:P, 5 * g:5 * g + 5, 2], mv[0:P, 5 * g:5 * g + 5, 2]).then_inc(s_rs, 1)
                dve.wait_ge(s_rs, g + 1)
                for b in range(5 * g, 5 * g + 5):
                    dve.tensor_scalar(h[0:P, b, :], xin[0:P, b, :], mv[0:P, b, 0:1], mv[0:P, b, 2:3], ALU.subtract, ALU.mult).then_inc(s_lnd, 1)
            for k in range(6):
                dve.wait_ge(s_wt, k + 1)
                W = (WlT if k < 3 else WrT)[:, k % 3, :, :]
                dve.tensor_copy(W, B[6 + k % 2][:, :].rearrange("p (c o) -> p c o", c=KC)).then_inc(s_wv, 1)

            dve.memset(rm[:, :], -3.0e38).then_inc(s_mix0, 1)
            dve.sem_inc(s_ln, 1)
            dve.wait_ge(s_mixw, 5 * 16)
            for c in range(KC):
                dve.tensor_copy(wrr[:, c, :], wr[:, c:c + 1].broadcast_to((128, P))).then_inc(s_wrr, 1)

            def ln_stats(src, k, n):
                dve.bn_stats(lst[:, k, 0:6], src).then_inc(s_ln, 1)
                dve.wait_ge(s_ln, n + 1)
                dve.nop(nofuse=True)
                dve.bn_aggr(lst[:, k, 6:8], lst[:, k, 0:6]).then_inc(s_ln, 1)
                return n + 2

            for L in L4:
                if L == 1:
                    dve.wait_ge(s_kmT, 1)
                    dve.tensor_reduce(kmx[:, :], psA[:, 0:KC * P].rearrange("p (c n) -> p c n", c=KC), AX.X, ALU.max).then_inc(s_km, 1)
                    dve.wait_ge(s_km, 1)
                    for c in range(KC):
                        dve.tensor_scalar(dg[:, c, :], ident[:, :], kmx[:, c:c + 1], None, ALU.mult).then_inc(s_km, 1)
                    dve.wait_ge(s_kmB, 1)
                    dve.tensor_copy(kmb[:, :], psA[0:P, 0:D]).then_inc(s_km, 1)
                    dve.wait_ge(s_km, 4)
                if L == 2:
                    dve.wait_ge(s_ctx, NB + 1)
                    dve.reciprocal(dn[:, :], psC[:, D:D + KC]).then_inc(s_bd, 1)
                    dve.wait_ge(s_bd, 1)
                    dve.tensor_scalar(dn[:, :], dn[:, :], 32.0 ** -0.5, None, ALU.mult).then_inc(s_bd, 1)
                    dve.wait_ge(s_bd, 2)
                    for c in range(KC):
                        dve.scalar_tensor_tensor(out=bd[:, c, :], in0=psC[:, c * 128:c * 128 + 128], scalar=dn[:, c:c + 1], in1=bdm[:, :], op0=ALU.mult, op1=ALU.mult).then_inc(s_bd, 1)
                    dve.wait_ge(s_bdp, 1)
                    dve.tensor_copy(bdT[:, :, :], psA[:, 0:256].rearrange("p (c n) -> p c n", c=KC)).then_inc(s_bd, 1)
                    dve.wait_ge(s_bdp, 2)
                    for c in range(KC):
                        dve.tensor_copy(Mx[:, c, :], B[4 + c][:, 0:D]).then_inc(s_bd, 1)

                def one_hots(b, q):
                    for u in range(U):
                        dve.wait_ge(s_mm[L], (q + b) * (U - 1) + max(u, 1))
                        dve.tensor_scalar(oh[:, u, :], iota[:, ds(b * P, P)], dstf[:, ds(q % NG * U + u, 1)], None, ALU.is_equal).then_inc(s_oh[L], 1)

                with dve.Fori(0, NB) as b:
                    q0, q1 = group_range(dve, b)
                    one_hots(b, q0)
                    with dve.If(q1 > q0 + 1):
                        with dve.Fori(q0 + 1, q1) as q:
                            one_hots(b, q)
                    dve.wait_ge(s_sum, L * NB + b + 1)
                    dve.tensor_scalar(rdeg[0:P, 0:1], psS[0:P, D:D + 1], 1.0, None, ALU.max).then_inc(s_mean, 1)
                    dve.wait_ge(s_mean, (L * NB + b) * 3 + 2)
                    dve.reciprocal(rdeg[0:P, 1:2], rdeg[0:P, 0:1]).then_inc(s_mean, 1)
                    dve.wait_ge(s_mean, (L * NB + b) * 3 + 3)
                    dve.tensor_scalar(st[0:P, 1, :], psS[0:P, 0:D], rdeg[0:P, 1:2], None, ALU.mult).then_inc(s_mean, 1)

                    if L == 0:
                        n = b * 6 + 1
                        heads = lambda t: t.rearrange("p (h e) -> p h e", h=8)
                        dve.wait_ge(s_qkv, b + 1)
                        dve.tensor_reduce(qst[:, 0, :], heads(psQK[0:P, 0:D]), AX.X, ALU.max).then_inc(s_mix0, 1)
                        dve.wait_ge(s_mix0, n + 1)
                        dve.tensor_tensor(heads(qsm[:, :]), heads(psQK[0:P, 0:D]), qst[:, 0, :].rearrange("p (h e) -> p h e", e=1).broadcast_to((P, 8, 32)), ALU.subtract).then_inc(s_mix0, 1)
                        dve.wait_ge(s_kvc, b * 2 + 3)
                        dve.tensor_tensor(rm[:, :], rm[:, :], blk(k_all, b), ALU.max).then_inc(s_mix0, 1)
                        dve.wait_ge(s_qx, b + 1)
                        dve.tensor_reduce(qst[:, 1, :], heads(qsm[:, :]), AX.X, ALU.add).then_inc(s_mix0, 1)
                        dve.wait_ge(s_mix0, n + 4)
                        dve.reciprocal(qst[:, 2, :], qst[:, 1, :]).then_inc(s_mix0, 1)
                        dve.wait_ge(s_mix0, n + 5)
                        dve.tensor_tensor(heads(blk(q_all, b)), heads(qsm[:, :]), qst[:, 2, :].rearrange("p (h e) -> p h e", e=1).broadcast_to((P, 8, 32)), ALU.mult).then_inc(s_mix0, 1)
                    if L == 1:
                        dve.tensor_tensor(ek[:, :], blk(k_all, b), kmb[:, :], ALU.subtract).then_inc(s_ek, 1)
                    if L == 2:
                        n = b * 12 + 1
                        dve.wait_ge(s_omx, b + 1)
                        n = ln_stats(psQK[0:P, 0:D], 0, n)
                        dve.wait_ge(s_lna, b * 2 + 1)
                        dve.reciprocal(lst[:, 0, 9:10], lst[:, 0, 8:9]).then_inc(s_ln, 1)
                        dve.wait_ge(s_ln, n + 1)
                        dve.tensor_scalar(ty[:, :], psQK[0:P, 0:D], lst[:, 0, 6:7], lst[:, 0, 9:10], ALU.subtract, ALU.mult).then_inc(s_ln, 1)
                        dve.wait_ge(s_ln, n + 2)
                        dve.tensor_tensor(ty[:, :], ty[:, :], gamma[:, :], ALU.mult).then_inc(s_ln, 1)
                        dve.wait_ge(s_ln, n + 3)
                        dve.wait_ge(s_xs, (b + 1) * 16)
                        dve.tensor_tensor(ty[:, :], ty[:, :], xs[:, :], ALU.add).then_inc(s_ln, 1)
                        dve.wait_ge(s_ln, n + 4)
                        dve.wait_ge(s_omm, L * NB + b + 1)
                        dve.tensor_tensor(x1s[:, :], ty[:, :], psO[0:P, 0:D], ALU.add).then_inc(s_ln, 1)
                        dve.wait_ge(s_ln, n + 5)
                        n = ln_stats(x1s[:, :], 1, n + 5)
                        dve.wait_ge(s_lna, b * 2 + 2)
                        dve.reciprocal(lst[:, 1, 9:10], lst[:, 1, 8:9]).then_inc(s_ln, 1)
                        dve.wait_ge(s_ln, n + 1)
                        dve.tensor_scalar(xls[:, :], x1s[:, :], lst[:, 1, 6:7], lst[:, 1, 9:10], ALU.subtract, ALU.mult).then_inc(s_ln, 1)
                        dve.wait_ge(s_ln, n + 2)
                        dve.tensor_tensor(blk(x1_all, b), x1s[:, :], xls[:, :], ALU.add).then_inc(s_ln, 1)

            dve.wait_ge(s_wrow, NB)
            dve.wait_ge(s_id, 18)
            dve.memset(A8, 0.0).then_inc(s_a8, 1)
            dve.memset(cnt[:, :, :], 0.0).then_inc(s_wc, 1)
            for i in range(NB):
                dve.tensor_tensor_reduce(junk[:, P * i:P * i + P], wrow[:, P * i:P * i + P], ident[0:P, 0:P], 1.0, 0.0, ALU.mult, ALU.add, wcol[:, i:i + 1]).then_inc(s_wc, 1)
            dve.wait_ge(s_wc, NB + 1)
            for i in range(NB):
                lo, hi = P * i, P * i + P
                if i:
                    dve.wait_ge(s_rank, 4 * i - 1)
                    dve.tensor_scalar(junk[:, 0:lo], wrow[:, 0:lo], wcol[:, i:i + 1], 0.0, ALU.is_ge, ALU.add, accum_out=cnt[:, i, 0:1]).then_inc(s_rank, 1)
                if i < NB - 1:
                    dve.tensor_scalar(junk[:, hi:N], wrow[:, hi:N], wcol[:, i:i + 1], 0.0, ALU.is_gt, ALU.add, accum_out=cnt[:, i, 1:2]).then_inc(s_rank, 1)
                dve.scalar_tensor_tensor(out=junk[:, lo:hi], in0=wrow[:, lo:hi], scalar=wcol[:, i:i + 1], in1=tril[:, :], op0=ALU.is_ge, op1=ALU.mult, accum_out=cnt[:, i, 2:3]).then_inc(s_rank, 1)
                dve.scalar_tensor_tensor(out=junk2, in0=wrow[:, lo:hi], scalar=wcol[:, i:i + 1], in1=triu[:, :], op0=ALU.is_gt, op1=ALU.mult, accum_out=cnt[:, i, 3:4]).then_inc(s_rank, 1)
            nr = 4 * NB - 2
            dve.wait_ge(s_rank, nr)
            dve.tensor_reduce(sel[:, :], cnt[:, :, :], AX.X, ALU.add).then_inc(s_rank, 1)
            dve.wait_ge(s_rank, nr + 1)
            dve.tensor_scalar(sel[:, :], sel[:, :], float(CHOSEN), None, ALU.is_lt).then_inc(s_rank, 1)

            dve.wait_ge(s_pt, 2)
            for k, (to, bank) in enumerate(((WgT, 0), (WqT, 2))):
                dve.tensor_copy(to, B[bank][:, :].rearrange("p (c o) -> p c o", c=KC)).then_inc(s_pv, 1)
            groups = lambda t, n: t.rearrange("p (g e) -> p g e", g=n)
            dve.wait_ge(s_w5, 12 * 16)
            for k, (t, mean, n) in enumerate(((Wkv.rearrange("p c d -> p (c d)"), cmean, 32), (bkv, bmean, 16))):
                dve.tensor_reduce(mean, groups(t, n), AX.X, ALU.add).then_inc(s_pv, 1)
                dve.wait_ge(s_pv, 3 + 3 * k)
                dve.tensor_scalar(mean, mean, 1.0 / 32, None, ALU.mult).then_inc(s_pv, 1)
                dve.wait_ge(s_pv, 4 + 3 * k)
                dve.tensor_tensor(groups(t, n), groups(t, n), mean.rearrange("p (g e) -> p g e", e=1).broadcast_to((t.shape[0], n, 32)), ALU.subtract).then_inc(s_pv, 1)
            dve.wait_ge(s_pt, 3)
            dve.tensor_copy(Wg[:, :, D:D + 8], B[4][:, 0:16].rearrange("p (c h) -> p c h", c=KC)).then_inc(s_pv, 1)
            dve.tensor_copy(bqc, B[5][:, 0:KC]).then_inc(s_pv, 1)
            dve.wait_ge(s_yw, NB + TB)
            dve.wait_ge(s_rank, 4 * NB)
            with dve.Fori(0, NB) as b:
                n = b * 9
                dve.scalar_tensor_tensor(out=x1s[:, :], in0=blk(yw, b), scalar=sel[:, ds(b, 1)], in1=blk(x1_all, b), op0=ALU.mult, op1=ALU.add).then_inc(s_x2, 1)
                dve.wait_ge(s_x2, n + 1)
                dve.bn_stats(lst[:, 0, 0:6], x1s[:, :]).then_inc(s_x2, 1)
                dve.wait_ge(s_x2, n + 2)
                dve.nop(nofuse=True)
                dve.bn_aggr(lst[:, 0, 6:8], lst[:, 0, 0:6]).then_inc(s_x2, 1)
                dve.wait_ge(s_x2sd, b + 1)
                dve.reciprocal(lst[:, 0, 9:10], lst[:, 0, 8:9]).then_inc(s_x2, 1)
                dve.wait_ge(s_x2, n + 4)
                dve.tensor_scalar(xls[:, :], x1s[:, :], lst[:, 0, 6:7], lst[:, 0, 9:10], ALU.subtract, ALU.mult).then_inc(s_x2, 1)
                dve.wait_ge(s_x2, n + 5)
                dve.tensor_tensor(blk(x1_all, b), x1s[:, :], xls[:, :], ALU.add).then_inc(s_x2, 1)
                dve.wait_ge(s_kvsd, b * 2 + 1)
                dve.tensor_reduce(ss[:, 0:16], groups(sq, 16), AX.X, ALU.add).then_inc(s_x2, 1)
                dve.wait_ge(s_kvsd, b * 2 + 2)
                dve.reciprocal(ss[:, 16:32], ss[:, 16:32]).then_inc(s_x2, 1)
                dve.wait_ge(s_x2, n + 8)
                dve.wait_ge(s_kva, b + 1)
                dve.tensor_tensor(groups(kvn, 16), groups(psV[0:P, :], 16), ss[:, 16:32].rearrange("p (g e) -> p g e", e=1).broadcast_to((P, 16, 32)), ALU.mult).then_inc(s_x2, 1)
            dve.wait_ge(s_kvd, 1)
            for c in range(KC):
                dve.scalar_tensor_tensor(out=bd[:, c, :], in0=psC[:, c * 128:c * 128 + 128], scalar=1.0 / N, in1=bdm[:, :], op0=ALU.mult, op1=ALU.mult).then_inc(s_k4, 1)
            dve.tensor_reduce(mx4, asd[:, :, 0:4].rearrange("p b h -> p h b"), AX.X, ALU.max).then_inc(s_k4, 1)
            dve.wait_ge(s_k4p, 1)
            dve.tensor_copy(WqpT, B[0][:, :].rearrange("p (c o) -> p c o", c=KC)).then_inc(s_k4, 1)
            dve.tensor_copy(bqp, B[5][:, 0:KC]).then_inc(s_k4, 1)
            dve.wait_ge(s_k4, 4)
            for c in range(KC):
                dve.tensor_tensor(WqpT[:, c, c * 128:c * 128 + 128], WqpT[:, c, c * 128:c * 128 + 128], ident[:, :], ALU.add).then_inc(s_k4, 1)
            dve.wait_ge(s_k4p, 2)
            dve.tensor_reduce(kx, B[7][0:4, 0:P], AX.X, ALU.max).then_inc(s_k4, 1)
            dve.wait_ge(s_k4, 8)
            dve.tensor_scalar(dg4, ident[0:4, 0:4], kx, None, ALU.mult).then_inc(s_k4, 1)
            dve.wait_ge(s_k4p, 3)
            dve.tensor_copy(Wpp, B[2][:, :].rearrange("p (c o) -> p c o", c=KC)).then_inc(s_k4, 1)
            dve.tensor_tensor(bpp, B[5][:, 4:4 + KC], b1m, ALU.add).then_inc(s_k4, 1)
            dve.wait_ge(s_k4p, 4)
            dve.tensor_copy(mx4, B[7][0:P, 128:132]).then_inc(s_k4, 1)
            dve.wait_ge(s_k4, 12)
            top = tab8[:, :, 4:8]
            dve.tensor_tensor(top, asd[:, :, 4:8], mx4.rearrange("p (b h) -> p b h", b=1).broadcast_to((P, NB, 4)), ALU.add).then_inc(s_k4, 1)
            dve.tensor_copy(tab8[:, :, 0:4], asd[:, :, 4:8]).then_inc(s_k4, 1)
            dve.tensor_tensor(wself, asd[:, :, 0:4], asd[:, :, 4:8], ALU.add).then_inc(s_k4, 1)
            dve.wait_ge(s_k4, 13)
            dve.scalar_tensor_tensor(out=top, in0=top, scalar=0.2, in1=top, op0=ALU.mult, op1=ALU.max).then_inc(s_k4, 1)
            dve.wait_ge(s_k4, 15)
            dve.scalar_tensor_tensor(out=wself, in0=wself, scalar=0.2, in1=wself, op0=ALU.mult, op1=ALU.max).then_inc(s_k4, 1)
            dve.wait_ge(s_k4, 17)
            dve.tensor_tensor(wself, wself, top, ALU.subtract).then_inc(s_k4, 1)

            def mix(g, blocks):
                for k in range(blocks):
                    if k == 0:
                        dve.wait_ge(s_p2, g + 1)
                    dve.tensor_tensor(blk(x1_all, g * TB + k), blk(x1_all, g * TB + k), B[4 + k][0:P, 0:D], ALU.add).then_inc(s_p2x, 1)
            with dve.Fori(0, NB // TB) as g:
                mix(g, TB)
            mix(NB // TB, NB % TB)

            dve.sem_inc(s_gat, 4)
            dve.wait_ge(s_k4x, 1)

            def weights(b, q):
                n = q + b
                for u in range(U):
                    dve.wait_ge(s_mm[3], n * (U - 1) + max(u, 1))
                    dve.tensor_scalar(oh[:, u, :], iota[:, ds(b * P, P)], dstf[:, ds(q % NG * U + u, 1)], None, ALU.is_equal).then_inc(s_oh[3], 1)
                rows4 = ds(q % RG * U, U)
                X = psX[:, 0:8 * U].rearrange("p (u h) -> p u h", u=U)
                dve.wait_ge(s_landed[3], q * U + U)
                dve.wait_ge(s_psx, n + 1)
                dve.tensor_tensor(ez[:, :, :], X[:, :, 0:4], G[:, rows4, D:GW], ALU.add).then_inc(s_z, 1)
                dve.wait_ge(s_z, n * 5 + 1)
                dve.scalar_tensor_tensor(out=ez[:, :, :], in0=ez[:, :, :], scalar=0.2, in1=ez[:, :, :], op0=ALU.mult, op1=ALU.max).then_inc(s_z, 1)
                dve.wait_ge(s_z, n * 5 + 2)
                dve.tensor_tensor(ez[:, :, :], ez[:, :, :], X[:, :, 4:8], ALU.subtract).then_inc(s_z, 1)
                dve.wait_ge(s_z, n * 5 + 3)
                dve.tensor_scalar(ez[:, :, :], ez[:, :, :], 0.0, None, ALU.min).then_inc(s_z, 1)
                dve.wait_ge(s_ew, n + 1)
                dve.tensor_tensor(wh[:, :, 0:D].rearrange("p u (h f) -> p u h f", h=4), G[:, rows4, 0:D].rearrange("p u (h f) -> p u h f", h=4),
                                  wh[:, :, D:GW].rearrange("p u (h f) -> p u h f", f=1).broadcast_to((128, U, 4, 64)), ALU.mult).then_inc(s_z, 1)

            heads4 = lambda t: t.rearrange("p (h f) -> p h f", h=4)
            wide4 = lambda t: t.rearrange("p (h f) -> p h f", f=1).broadcast_to((P, 4, 64))
            with dve.Fori(0, NB) as b:
                q0, q1 = group_range(dve, b)
                weights(b, q0)
                with dve.If(q1 > q0 + 1):
                    with dve.Fori(q0 + 1, q1) as q:
                        weights(b, q)
                n = b * 7 + 4
                ws = blk(wself, b)
                dve.wait_ge(s_sum, 3 * NB + b + 1)
                dve.tensor_tensor(rs8[:, 0:4], psS[0:P, D:GW], ws, ALU.add).then_inc(s_gat, 1)
                dve.wait_ge(s_gat, n + 1)
                dve.reciprocal(rs8[:, 4:8], rs8[:, 0:4]).then_inc(s_gat, 1)
                dve.wait_ge(s_hin, (3 * NB + b + 1) * 16)
                dve.tensor_tensor(heads4(ty[:, :]), heads4(st[0:P, 0, :]), wide4(ws), ALU.mult).then_inc(s_gat, 1)
                dve.wait_ge(s_gat, n + 3)
                dve.tensor_tensor(ty[:, :], ty[:, :], psS[0:P, 0:D], ALU.add).then_inc(s_gat, 1)
                dve.wait_ge(s_gat, n + 4)
                dve.tensor_tensor(heads4(ty[:, :]), heads4(ty[:, :]), wide4(rs8[:, 4:8]), ALU.mult).then_inc(s_gat, 1)
                dve.wait_ge(s_gat, n + 5)
                dve.tensor_tensor(ty[:, :], ty[:, :], gbias, ALU.add).then_inc(s_gat, 1)
                dve.wait_ge(s_gat, n + 6)
                dve.scalar_tensor_tensor(out=blk(x1_all, b), in0=ty[:, :], scalar=0.0, in1=blk(x1_all, b), op0=ALU.max, op1=ALU.add).then_inc(s_gat, 1)

            dve.wait_ge(s_gat, NB * 7 + 4)
            with dve.Fori(0, NB) as b:
                dve.bn_stats(lst[:, 0, 0:6], blk(x1_all, b)).then_inc(s_m, 1)
                dve.wait_ge(s_m, b * 4 + 1)
                dve.nop(nofuse=True)
                dve.bn_aggr(lst[:, 0, 6:8], lst[:, 0, 0:6]).then_inc(s_m, 1)
                dve.wait_ge(s_msd, b + 1)
                dve.reciprocal(lst[:, 0, 9:10], lst[:, 0, 8:9]).then_inc(s_m, 1)
                dve.wait_ge(s_m, b * 4 + 3)
                dve.wait_ge(s_mxTe, b * 2 + 1)
                dve.tensor_scalar(xls[:, :], blk(x1_all, b), lst[:, 0, 6:7], lst[:, 0, 9:10], ALU.subtract, ALU.mult).then_inc(s_m, 1)
            wide = lambda t: t.broadcast_to((P, NB, 4))
            dve.wait_ge(s_mge, NB)
            dve.tensor_reduce(g1, gl, AX.X, ALU.max).then_inc(s_gx, 1)
            dve.wait_ge(s_gx, 1)
            dve.tensor_tensor(gx, gl, wide(g1), ALU.subtract).then_inc(s_gx, 1)
            dve.wait_ge(s_gxe, 1)
            dve.tensor_reduce(g1, gx, AX.X, ALU.add).then_inc(s_gx, 1)
            dve.wait_ge(s_gx, 3)
            dve.reciprocal(g1, g1).then_inc(s_gx, 1)
            dve.wait_ge(s_gx, 4)
            dve.tensor_tensor(gx, gx, wide(g1), ALU.mult).then_inc(s_gx, 1)
            dve.memset(gr2, 0.0).then_inc(s_gx, 1)
            dve.wait_ge(s_gx, 6)
            n = 6
            for i in range(4):
                for j in range(4):
                    if i != j:
                        op = ALU.is_ge if j < i else ALU.is_gt
                        dve.tensor_tensor(ga[:, :, 0:1], gx[:, :, j:j + 1], gx[:, :, i:i + 1], op).then_inc(s_gx, 1)
                        dve.wait_ge(s_gx, n + 1)
                        dve.tensor_tensor(gr2[:, :, i:i + 1], gr2[:, :, i:i + 1], ga[:, :, 0:1], ALU.add).then_inc(s_gx, 1)
                        n += 2
                        dve.wait_ge(s_gx, n)
            dve.tensor_reduce(g1, gx, AX.X, ALU.max).then_inc(s_gx, 1)
            dve.wait_ge(s_gx, n + 1)
            dve.tensor_tensor(gp, gx, wide(g1), ALU.subtract).then_inc(s_gx, 1)
            dve.wait_ge(s_gxe, 2)
            dve.scalar_tensor_tensor(out=gp, in0=gr2, scalar=2.0, in1=gp, op0=ALU.is_lt, op1=ALU.mult).then_inc(s_gx, 1)
            dve.wait_ge(s_gx, n + 3)
            dve.tensor_reduce(g1, gp, AX.X, ALU.add).then_inc(s_gx, 1)
            dve.wait_ge(s_gx, n + 4)
            dve.reciprocal(g1, g1).then_inc(s_gx, 1)
            dve.wait_ge(s_gx, n + 5)
            dve.tensor_tensor(gp, gp, wide(g1), ALU.mult).then_inc(s_gx, 1)
            dve.wait_ge(s_gx, n + 6)

            def experts(b):
                x = blk(x1_all, b)
                dve.wait_ge(s_tm, b + 1)
                dve.tensor_tensor(x, x, B[6][0:P, 0:D], ALU.add).then_inc(s_acc, 1)
                for k in range(4):
                    dve.wait_ge(s_acc, b * 5 + k + 2)
                    dve.scalar_tensor_tensor(out=x, in0=B[4 + k // 2][0:P, k % 2 * D:k % 2 * D + D], scalar=gp[:, ds(b, 1), k:k + 1].rearrange("p a h -> p (a h)"), in1=x, op0=ALU.mult, op1=ALU.add).then_inc(s_acc, 1)
            with dve.Fori(0, NB) as b:
                experts(b)

        @block.scalar
        def _(act):
            for g in range(5):
                act.wait_ge(s_mv, 5 * g + 5)
                act.wait_ge(s_id, 7)
                act.activation(mv[0:P, 5 * g:5 * g + 5, 2], mv[0:P, 5 * g:5 * g + 5, 1], ACT.Sqrt, bias=eps[0:P, :]).then_inc(s_sd, 1)
            for L in L4:
                if L == 0:
                    act.sem_inc(s_hfree, 1)
                    act.sem_inc(s_ho, 1)
                    act.sem_inc(s_kvc, 2)
                if L == 2:
                    act.sem_inc(s_qTe, 1)
                with act.Fori(0, NB) as b:
                    act.wait_ge(s_hT, L * NB + b + 2)
                    act.activation(rT[:, 0, 0:KC * P], psH[:, 0:KC * P], ACT.Copy).then_inc(s_he, 1)
                    act.wait_ge(s_mT, L * NB + b + 1)
                    act.activation(rT[:, 1, 0:KC * P], psM[:, 0:KC * P], ACT.Copy).then_inc(s_me, 1)
                    if L < 2:
                        act.wait_ge(s_omm, L * NB + b + 1)
                        act.wait_ge(s_hfree, L * NB + b + 1)
                        act.activation(ho[0:P, :], psO[0:P, 0:D], ACT.Relu).then_inc(s_ho, 1)
                    if L == 0:
                        act.wait_ge(s_qkv, b + 1)
                        act.activation(blk(k_all, b), psV[0:P, 0:D], ACT.Copy).then_inc(s_kvc, 1)
                        act.activation(blk(v_all, b), psV[0:P, D:2 * D], ACT.Copy).then_inc(s_kvc, 1)
                        act.wait_ge(s_mix0, b * 6 + 3)
                        act.activation(qsm[:, :], qsm[:, :], ACT.Exp).then_inc(s_qx, 1)
                    if L == 1:
                        act.wait_ge(s_ek, b + 1)
                        act.activation(ek[:, :], ek[:, :], ACT.Exp).then_inc(s_ekx, 1)
                    if L == 2:
                        act.wait_ge(s_qTe, b + 1)
                        act.activation(qsm[:, :], blk(q_all, b), ACT.Copy).then_inc(s_qs, 1)
                        act.wait_ge(s_qT, b + 1)
                        act.activation(qT[:, :], psV[:, 0:KC * P], ACT.Copy).then_inc(s_qTe, 1)
                        for k in range(2):
                            act.wait_ge(s_ln, b * 12 + 3 + 7 * k)
                            act.activation(lst[:, k, 8:9], lst[:, k, 7:8], ACT.Sqrt, bias=eps[0:P, :]).then_inc(s_lna, 1)
                        act.wait_ge(s_xlT, b + 1)
                        act.activation(xlT[:, :, ds(b * P, P)], psA[:, 0:KC * P].rearrange("p (c n) -> p c n", c=KC), ACT.Copy).then_inc(s_xlTe, 1)
                        act.wait_ge(s_rw, b + 1)
                        act.activation(wrow[:, ds(b * P, P)], psC[0:P, 0:P], ACT.Identity, bias=br[:, :]).then_inc(s_wrow, 1)

            act.sem_inc(s_ge, 4)
            act.sem_inc(s_yw, TB)
            act.wait_ge(s_fw, 4 * 16)
            act.wait_ge(s_gdone, 3)

            def ffn(g, blocks):
                for m in range(HC):
                    act.wait_ge(s_st1, g * HC + m + 1)
                    act.activation(hT[:, m, 0:blocks * P], B[m % 4][:, 0:blocks * P], ACT.Gelu_apprx_tanh, bias=b1c[:, m:m + 1]).then_inc(s_ge, 1)
                act.wait_ge(s_wc, NB + 1)
                act.wait_ge(s_st2, g + 1)
                for k in range(blocks):
                    act.activation(blk(yw, g * TB + k), B[4 + k][0:P, 0:D], ACT.Identity, scale=wcol[:, ds(g * TB + k, 1)]).then_inc(s_yw, 1)
            with act.Fori(0, NB // TB) as g:
                ffn(g, TB)
            ffn(NB // TB, NB % TB)

            xT = lambda b: xlT[:, :, ds(b * P, P)]
            two = lambda t: t[:, 0:KC * P].rearrange("p (c n) -> p c n", c=KC)
            act.wait_ge(s_w5, 12 * 16)
            with act.Fori(0, NB) as b:
                act.wait_ge(s_x2, b * 9 + 3)
                act.activation(lst[:, 0, 8:9], lst[:, 0, 7:8], ACT.Sqrt, bias=eps[0:P, :]).then_inc(s_x2sd, 1)
                act.wait_ge(s_x2T, b + 1)
                act.activation(rT[:, 0, 0:KC * P], psH[:, 0:KC * P], ACT.Copy).then_inc(s_x2Te, 1)
                act.activation(xT(b), two(psH), ACT.Copy).then_inc(s_x2Te, 1)
                act.wait_ge(s_hkv, b * 2 + 1)
                act.wait_ge(s_hfree, 2 * NB + b + 1)
                act.activation(hs, psO[0:P, 0:D + 8], ACT.Copy).then_inc(s_hs, 1)
                act.activation(blk(asd, b), psO[0:P, D:D + 8], ACT.Copy).then_inc(s_hsa, 1)
                act.wait_ge(s_hkv, b * 2 + 2)
                act.activation(sq, psV[0:P, :], ACT.Square).then_inc(s_kvsd, 1)
                act.wait_ge(s_x2, b * 9 + 7)
                act.activation(ss[:, 16:32], ss[:, 0:16], ACT.Sqrt, scale=1.0 / 32, bias=eps[0:P, :]).then_inc(s_kvsd, 1)
            act.wait_ge(s_k4, 18)
            act.activation(wself, wself, ACT.Exp).then_inc(s_k4x, 1)

            def mix(g, blocks):
                for m in range(KC):
                    act.wait_ge(s_p1, g * KC + m + 1)
                    act.activation(gT[:, m, 0:blocks * P], B[m][:, 0:blocks * P], ACT.Gelu, bias=bpp[:, m:m + 1]).then_inc(s_p1e, 1)
            with act.Fori(0, NB // TB) as g:
                mix(g, TB)
            mix(NB // TB, NB % TB)

            def weights(b, q):
                n = q + b
                act.wait_ge(s_ohT, n + 1)
                act.activation(ohT[:, :], psT[0:P, :], ACT.Copy).then_inc(s_ohTe, 1)
                act.wait_ge(s_z, n * 5 + 4)
                act.activation(wh[:, :, D:GW], ez[:, :, :], ACT.Exp).then_inc(s_ew, 1)
            with act.Fori(0, NB) as b:
                q0, q1 = group_range(act, b)
                weights(b, q0)
                with act.If(q1 > q0 + 1):
                    with act.Fori(q0 + 1, q1) as q:
                        weights(b, q)

            act.sem_inc(s_mxTe, 1)
            with act.Fori(0, NB) as b:
                act.wait_ge(s_m, b * 4 + 2)
                act.activation(lst[:, 0, 8:9], lst[:, 0, 7:8], ACT.Sqrt, bias=eps[0:P, :]).then_inc(s_msd, 1)
                act.wait_ge(s_mxT, b + 1)
                act.activation(rT[:, 0, 0:KC * P], psH[:, 0:KC * P], ACT.Copy).then_inc(s_mxTe, 1)
                act.activation(xT(b), two(psH), ACT.Copy).then_inc(s_mxTe, 1)
                act.wait_ge(s_mg, b + 1)
                act.activation(blk(gl, b), psO[0:P, 0:4], ACT.Copy).then_inc(s_mge, 1)
            for k, (t, n) in enumerate(((gx, 2), (gp, 32))):
                act.wait_ge(s_gx, n)
                act.activation(t, t, ACT.Exp).then_inc(s_gxe, 1)
            act.sem_inc(s_e2, 4)

            def experts(g, blocks):
                n = blocks * P
                bias = [sb1[:, 0:1], sb1[:, 1:2]] + [eb1[:, k:k + 1] for k in range(4)] + [sb2[:, 0:1]] + [eb2[0:64, k:k + 1] for k in range(4)]
                for k in range(11):
                    rows_ = 64 if k >= 7 else 128
                    act.wait_ge(s_e1, g * 11 + k + 1)
                    act.activation(ffh[k][0:rows_, 0:n], B[k % 4][0:rows_, 0:n], ACT.Relu, bias=bias[k]).then_inc(s_e2, 1)
            with act.Fori(0, NB // TB) as g:
                experts(g, TB)
            experts(NB // TB, NB % TB)

        @block.tensor
        def _(pe):
            pe.wait_ge(s_id, 14)
            pe.wait_ge(s_row, 1)
            for c in range(4):
                for a in range(2):
                    k = 2 * c + a
                    if k >= 4:
                        pe.wait_ge(s_ev, k - 3)
                    pe.transpose(B[k % 4][:, 0:chunk_rows[c]], rows[0:chunk_rows[c], a, c, :], ident[0:chunk_rows[c], 0:chunk_rows[c]]).then_inc(s_et, 1)
            pe.wait_ge(s_red, 8)
            for q in range(2):
                for c in range(4):
                    pe.transpose(B[4 + q][0:1, 128 * c:128 * c + 128], red[:, 8 + 4 * q + c:9 + 4 * q + c], ident[:, :]).then_inc(s_rt, 1)
            pe.wait_ge(s_w, 9 * 16)
            for k in range(6):
                if k >= 2:
                    pe.wait_ge(s_wv, k - 1)
                for cd in range(KC):
                    for co in range(KC):
                        last = pe.transpose(B[6 + k % 2][:, cd * D + co * 128:cd * D + co * 128 + 128], wst[:, k, co, cd * 128:cd * 128 + 128], ident[:, :])
                last.then_inc(s_wt, 1)
            pe.wait_ge(s_wv, 6)
            pe.wait_ge(s_qe, 2)
            for L in L4:
                pe.sem_inc(s_mm[L], U - 1)
                pe.sem_inc(s_free[L], RG)
                if L == 0:
                    pe.sem_inc(s_hT, 1)
                    pe.sem_inc(s_mean, 1)
                    pe.wait_ge(s_mixw, 5 * 16)
                if L == 1:
                    pe.wait_ge(s_mix0, 6 * NB + 1)
                    for c in range(KC):
                        m = pe.transpose(psA[:, c * P:c * P + P], rm[:, c * 128:c * 128 + 128], ident[0:P, 0:P])
                    m.then_inc(s_kmT, 1)
                    pe.wait_ge(s_km, 3)
                    pe.matmul(psA[0:P, 0:D], ones128[:, :], dg[:, :, :].rearrange("p c n -> p (c n)"), start=True, stop=True).then_inc(s_kmB, 1)
                    pe.matmul(psC[:, 0:D + KC], zrow[:, 0:128], zrow[:, 0:D + KC], start=True, stop=False, skip_group_check=True)
                if L == 2:
                    pe.matmul(psC[:, 0:D + KC], zrow[:, 0:128], zrow[:, 0:D + KC], start=False, stop=True, skip_group_check=True).then_inc(s_ctx, 1)
                    pe.wait_ge(s_bd, 4)
                    for c in range(KC):
                        m = pe.transpose(psA[:, c * 128:c * 128 + 128], bd[:, c, :], ident[:, :])
                    m.then_inc(s_bdp, 1)
                    pe.wait_ge(s_bd, 5)
                    for c in range(KC):
                        m = pe.matmul(B[4 + c][:, 0:D], bdT[:, c, :], Wout[:, c, :], start=True, stop=True)
                    m.then_inc(s_bdp, 1)

                def sums(b, q, first):
                    for u in range(U):
                        pe.wait_ge(s_landed[L], q * U + u + 1)
                        pe.wait_ge(s_oh[L], (q + b) * U + u + 1)
                        m = pe.matmul(psS[0:P, 0:D + 1], oh[:, u, :], G[:, ring(q, u), 0:D + 1].rearrange("p a d -> p (a d)"),
                                  start=first and u == 0, stop=False, skip_group_check=True)
                        if u:
                            m.then_inc(s_mm[L], 1)
                        elif not first:
                            m.then_inc(s_free[L], 1)

                with pe.Fori(0, NB) as b:
                    q0, q1 = group_range(pe, b)
                    pe.wait_ge(s_mean, (L * NB + b) * 3 + 1)
                    sums(b, q0, True)
                    with pe.If(q1 > q0 + 1):
                        with pe.Fori(q0 + 1, q1) as q:
                            sums(b, q, False)
                    pe.matmul(psS[0:P, 0:D + 1], zrow[:, 0:P], zrow[:, 0:D + 1], start=False, stop=True, skip_group_check=True).then_inc(s_sum, 1)
                    pe.wait_ge(s_hin, (L * NB + b + 1) * 16)
                    for c in range(KC):
                        m = pe.transpose(psH[:, c * P:c * P + P], st[0:P, 0, c * 128:c * 128 + 128], ident[0:P, 0:P])
                    m.then_inc(s_hT, 1)
                    pe.wait_ge(s_mean, (L * NB + b) * 3 + 4)
                    for c in range(KC):
                        m = pe.transpose(psM[:, c * P:c * P + P], st[0:P, 1, c * 128:c * 128 + 128], ident[0:P, 0:P])
                    m.then_inc(s_mT, 1)
                    if L == 2:
                        pe.wait_ge(s_qs, b + 1)
                        for c in range(KC):
                            m = pe.transpose(psV[:, c * P:c * P + P], qsm[:, c * 128:c * 128 + 128], ident[0:P, 0:P])
                        m.then_inc(s_qT, 1)
                    pe.wait_ge(s_he, L * NB + b + 1)
                    if L < 2:
                        pe.wait_ge(s_ho, L * NB + b + 1)
                    else:
                        pe.wait_ge(s_ln, b * 12 + 1)
                    for c in range(KC):
                        pe.matmul(psO[0:P, 0:D], rT[:, 0, c * P:c * P + P], WrT[:, L, c, :], start=(c == 0), stop=False)
                    pe.matmul(psO[0:P, 0:D], ones[:, :], bl[:, L, :], start=False, stop=False)
                    pe.wait_ge(s_me, L * NB + b + 1)
                    for c in range(KC):
                        m = pe.matmul(psO[0:P, 0:D], rT[:, 1, c * P:c * P + P], WlT[:, L, c, :], start=False, stop=(c == KC - 1))
                    m.then_inc(s_omm, 1)
                    if L == 0:
                        pe.wait_ge(s_mix0, b * 6 + 1)
                        pe.wait_ge(s_kvc, b * 2 + 2)
                        for c in range(KC):
                            pe.matmul(psQK[0:P, 0:D], rT[:, 0, c * P:c * P + P], Wqkv[:, c, 0:D], start=(c == 0), stop=(c == KC - 1))
                        for c in range(KC):
                            m = pe.matmul(psV[0:P, :], rT[:, 0, c * P:c * P + P], Wqkv[:, c, D:3 * D], start=(c == 0), stop=(c == KC - 1))
                        m.then_inc(s_qkv, 1)
                    if L == 1:
                        pe.wait_ge(s_ekx, b + 1)
                        for c in range(KC):
                            pe.matmul(psC[:, c * 128:c * 128 + 128], ek[:, c * 128:c * 128 + 128], v_all[:, ds(b, 1), c * 128:c * 128 + 128].rearrange("p a d -> p (a d)"),
                                      start=False, stop=False, skip_group_check=True)
                        for c in range(KC):
                            m = pe.matmul(psC[:, D + c:D + c + 1], ek[:, c * 128:c * 128 + 128], ones128[0:P, 0:1], start=False, stop=False, skip_group_check=True)
                        m.then_inc(s_ctx, 1)
                    if L == 2:
                        pe.wait_ge(s_qTe, b + 2)
                        pe.wait_ge(s_bd, 7)
                        for c in range(KC):
                            m = pe.matmul(psQK[0:P, 0:D], qT[:, c * P:c * P + P], Mx[:, c, :], start=(c == 0), stop=(c == KC - 1))
                        m.then_inc(s_omx, 1)
                        pe.wait_ge(s_ln, b * 12 + 12)
                        for c in range(KC):
                            m = pe.transpose(psA[:, c * P:c * P + P], xls[:, c * 128:c * 128 + 128], ident[0:P, 0:P])
                        m.then_inc(s_xlT, 1)
                        pe.wait_ge(s_xlTe, b + 1)
                        for c in range(KC):
                            m = pe.matmul(psC[0:P, 0:P], wrr[:, c, :], xlT[:, c, ds(b * P, P)], start=(c == 0), stop=(c == KC - 1))
                        m.then_inc(s_rw, 1)

            pe.wait_ge(s_fw, 4 * 16)
            pe.wait_ge(s_wrow, NB)

            def ffn(g, blocks):
                n = blocks * P
                for m in range(HC):
                    pe.wait_ge(s_ge, g * HC + m + 1)
                    for c in range(KC):
                        x = pe.matmul(B[m % 4][:, 0:n], w1[:, c, m * 128:m * 128 + 128], xlT[:, c, ds(g * TOK, n)], start=(c == 0), stop=(c == KC - 1))
                    x.then_inc(s_st1, 1)
                for k in range(blocks):
                    pe.wait_ge(s_yw, g * TB + k + 1)
                    pe.matmul(B[4 + k][0:P, 0:D], ones[:, :], b2r[:, :], start=True, stop=False)
                for m in range(HC):
                    pe.wait_ge(s_ge, g * HC + m + 5)
                    for k in range(blocks):
                        x = pe.matmul(B[4 + k][0:P, 0:D], hT[:, m, k * P:k * P + P], w2[:, m, :], start=False, stop=(m == HC - 1))
                x.then_inc(s_st2, 1)
            with pe.Fori(0, NB // TB) as g:
                ffn(g, TB)
            ffn(NB // TB, NB % TB)

            pe.wait_ge(s_yw, NB + TB)
            pe.wait_ge(s_w4, 18 * 16)
            for k, (w, bank) in enumerate(((Wg, 0), (Wq, 2))):
                for i in range(KC):
                    for j in range(KC):
                        m = pe.transpose(B[bank][:, j * D + i * 128:j * D + i * 128 + 128], w[:, i, j * 128:j * 128 + 128], ident[:, :])
                m.then_inc(s_pt, 1)
            pe.wait_ge(s_pv, 1)
            pe.wait_ge(s_w5, 12 * 16)
            for i in range(KC):
                for j in range(KC):
                    pe.matmul(B[4][:, i * 8:i * 8 + 8], WgT[:, j, i * 128:i * 128 + 128], A8[:, j, :], start=(j == 0), stop=(j == KC - 1))
            for c in range(KC):
                m = pe.matmul(B[5][:, c:c + 1], bq[:, c * 128:c * 128 + 128], ones[:, 0:1], start=True, stop=True)
            m.then_inc(s_pt, 1)
            pe.wait_ge(s_pv, 10)
            pe.sem_inc(s_hsa, 1)
            pe.sem_inc(s_kva, 1)
            pe.matmul(psC[:, 0:D], zrow[:, 0:128], zrow[:, 0:D], start=True, stop=False, skip_group_check=True)
            with pe.Fori(0, NB) as b:
                pe.wait_ge(s_x2, b * 9 + 5)
                for c in range(KC):
                    m = pe.transpose(psH[:, c * P:c * P + P], xls[:, c * 128:c * 128 + 128], ident[0:P, 0:P])
                m.then_inc(s_x2T, 1)
                pe.wait_ge(s_x2Te, b * 2 + 2)
                pe.wait_ge(s_hsa, b + 1)
                for c in range(KC):
                    m = pe.matmul(psO[0:P, 0:D + 8], rT[:, 0, c * P:c * P + P], Wg[:, c, :], start=(c == 0), stop=(c == KC - 1))
                m.then_inc(s_hkv, 1)
                for c in range(KC):
                    pe.matmul(psV[0:P, :], rT[:, 0, c * P:c * P + P], Wkv[:, c, :], start=(c == 0), stop=False)
                pe.matmul(psV[0:P, :], ones[:, :], bkv, start=False, stop=True).then_inc(s_hkv, 1)
                pe.wait_ge(s_kvg, b * 2 + 2)
                for c in range(KC):
                    m = pe.matmul(psC[:, c * 128:c * 128 + 128], kvn[:, c * 128:c * 128 + 128], kvn[:, D + c * 128:D + c * 128 + 128], start=False, stop=False, skip_group_check=True)
                m.then_inc(s_kva, 1)
            pe.matmul(psC[:, 0:D], zrow[:, 0:128], zrow[:, 0:D], start=False, stop=True, skip_group_check=True).then_inc(s_kvd, 1)
            pe.wait_ge(s_k4, 2)
            for c in range(KC):
                pe.matmul(B[0][:, c * D:c * D + D], bd[:, c, :], WqT[:, c, :], start=True, stop=True)
                m = pe.matmul(B[5][:, c:c + 1], bd[:, c, :], bqc[:, c:c + 1], start=True, stop=True)
            m.then_inc(s_k4p, 1)
            pe.wait_ge(s_k4, 3)
            pe.transpose(B[7][0:4, 0:P], mx4, ident[0:P, 0:P]).then_inc(s_k4p, 1)
            pe.wait_ge(s_k4, 7)
            for i in range(KC):
                for j in range(KC):
                    pe.matmul(B[2][:, i * D:i * D + D], WqpT[:, j, i * 128:i * 128 + 128], m1[:, j, :], start=(j == 0), stop=(j == KC - 1))
                for j in range(KC):
                    m = pe.matmul(B[5][:, 4 + i:5 + i], m1[:, j, i * 128:i * 128 + 128], bqp[:, j:j + 1], start=(j == 0), stop=(j == KC - 1))
            m.then_inc(s_k4p, 1)
            pe.wait_ge(s_k4, 9)
            pe.matmul(B[7][0:P, 128:132], ones128[0:4, 0:P], dg4, start=True, stop=True).then_inc(s_k4p, 1)

            pe.wait_ge(s_k4, 11)
            pe.sem_inc(s_p1e, 2)
            pe.sem_inc(s_p2x, TB)

            def mix(g, blocks):
                n = blocks * P
                for m in range(KC):
                    pe.wait_ge(s_p1e, g * KC + m + 1)
                    for c in range(KC):
                        x = pe.matmul(B[m][:, 0:n], Wpp[:, c, m * 128:m * 128 + 128], xlT[:, c, ds(g * TOK, n)], start=(c == 0), stop=(c == KC - 1))
                    x.then_inc(s_p1, 1)
                pe.wait_ge(s_p1e, g * KC + 4)
                for k in range(blocks):
                    pe.wait_ge(s_p2x, g * TB + k + 1)
                    pe.matmul(B[4 + k][0:P, 0:D], ones[:, :], b2m, start=True, stop=False)
                    for m in range(KC):
                        x = pe.matmul(B[4 + k][0:P, 0:D], gT[:, m, k * P:k * P + P], m2[:, m, :], start=False, stop=(m == KC - 1))
                x.then_inc(s_p2, 1)
            with pe.Fori(0, NB // TB) as g:
                mix(g, TB)
            mix(NB // TB, NB % TB)

            pe.sem_inc(s_mm[3], U - 1)
            pe.sem_inc(s_free[3], RG)

            def edges(b, q, first):
                n = q + b
                for u in range(U):
                    pe.wait_ge(s_oh[3], n * U + u + 1)
                    m = pe.transpose(psT[0:P, u * ET:u * ET + ET], oh[:, u, :], ident[:, :])
                m.then_inc(s_ohT, 1)
                pe.wait_ge(s_ohTe, n + 1)
                for u in range(U):
                    m = pe.matmul(psX[:, 8 * u:8 * u + 8], ohT[:, u * ET:u * ET + ET], blk(tab8, b), start=True, stop=True)
                m.then_inc(s_psx, 1)
                pe.wait_ge(s_z, n * 5 + 5)
                for u in range(U):
                    m = pe.matmul(psS[0:P, 0:GW], oh[:, u, :], wh[:, u, :], start=first and u == 0, stop=False, skip_group_check=True)
                    if u:
                        m.then_inc(s_mm[3], 1)
                    elif not first:
                        m.then_inc(s_free[3], 1)

            with pe.Fori(0, NB) as b:
                q0, q1 = group_range(pe, b)
                pe.wait_ge(s_gat, b * 7 + 1)
                edges(b, q0, True)
                with pe.If(q1 > q0 + 1):
                    with pe.Fori(q0 + 1, q1) as q:
                        edges(b, q, False)
                pe.matmul(psS[0:P, 0:GW], zrow[:, 0:P], zrow[:, 0:GW], start=False, stop=True, skip_group_check=True).then_inc(s_sum, 1)

            pe.wait_ge(s_w6, 14 * 16)
            with pe.Fori(0, NB) as b:
                pe.wait_ge(s_m, b * 4 + 4)
                for c in range(KC):
                    m = pe.transpose(psH[:, c * P:c * P + P], xls[:, c * 128:c * 128 + 128], ident[0:P, 0:P])
                m.then_inc(s_mxT, 1)
                pe.wait_ge(s_mxTe, b * 2 + 3)
                for c in range(KC):
                    pe.matmul(psO[0:P, 0:4], rT[:, 0, c * P:c * P + P], gW[:, c, :], start=(c == 0), stop=False)
                pe.matmul(psO[0:P, 0:4], ones[:, :], gbr, start=False, stop=True).then_inc(s_mg, 1)

            pe.wait_ge(s_mge, NB)
            pe.sem_inc(s_acc, 1)

            def experts(g, blocks):
                n = blocks * P
                for k in range(11):
                    to = B[k % 4]
                    pe.wait_ge(s_e2, g * 11 + (k + 2 if k < 3 else k + 1))
                    if k < 6:
                        for c in range(KC):
                            w = sW1[:, c, k * 128:k * 128 + 128] if k < 2 else eW1[:, k - 2, c, :]
                            m = pe.matmul(to[:, 0:n], w, xlT[:, c, ds(g * TOK, n)], start=(c == 0), stop=(c == KC - 1))
                    elif k == 6:
                        for c in range(KC):
                            m = pe.matmul(to[:, 0:n], sW2[:, c, :], ffh[c][:, 0:n], start=(c == 0), stop=(c == KC - 1))
                    else:
                        m = pe.matmul(to[0:64, 0:n], eW2[:, k - 7, :], ffh[k - 5][:, 0:n], start=True, stop=True)
                    m.then_inc(s_e1, 1)
                pe.wait_ge(s_e2, g * 11 + 15)
                for k in range(blocks):
                    b = g * TB + k
                    pe.wait_ge(s_acc, b * 5 + 1)
                    for e in range(2):
                        pe.matmul(B[4 + e][0:P, :], ones[:, :], b3[:, (1 + 2 * e) * D:(3 + 2 * e) * D], start=True, stop=False, skip_group_check=True)
                        for i in range(2):
                            pe.matmul(B[4 + e][0:P, i * D:i * D + D], ffh[7 + 2 * e + i][0:64, k * P:k * P + P], eW3[0:64, 2 * e + i, :], start=False, stop=(i == 1), skip_group_check=True)
                    pe.matmul(B[6][0:P, 0:D], ones[:, :], b3[:, 0:D], start=True, stop=False)
                    pe.matmul(B[6][0:P, 0:D], ffh[6][:, k * P:k * P + P], sW3[:, 0, :], start=False, stop=True).then_inc(s_tm, 1)
            with pe.Fori(0, NB // TB) as g:
                experts(g, TB)
            experts(NB // TB, NB % TB)


_INS = (["x", "src", "dst"] + [f"L0_gnn_{n}" for k in (1, 2, 3) for n in (f"W{k}l", f"b{k}l", f"W{k}r")]
        + [f"L0_mix_{n}" for n in "Wqkv Wout gamma".split()] + [f"L0_ffn_{n}" for n in "wr br w1 b1 w2 b2".split()]
        + [f"L1_gnn_{n}" for n in "W att_src att_dst bias".split()]
        + [f"L1_mix_{n}" for n in "w_qkv b_qkv kln_g kln_b vln_g vln_b w1 b1 w2 b2".split()]
        + [f"L1_ffn_{n}" for n in "sW1 sb1 sW2 sb2 sW3 sb3 eW1 eb1 eW2 eb2 eW3 eb3 gW gb".split()])


def kernel(**inputs):
    import numpy as _np
    import concourse.bacc as _bacc
    from concourse import mybir as _mybir
    from concourse.bass_utils import run_bass_kernel_spmd as _run
    nc = _bacc.Bacc("TRN2", target_bir_lowering=False, num_devices=1)
    arrays, args = {}, {}
    for name in _INS:
        a = _np.ascontiguousarray(inputs[name])
        arrays[f"in_{name}_dram"] = a
        args[name] = nc.dram_tensor(f"in_{name}_dram", a.shape, _mybir.dt.from_np(a.dtype), kind="ExternalInput").ap()
    out = nc.dram_tensor("out_0_dram", (N, D), F32, kind="ExternalOutput").ap()
    build(nc, args, out)
    r = _run(nc, [arrays], core_ids=[0])
    return r.results[0]["out_0_dram"]
```

```python
from contextlib import ExitStack

import concourse.bass as bass
from concourse import mybir

F32 = mybir.dt.float32
I32 = mybir.dt.int32
BF16 = mybir.dt.bfloat16
ALU = mybir.AluOpType
ACT = mybir.ActivationFunctionType
AX = mybir.AxisListType

N, D, E = 3125, 256, 50000
P = 125
NB = N // P
KC = D // 128
ET = 128
NT = -(-E // ET)
U = 4
NG = -(-NT // U)
GS = 16
RG = GS // U
LAG = 4
GW = 260
EPS = 1e-5
H1 = 4 * D
HC = H1 // 128
TB = 4
TOK = TB * P
CHOSEN = max(1, N // 2) - 1
ds = bass.ds


def build(nc, I, out):
    with ExitStack() as ctx:
        def sb(name, shape, dt=F32):
            return ctx.enter_context(nc.sbuf_tensor(name, shape, dt))

        def sem(name):
            return ctx.enter_context(nc.semaphore(name))

        bigk = sb("bigk", [128, NB * D])
        bigv = sb("bigv", [128, NB * D])
        bigx = sb("bigx", [128, NB * D])
        bigq = sb("bigq", [128, NB * D])
        ho = sb("ho", [128, D])
        iota = sb("iota", [128, N])
        G = sb("G", [128, GS, GW])
        oh = sb("oh", [128, U, P])
        ident = sb("ident", [128, 128])
        eps = sb("eps", [128, 1])
        ones = sb("ones", [1, P])
        zrow = sb("zrow", [1, 512], BF16)
        idx = sb("idx", [128, NG * U], I32)
        idxc = sb("idxc", [128, 16], I32)
        dstf = sb("dstf", [128, NG * U])
        qrun = sb("qrun", [1, 2, NB + 1], I32)
        st = sb("st", [128, 2, D])
        rT = sb("rT", [128, 2, KC * 128])
        st6 = sb("st6", [128, NB, 6])
        mv = sb("mv", [128, NB, 3])
        rdeg = sb("rdeg", [128, 2])
        gamma = sb("gamma", [P, D])
        rm = sb("rm", [P, D])
        kmb = sb("kmb", [P, D])
        kmx = sb("kmx", [128, KC])
        dg = sb("dg", [128, KC, 128])
        ones128 = sb("ones128", [128, P])
        bdm = sb("bdm", [128, 128])
        qst = sb("qst", [P, 3, 8])
        qsm = sb("qsm", [P, D])
        ek = sb("ek", [P, D])
        dn = sb("dn", [128, KC])
        bd = sb("bd", [128, KC, 128])
        bdT = sb("bdT", [128, KC, 128])
        qT = sb("qT", [128, KC * P])
        ty = sb("ty", [P, D])
        xs = sb("xs", [P, D])
        x1s = sb("x1s", [P, D])
        xls = sb("xls", [P, D])
        lst = sb("lst", [P, 2, 10])
        wr = sb("wr", [128, KC])
        wrr = sb("wrr", [128, KC, P])
        br = sb("br", [P, 1])
        b1c = sb("b1c", [128, HC])
        b2r = sb("b2r", [1, D])
        wcol = sb("wcol", [P, NB])
        cnt = sb("cnt", [P, NB, 4])
        sel = sb("sel", [P, NB])
        tril = sb("tril", [P, P])
        triu = sb("triu", [P, P])
        bl = sb("bl", [1, 3, D])
        ohT = sb("ohT", [P, U * ET], BF16)
        ez = sb("ez", [128, U, 4])
        rs8 = sb("rs8", [P, 8])
        actw = sb("actw", [P, 1])
        identh = sb("identh", [128, 128], BF16)
        tabh = sb("tabh", [P, 3, NB, 8], BF16)
        wA = sb("wA", [128, 11 * KC * D])
        wB = sb("wB", [128, 2 * KC * H1])
        PS = ctx.enter_context(nc.psum_tensor("PS", [128, 8, 512], F32))
        B = [PS[:, k, :] for k in range(8)]
        psH, psHM, psO = B[1:4]
        psQK, psV = B[4], B[5]
        psC, psA = B[6], B[7]
        psT = B[2][:, 0:U * ET // 2].bitcast(BF16)

        tab = [nc.dram_tensor(f"tab{k}", [N, D], F32, kind="Internal").ap() for k in range(3)]
        gtab = nc.dram_tensor("gtab", [N, GW], F32, kind="Internal").ap()
        tabb = [t.rearrange("(b p) d -> p b d", p=P) for t in tab]

        by_block = [t[0:P, :].rearrange("p (b d) -> p b d", b=NB) for t in (bigk, bigv, bigx, bigq)]
        k_all, v_all, x1_all, q_all = by_block
        xin, h = q_all, x1_all
        xlT = bigk[:, 0:KC * N].rearrange("p (c n) -> p c n", c=KC)

        def blk(t, b):
            return t[:, ds(b, 1), :].rearrange("p a d -> p (a d)")

        wrow = bigv[0:P, 0:N]
        yw = q_all
        hT = G[:, :, :].rearrange("p s d -> p (s d)")[:, 0:HC * TOK].rearrange("p (m n) -> p m n", m=HC)
        junk = bigv[0:P, N:2 * N]
        junk2 = bigv[0:P, 2 * N:2 * N + P]

        def part(buf, at, *shape):
            n = 1
            for k in shape:
                n *= k
            v = buf[:, at:at + n]
            names = "abc"[:len(shape)]
            return v.rearrange(f"p ({' '.join(names)}) -> p {' '.join(names)}", **dict(zip(names, shape)))
        W1 = KC * D
        WlT, WrT = part(wA, 0, 3, KC, D), part(wA, 3 * W1, 3, KC, D)
        Wqkv = part(wA, 6 * W1, KC, 3 * D)
        Wout = part(wA, 9 * W1, KC, D)
        Mx = part(wA, 10 * W1, KC, D)
        w1, w2 = part(wB, 0, KC, H1), part(wB, KC * H1, HC, D)

        Wg = part(wA, 0, KC, D + 8)
        at = KC * (D + 8)
        Wkv = part(wA, at, KC, 2 * D)
        at += 2 * W1
        Wq, WqT, WqpT, m1, m2, Wpp, WgT = [part(wA, at + k * W1, KC, D) for k in range(7)]
        at += 7 * W1
        A8 = part(wA, at, KC, 8)
        bqc, bqp, b1m, bpp = [part(wA, at + 16 + KC * k, KC) for k in range(4)]
        cmean = wA[:, at + 24:at + 56]
        gbk = bigv[0:P, 0:4 * D].rearrange("p (a d) -> p a d", a=2)
        kvn = bigv[0:P, 1024:1536]
        sq = bigv[0:P, 1536:2048]
        hs = bigv[0:P, 2048:2048 + D + 8]
        gbias = bigv[0:P, 2320:2320 + D]
        bkv = bigv[0:1, 2576:2576 + 2 * D]
        bq = bigv[0:1, 3088:3088 + D]
        b2m = bigv[0:1, 3344:3344 + D]
        b3 = bigv[0:P, 3600:3600 + 5 * D]
        asd = bigv[0:P, 4880:4880 + 8 * NB].rearrange("p (b h) -> p b h", b=NB)
        tab8 = bigv[0:P, 5080:5080 + 8 * NB].rearrange("p (b h) -> p b h", b=NB)
        tabr = bigv[0:P, 6000:6000 + 8 * NB].rearrange("p (b h) -> p b h", b=NB)
        wself = bigv[0:P, 5280:5280 + 4 * NB].rearrange("p (b h) -> p b h", b=NB)
        ss = bigv[0:P, 5380:5412]
        mx4 = bigv[0:P, 5412:5416]
        kx = bigv[0:4, 5416:5417]
        dg4 = bigv[0:4, 5420:5424]
        bmean = bigv[0:1, 5424:5440]
        gbr = bigv[0:1, 5440:5444]
        gl, gx, gr2, ga, gp = [bigv[0:P, 5444 + k * 4 * NB:5444 + (k + 1) * 4 * NB].rearrange("p (b h) -> p b h", b=NB) for k in range(5)]
        g1 = bigv[0:P, 5944:5944 + NB].rearrange("p (b h) -> p b h", b=NB)
        at = 0
        def take(*shape):
            nonlocal at
            n = 1
            for k in shape:
                n *= k
            at += n
            return part(wB, at - n, *shape)
        sW1, sW2, sW3 = take(KC, D), take(KC, 128), take(1, D)
        eW1, eW2, eW3 = take(4, KC, 128), take(4, 64), take(4, D)
        gW, sb1, sb2, eb1, eb2 = take(KC, 4), take(KC), take(1), take(4), take(4)
        gT = bigq[:, 0:KC * TOK].rearrange("p (m n) -> p m n", m=KC)
        ffh = [bigq[:, k * TOK:(k + 1) * TOK] for k in range(11)]

        ohA = bigq[:, 0:U * P // 2].bitcast(BF16).rearrange("p (u n) -> p u n", u=U)
        wh = bigq[:, 512:512 + 2 * U * GW].rearrange("p (u d) -> p u d", u=2 * U)

        rows = bigk[:, 0:2 * 4 * ET].rearrange("p (a c e) -> p a c e", a=2, c=4)
        rowsi = bigk[:, 1024:2048].bitcast(I32).rearrange("p (a c e) -> p a c e", a=2, c=4)
        red = bigk[:, 2048:2048 + 40]
        redi = bigk[:, 2096:2104].bitcast(I32)
        wst = bigv[:, 3200:3200 + 6 * KC * D].rearrange("p (m c d) -> p m c d", m=6, c=KC)

        s_edges = sem("s_edges")
        s_x = [sem(f"s_xin{g}") for g in range(5)]
        s_w = sem("s_w")
        s_id = sem("s_id")
        s_pad = sem("s_pad")
        s_row = sem("s_row")
        s_et = sem("s_et")
        s_ev = sem("s_ev")
        s_wt = sem("s_wt")
        s_wv = sem("s_wv")
        s_red = sem("s_red")
        s_rt = sem("s_rt")
        s_tb = sem("s_tb")
        s_qe = sem("s_qe")
        s_st = sem("s_st")
        s_mv = sem("s_mv")
        s_rs = sem("s_rs")
        s_sd = sem("s_sd")
        s_lnd = sem("s_lnd")
        s_tab0 = sem("s_tab0")
        s_cnt = sem("s_cnt")
        L4 = range(3)
        s_gath = [[sem(f"s_gath{k}_{u}") for u in range(LAG)] for k in range(4)]
        s_ic = [sem(f"s_ic{k}") for k in range(4)]
        s_landed = [sem(f"s_landed{k}") for k in range(4)]
        s_free = [sem(f"s_free{k}") for k in range(4)]
        s_oh = [sem(f"s_oh{k}") for k in range(4)]
        s_mm = [sem(f"s_mm{k}") for k in range(4)]
        s_sum = sem("s_sum")
        s_mean = sem("s_mean")
        s_gat = sem("s_gat")
        s_hin = sem("s_hin")
        s_hT = sem("s_hT")
        s_he = sem("s_he")
        s_mT = sem("s_mT")
        s_omm = sem("s_omm")
        s_ho = sem("s_ho")
        s_hfree = sem("s_hfree")
        s_sto = sem("s_sto")
        s_mixw = sem("s_mixw")
        s_gdone = sem("s_gdone")
        s_out = sem("s_out")
        s_fw = sem("s_fw")
        s_wc = sem("s_wc")
        s_rank = sem("s_rank")
        s_ge = sem("s_ge")
        s_st2 = sem("s_st2")
        s_yw = sem("s_yw")
        s_st1 = sem("s_st1")
        s_w4 = sem("s_w4")
        s_w5 = sem("s_w5")
        s_w6 = sem("s_w6")
        s_a8 = sem("s_a8")
        s_x2 = sem("s_x2")
        s_x2sd = sem("s_x2sd")
        s_x2T = sem("s_x2T")
        s_x2Te = sem("s_x2Te")
        s_hkv = sem("s_hkv")
        s_hs = sem("s_hs")
        s_kvsd = sem("s_kvsd")
        s_hsa = sem("s_hsa")
        s_kvg = sem("s_kvg")
        s_kvn = sem("s_kvn")
        s_kva = sem("s_kva")
        s_gst = sem("s_gst")
        s_pt = sem("s_pt")
        s_pv = sem("s_pv")
        s_kvd = sem("s_kvd")
        s_k4 = sem("s_k4")
        s_k4p = sem("s_k4p")
        s_k4x = sem("s_k4x")
        s_p1 = sem("s_p1")
        s_p1e = sem("s_p1e")
        s_p2 = sem("s_p2")
        s_p2x = sem("s_p2x")
        s_ohT = sem("s_ohT")
        s_ohTe = sem("s_ohTe")
        s_psx = sem("s_psx")
        s_z = sem("s_z")
        s_ew = sem("s_ew")
        s_ohA = sem("s_ohA")
        s_m = sem("s_m")
        s_msd = sem("s_msd")
        s_mxT = sem("s_mxT")
        s_mxTe = sem("s_mxTe")
        s_mg = sem("s_mg")
        s_mge = sem("s_mge")
        s_gx = sem("s_gx")
        s_gxe = sem("s_gxe")
        s_e1 = sem("s_e1")
        s_e2 = sem("s_e2")
        s_tm = sem("s_tm")
        s_acc = sem("s_acc")
        s_actw = sem("s_actw")
        s_b3 = sem("s_b3")
        s_mix0 = sem("s_mix0")
        s_qkv = sem("s_qkv")
        s_kvc = sem("s_kvc")
        s_qx = sem("s_qx")
        s_km = sem("s_km")
        s_kmT = sem("s_kmT")
        s_kmB = sem("s_kmB")
        s_ek = sem("s_ek")
        s_ekx = sem("s_ekx")
        s_ctx = sem("s_ctx")
        s_bd = sem("s_bd")
        s_bdp = sem("s_bdp")
        s_xs = sem("s_xs")
        s_qs = sem("s_qs")
        s_qT = sem("s_qT")
        s_qTe = sem("s_qTe")
        s_omx = sem("s_omx")
        s_ln = sem("s_ln")
        s_lna = sem("s_lna")
        s_xlT = sem("s_xlT")
        s_xlTe = sem("s_xlTe")
        s_rw = sem("s_rw")
        s_wrow = sem("s_wrow")
        s_wrr = sem("s_wrr")

        block = ctx.enter_context(nc.Block())
        full = E // ET // 128
        rest = E // ET - full * 128
        tail = E - (E // ET) * ET
        chunk_rows = [128] * full + [rest + 1]

        def group_range(eng, b):
            return [eng.value_load(qrun[0:1, k, ds(b, 1)], min_val=k, max_val=NB * NG) for k in range(2)]

        def layer(eng, body):
            for b in range(3):
                body(b, True, b > 0, b > 1, False)
            with eng.Fori(3, NB) as b:
                body(b, True, True, True, True)
            for k in range(3):
                body(NB + k, False, k < 1, k < 2, True)

        def rows_of(b):
            return PS[0:P, ds(3 + b % 2, 1), :].rearrange("p a n -> p (a n)")

        def sums_of(L, b):
            return PS[0:P, ds((L * NB + b) % 2, 1), 0:D + 1].rearrange("p a n -> p (a n)")

        def kv_of(b):
            return PS[0:P, ds(4 + b % 2, 1), :].rearrange("p a n -> p (a n)")

        def stream(eng, begin, step, end, late=None):
            def body(b, first, last):
                q0, q1 = [eng.value_load(qrun[0:1, 0, ds(b + k, 1)], min_val=0, max_val=NB * NG) for k in range(2)]
                begin(b)
                with eng.If(q1 > q0):
                    with eng.Fori(q0, q1) as q:
                        step(b, q, b, q + 1)
                if late and not first:
                    late(b - 1)
                step(b, q1, None if last else b + 1, q1)
                end(b)
            body(0, True, False)
            with eng.Fori(1, NB - 1) as b:
                body(b, False, False)
            body(NB - 1, False, True)
            if late:
                late(NB - 1)

        def ring(q, u):
            return ds(q % RG * U + u, 1)

        @block.sync
        def _(sp):
            sp.wait_ge(s_pad, 2)
            for a, e in enumerate((I["src"], I["dst"])):
                sp.dma_start(rowsi[:, a, 0:full, :], e[0:full * 128 * ET].rearrange("(c p e) -> p c e", p=128, e=ET)).then_inc(s_edges, 16)
                sp.dma_start(rowsi[0:rest, a, full, :], e[full * 128 * ET:(E // ET) * ET].rearrange("(p e) -> p e", e=ET)).then_inc(s_edges, 16)
                sp.dma_start(rowsi[rest:rest + 1, a, full, 0:tail], e[(E // ET) * ET:E].rearrange("(p e) -> p e", p=1)).then_inc(s_edges, 16)
            for g in range(5):
                sp.dma_start(xin[0:P, 5 * g:5 * g + 5, :], I["x"].rearrange("(b p) d -> p b d", p=P)[:, 5 * g:5 * g + 5, :]).then_inc(s_x[g], 16)
            for k in range(3):
                sp.dma_start(wst[:, k, :, :], I[f"L0_gnn_W{k+1}l"].rearrange("(c p) d -> p c d", p=128)).then_inc(s_w, 16)
                sp.dma_start(wst[:, 3 + k, :, :], I[f"L0_gnn_W{k+1}r"].rearrange("(c p) d -> p c d", p=128)).then_inc(s_w, 16)
                sp.dma_start(bl[:, k, :], I[f"L0_gnn_b{k+1}l"].rearrange("(a d) -> a d", a=1)).then_inc(s_w, 16)
            sp.dma_start(Wqkv[:, :, :], I["L0_mix_Wqkv"].rearrange("(c p) d -> p c d", p=128)).then_inc(s_mixw, 16)
            sp.dma_start(Wout[:, :, :], I["L0_mix_Wout"].rearrange("(c p) d -> p c d", p=128)).then_inc(s_mixw, 16)
            sp.dma_start(gamma[:, :], I["L0_mix_gamma"].rearrange("(a d) -> a d", a=1).broadcast_to((P, D))).then_inc(s_mixw, 16)
            sp.dma_start(wr[:, :], I["L0_ffn_wr"].rearrange("(c p) o -> p (c o)", p=128), allow_slow_non_contiguous=True).then_inc(s_mixw, 16)
            sp.dma_start(br[:, :], I["L0_ffn_br"].rearrange("(a d) -> a d", a=1).broadcast_to((P, 1))).then_inc(s_mixw, 16)
            sp.dma_start(w1[:, :, :], I["L0_ffn_w1"].rearrange("(c p) d -> p c d", p=128)).then_inc(s_fw, 16)
            sp.dma_start(w2[:, :, :], I["L0_ffn_w2"].rearrange("(c p) d -> p c d", p=128)).then_inc(s_fw, 16)
            sp.dma_start(b1c[:, :], I["L0_ffn_b1"].rearrange("(c p) -> p c", p=128), allow_slow_non_contiguous=True).then_inc(s_fw, 16)
            sp.dma_start(b2r[:, :], I["L0_ffn_b2"].rearrange("(a d) -> a d", a=1)).then_inc(s_fw, 16)
            for g in range(5):
                sp.wait_ge(s_lnd, 5 * g + 5)
                sp.dma_start(tabb[0][:, 5 * g:5 * g + 5, :], h[0:P, 5 * g:5 * g + 5, :]).then_inc(s_tab0, 16)
            for L in L4:
                if L == 0:
                    sp.wait_ge(s_tab0, 5 * 16)
                else:
                    sp.wait_ge(s_sto, L * NB * 16)
                def own_rows(b):
                    sp.wait_ge(s_hT, L * NB + b + 1)
                    sp.dma_start(st[0:P, 0, :], tab[L][ds(b * P, P), :]).then_inc(s_hin, 16)

                def results(b):
                    if L < 2:
                        sp.wait_ge(s_ho, L * NB + b + 2)
                        sp.dma_start(tab[L + 1][ds(b * P, P), :], ho[0:P, :]).then_inc(s_sto, 16)
                        sp.wait_ge(s_sto, (L * NB + b + 1) * 16)
                        sp.sem_inc(s_hfree, 1)
                    else:
                        sp.wait_ge(s_ln, b * 12 + 1)
                        sp.dma_start(xs[:, :], I["x"][ds(b * P, P), :]).then_inc(s_xs, 16)
                own_rows(0)
                with sp.Fori(0, NB - 1) as b:
                    own_rows(b + 1)
                    results(b)
                results(NB - 1)
            row = lambda t: t.rearrange("(a d) -> a d", a=1)
            sp.wait_ge(s_rw, NB)
            sp.wait_ge(s_a8, 1)
            sp.dma_start(Wg[:, :, 0:D], I["L1_gnn_W"].rearrange("(c p) d -> p c d", p=128)).then_inc(s_w4, 16)
            for a, w in enumerate((I["L1_gnn_att_src"], I["L1_gnn_att_dst"])):
                for k in range(4):
                    lo = 64 * (k % 2)
                    sp.dma_start(A8[lo:lo + 64, k // 2, 4 * a + k:4 * a + k + 1], w[k:k + 1, :].rearrange("a f -> f a"), allow_slow_non_contiguous=True).then_inc(s_w4, 16)
            wq = I["L1_mix_w_qkv"].rearrange("(c p) (h t e) -> c t p h e", p=128, t=3, e=32)
            for c in range(KC):
                for t in range(3):
                    to = Wq[:, c, :] if t == 0 else Wkv[:, c, (t - 1) * D:t * D]
                    sp.dma_start(to.rearrange("p (h e) -> p h e", h=8), wq[c, t]).then_inc(s_w4, 16)
            sp.dma_start(m1[:, :, :], I["L1_mix_w1"].rearrange("(c p) d -> p c d", p=128)).then_inc(s_w4, 16)
            sp.dma_start(m2[:, :, :], I["L1_mix_w2"].rearrange("(c p) d -> p c d", p=128)).then_inc(s_w4, 16)
            sp.dma_start(b1m[:, :], I["L1_mix_b1"].rearrange("(c p) -> p c", p=128), allow_slow_non_contiguous=True).then_inc(s_w4, 16)
            sp.wait_ge(s_rank, 4 * NB)
            for a, n in enumerate(("g", "b")):
                for k, t in enumerate(("kln", "vln")):
                    sp.dma_start(gbk[:, a, k * D:(k + 1) * D].rearrange("p (h e) -> p h e", h=8),
                                 I[f"L1_mix_{t}_{n}"].rearrange("(a b e) -> a b e", a=1, b=1).broadcast_to((P, 8, 32))).then_inc(s_w5, 16)
            bs = I["L1_mix_b_qkv"].rearrange("(a h t e) -> t a h e", a=1, t=3, e=32)
            for t in range(3):
                to = bq if t == 0 else bkv[:, (t - 1) * D:t * D]
                sp.dma_start(to.rearrange("p (h e) -> p h e", h=8), bs[t]).then_inc(s_w5, 16)
            sp.dma_start(gbias, row(I["L1_gnn_bias"]).broadcast_to((P, D))).then_inc(s_w5, 16)
            sp.dma_start(b2m, row(I["L1_mix_b2"])).then_inc(s_w5, 16)
            sp.dma_start(b3[:, 0:D], row(I["L1_ffn_sb3"]).broadcast_to((P, D))).then_inc(s_w5, 16)
            sp.dma_start(b3[:, D:5 * D], I["L1_ffn_eb3"].rearrange("(a e) d -> a (e d)", a=1).broadcast_to((P, 4 * D))).then_inc(s_w5, 16)
            sp.dma_start(gbr, row(I["L1_ffn_gb"])).then_inc(s_w5, 16)
            sp.wait_ge(s_st2, NB // TB + 1)
            sp.dma_start(sW1, I["L1_ffn_sW1"].rearrange("(c p) d -> p c d", p=128)).then_inc(s_w6, 16)
            sp.dma_start(sW2, I["L1_ffn_sW2"].rearrange("(c p) d -> p c d", p=128)).then_inc(s_w6, 16)
            sp.dma_start(sW3[:, 0, :], I["L1_ffn_sW3"]).then_inc(s_w6, 16)
            for k in range(4):
                sp.dma_start(eW1[:, k, :, :], I["L1_ffn_eW1"][k].rearrange("(c p) d -> p c d", p=128)).then_inc(s_w6, 16)
            sp.dma_start(eW2, I["L1_ffn_eW2"].rearrange("k p d -> p k d")).then_inc(s_w6, 16)
            sp.dma_start(eW3[0:64, :, :], I["L1_ffn_eW3"].rearrange("k p d -> p k d")).then_inc(s_w6, 16)
            sp.dma_start(gW, I["L1_ffn_gW"].rearrange("(c p) d -> p c d", p=128), allow_slow_non_contiguous=True).then_inc(s_w6, 16)
            sp.dma_start(sb1, I["L1_ffn_sb1"].rearrange("(c p) -> p c", p=128), allow_slow_non_contiguous=True).then_inc(s_w6, 16)
            sp.dma_start(sb2, I["L1_ffn_sb2"].rearrange("(p c) -> p c", c=1), allow_slow_non_contiguous=True).then_inc(s_w6, 16)
            sp.dma_start(eb1, I["L1_ffn_eb1"].rearrange("k p -> p k"), allow_slow_non_contiguous=True).then_inc(s_w6, 16)
            sp.dma_start(eb2[0:64, :], I["L1_ffn_eb2"].rearrange("k p -> p k"), allow_slow_non_contiguous=True).then_inc(s_w6, 16)
            with sp.Fori(0, NB) as b:
                sp.wait_ge(s_hs, b + 1)
                sp.dma_start(gtab[ds(b * P, P), :], hs[:, 0:GW]).then_inc(s_gst, 16)
                sp.wait_ge(s_gst, (b + 1) * 16)
                sp.sem_inc(s_hfree, 1)
            sp.wait_ge(s_gst, NB * 16)
            with sp.Fori(0, NB) as b:
                sp.wait_ge(s_gat, b * 7 + 5)
                sp.dma_start(st[0:P, 0, :], gtab[ds(b * P, P), 0:D]).then_inc(s_hin, 16)
            with sp.Fori(0, NB) as b:
                sp.wait_ge(s_acc, b * 5 + 11)
                sp.dma_start(out[ds(b * P, P), :], blk(x1_all, b)).then_inc(s_out, 16)
            sp.wait_ge(s_out, NB * 16)

        @block.gpsimd
        def _(pool):
            pool.memset(ident[:, :], 1.0).then_inc(s_id, 1)
            pool.memset(G[:, :, D:GW], 1.0).then_inc(s_id, 1)
            pool.memset(idx[:, :], 0).then_inc(s_id, 1)
            pool.iota(bigv[:, 0:N].bitcast(I32), pattern=[[1, N]], base=0, channel_multiplier=0).then_inc(s_id, 1)
            pool.wait_ge(s_id, 4)
            pool.affine_select(out=ident[:, :], in_=ident[:, :], compare_op=ALU.is_equal, fill=0.0,
                               base=0, pattern=[[-1, 128]], channel_multiplier=1).then_inc(s_id, 1)
            pool.memset(ones[:, :], 1.0).then_inc(s_id, 1)
            pool.memset(eps[:, :], EPS).then_inc(s_id, 1)
            pool.memset(zrow[:, :], 0.0).then_inc(s_id, 1)
            pool.memset(ones128[:, :], 1.0).then_inc(s_id, 1)
            pool.memset(bdm[:, :], 0.0).then_inc(s_id, 1)
            pool.wait_ge(s_id, 10)
            for q in range(4):
                pool.memset(bdm[32 * q:32 * q + 32, 32 * q:32 * q + 32], 1.0).then_inc(s_id, 1)
            pool.wait_ge(s_id, 14)
            pool.memset(tril[:, :], 1.0).then_inc(s_id, 1)
            pool.memset(triu[:, :], 1.0).then_inc(s_id, 1)
            pool.wait_ge(s_id, 16)
            pool.affine_select(out=tril[:, :], in_=tril[:, :], compare_op=ALU.is_gt, fill=0.0,
                               base=0, pattern=[[-1, P]], channel_multiplier=1).then_inc(s_id, 1)
            pool.affine_select(out=triu[:, :], in_=triu[:, :], compare_op=ALU.is_gt, fill=0.0,
                               base=0, pattern=[[1, P]], channel_multiplier=-1).then_inc(s_id, 1)
            pool.wait_ge(s_qe, 2)
            for L in range(4):
                if L == 3:
                    pool.wait_ge(s_w5, 12 * 16)
                    with pool.Fori(0, NB) as b:
                        pool.wait_ge(s_kvn, b * 3 + 7)
                        pool.tensor_tensor(kvn, kvn, gbk[:, 0, :], ALU.mult).then_inc(s_kvg, 1)
                        pool.wait_ge(s_kvg, b * 2 + 1)
                        pool.tensor_tensor(kvn, kvn, gbk[:, 1, :], ALU.add).then_inc(s_kvg, 1)
                if L == 0:
                    pool.wait_ge(s_tab0, 5 * 16)
                elif L == 3:
                    pool.wait_ge(s_gst, NB * 16)
                else:
                    pool.wait_ge(s_sto, L * NB * 16)
                groups = pool.value_load(qrun[0:1, 1, NB - 1:NB], min_val=1, max_val=NB * NG)

                def gathers(q, slot):
                    pool.tensor_copy(idxc[:, slot:slot + U], idx[:, ds(q % NG * U, U)]).then_inc(s_ic[L], 1)
                    pool.wait_ge(s_ic[L], q + 1)
                    pool.wait_ge(s_free[L], q + 1)
                    for u in range(U):
                        if not isinstance(q, int):
                            pool.wait_ge(s_gath[L][u], q * 16)
                            pool.sem_inc(s_landed[L], 1)
                        pool.indirect_dma_start(out=G[:, slot + u, 0:D if L < 3 else GW], out_offset=None, in_=tab[L][:, :] if L < 3 else gtab[:, :],
                                                in_offset=bass.IndirectOffsetOnAxis(ap=idxc[:, slot + u:slot + u + 1], axis=0)).then_inc(s_gath[L][u], 16)

                gathers(0, 0)
                with pool.Fori(1, groups, RG) as q:
                    for k in range(RG):
                        gathers(q + k, (k + 1) % RG * U)
                for u in range(LAG):
                    pool.wait_ge(s_gath[L][u], ((groups + (RG - 2)) // RG * RG + 1) * 16)
                    pool.sem_inc(s_landed[L], 1)
                pool.sem_inc(s_gdone, 1)

        @block.vector
        def _(dve):
            dve.memset(rowsi[:, 0, :, :], 0).then_inc(s_pad, 1)
            dve.memset(rowsi[:, 1, :, :], N).then_inc(s_pad, 1)
            dve.wait_ge(s_id, 4)
            dve.tensor_copy(iota[:, :], bigv[:, 0:N].bitcast(I32)).then_inc(s_cnt, 1)
            dve.memset(dstf[:, :], float(N)).then_inc(s_cnt, 1)
            dve.wait_ge(s_edges, 96)
            dve.tensor_copy(rows[:, :, :, :], rowsi[:, :, :, :]).then_inc(s_row, 1)
            dve.wait_ge(s_row, 1)
            c1 = red[:, 0:4]
            c2 = red[:, 4:8]
            dve.tensor_reduce(c1, rows[:, 1, :, :], AX.X, ALU.min).then_inc(s_red, 1)
            dve.tensor_scalar(bigk[:, 4096:4096 + 512].rearrange("p (c e) -> p c e", c=4), rows[:, 1, :, :], float(N - 1), None, ALU.min).then_inc(s_red, 1)
            dve.wait_ge(s_red, 2)
            dve.tensor_reduce(c2, bigk[:, 4096:4096 + 512].rearrange("p (c e) -> p c e", c=4), AX.X, ALU.max).then_inc(s_red, 1)
            dve.wait_ge(s_red, 3)
            dve.tensor_scalar(red[:, 16:24], red[:, 0:8], 0.5, 1.0 / P, ALU.add, ALU.mult).then_inc(s_red, 1)
            dve.wait_ge(s_red, 4)
            dve.tensor_copy(redi, red[:, 16:24]).then_inc(s_red, 1)
            dve.wait_ge(s_red, 5)
            dve.tensor_copy(red[:, 24:32], redi).then_inc(s_red, 1)
            dve.wait_ge(s_red, 6)
            dve.tensor_tensor(red[:, 32:40], red[:, 24:32], red[:, 16:24], ALU.is_gt).then_inc(s_red, 1)
            dve.wait_ge(s_red, 7)
            dve.tensor_tensor(red[:, 8:16], red[:, 24:32], red[:, 32:40], ALU.subtract).then_inc(s_red, 1)
            for c in range(4):
                for a in range(2):
                    k = 2 * c + a
                    dve.wait_ge(s_et, k + 1)
                    src_ps = B[k % 4][:, 0:chunk_rows[c]]
                    dst_sb = (idx if a == 0 else dstf)[:, 128 * c:128 * c + chunk_rows[c]]
                    dve.tensor_copy(dst_sb, src_ps).then_inc(s_ev, 1)
            gr = bigk[0:1, 3000:3000 + 4 * NG]
            gmin, gmax, gt = gr[:, 0:NG], gr[:, NG:2 * NG], gr[:, 2 * NG:3 * NG]
            fl = bigk[0:1, 3400:3404]
            qs, qg = bigk[0:1, 3410:3410 + NB], bigk[0:1, 3440:3440 + NB]
            le = bigk[0:1, 3470:3470 + NB * NG].rearrange("p (b g) -> p b g", b=NB)
            dve.wait_ge(s_rt, 8)
            dve.tensor_reduce(gmin, B[4][0:1, 0:NG * U].rearrange("p (g u) -> p g u", u=U), AX.X, ALU.min).then_inc(s_tb, 1)
            dve.tensor_reduce(gmax, B[5][0:1, 0:NG * U].rearrange("p (g u) -> p g u", u=U), AX.X, ALU.max).then_inc(s_tb, 1)
            dve.wait_ge(s_tb, 2)
            dve.tensor_tensor(gt[:, 0:NG - 1], gmin[:, 1:NG], gmax[:, 0:NG - 1], ALU.is_lt).then_inc(s_tb, 1)
            dve.wait_ge(s_tb, 3)
            dve.tensor_reduce(fl[:, 0:1], gt[:, 0:NG - 1], AX.X, ALU.max).then_inc(s_tb, 1)
            dve.tensor_tensor(le, gmin.rearrange("p (b g) -> p b g", b=1).broadcast_to((1, NB, NG)), iota[0:1, 0:NB].rearrange("p (b g) -> p b g", g=1).broadcast_to((1, NB, NG)), ALU.is_le).then_inc(s_tb, 1)
            dve.wait_ge(s_tb, 5)
            dve.tensor_reduce(qs, le, AX.X, ALU.add).then_inc(s_tb, 1)
            dve.tensor_scalar(qg, iota[0:1, 0:NB], float(NG - 1), float(NG), ALU.mult, ALU.add).then_inc(s_tb, 1)
            dve.wait_ge(s_tb, 7)
            dve.tensor_scalar(qs, qs, 1.0, None, ALU.max).then_inc(s_tb, 1)
            dve.wait_ge(s_tb, 8)
            dve.tensor_tensor(qg, qg, qs, ALU.subtract).then_inc(s_tb, 1)
            dve.wait_ge(s_tb, 9)
            dve.scalar_tensor_tensor(out=qs, in0=qg, scalar=fl[:, 0:1], in1=qs, op0=ALU.mult, op1=ALU.add).then_inc(s_tb, 1)
            dve.memset(qrun[:, 0, 0:1], 0).then_inc(s_tb, 1)
            dve.wait_ge(s_tb, 11)
            dve.tensor_copy(qrun[:, 1, 0:NB], qs).then_inc(s_qe, 1)
            dve.tensor_scalar(qg, qs, -1.0, None, ALU.add).then_inc(s_tb, 1)
            dve.wait_ge(s_tb, 12)
            dve.tensor_copy(qrun[:, 0, 1:NB + 1], qg).then_inc(s_qe, 1)

            for g in range(5):
                dve.wait_ge(s_x[g], 16)
                for b in range(5 * g, 5 * g + 5):
                    dve.bn_stats(st6[0:P, b, :], xin[0:P, b, :]).then_inc(s_st, 1)
                for b in range(5 * g, 5 * g + 5):
                    dve.wait_ge(s_st, b + 1)
                    dve.bn_aggr(mv[0:P, b, 0:2], st6[0:P, b, :]).then_inc(s_mv, 1)
            for g in range(5):
                dve.wait_ge(s_sd, g + 1)
                dve.reciprocal(mv[0:P, 5 * g:5 * g + 5, 2], mv[0:P, 5 * g:5 * g + 5, 2]).then_inc(s_rs, 1)
                dve.wait_ge(s_rs, g + 1)
                for b in range(5 * g, 5 * g + 5):
                    dve.tensor_scalar(h[0:P, b, :], xin[0:P, b, :], mv[0:P, b, 0:1], mv[0:P, b, 2:3], ALU.subtract, ALU.mult).then_inc(s_lnd, 1)
            for k in range(6):
                dve.wait_ge(s_wt, k + 1)
                W = (WlT if k < 3 else WrT)[:, k % 3, :, :]
                dve.tensor_copy(W, B[6 + k % 2][:, :].rearrange("p (c o) -> p c o", c=KC)).then_inc(s_wv, 1)

            dve.memset(rm[:, :], -3.0e38).then_inc(s_mix0, 1)
            dve.sem_inc(s_ln, 1)
            dve.wait_ge(s_mixw, 5 * 16)
            for c in range(KC):
                dve.tensor_copy(wrr[:, c, :], wr[:, c:c + 1].broadcast_to((128, P))).then_inc(s_wrr, 1)

            def ln_stats(src, k, n):
                dve.bn_stats(lst[:, k, 0:6], src).then_inc(s_ln, 1)
                dve.wait_ge(s_ln, n + 1)
                dve.nop(nofuse=True)
                dve.bn_aggr(lst[:, k, 6:8], lst[:, k, 0:6]).then_inc(s_ln, 1)
                return n + 2

            for L in L4:
                if L == 1:
                    dve.wait_ge(s_kmT, 1)
                    dve.tensor_reduce(kmx[:, :], psA[:, 0:KC * P].rearrange("p (c n) -> p c n", c=KC), AX.X, ALU.max).then_inc(s_km, 1)
                    dve.wait_ge(s_km, 1)
                    for c in range(KC):
                        dve.tensor_scalar(dg[:, c, :], ident[:, :], kmx[:, c:c + 1], None, ALU.mult).then_inc(s_km, 1)
                    dve.wait_ge(s_kmB, 1)
                    dve.tensor_copy(kmb[:, :], psA[0:P, 0:D]).then_inc(s_km, 1)
                    dve.wait_ge(s_km, 4)
                if L == 2:
                    dve.wait_ge(s_ctx, NB + 2)
                    dve.reciprocal(dn[:, :], psC[:, D:D + KC]).then_inc(s_bd, 1)
                    dve.wait_ge(s_bd, 1)
                    dve.tensor_scalar(dn[:, :], dn[:, :], 32.0 ** -0.5, None, ALU.mult).then_inc(s_bd, 1)
                    dve.wait_ge(s_bd, 2)
                    for c in range(KC):
                        dve.scalar_tensor_tensor(out=bd[:, c, :], in0=psC[:, c * 128:c * 128 + 128], scalar=dn[:, c:c + 1], in1=bdm[:, :], op0=ALU.mult, op1=ALU.mult).then_inc(s_bd, 1)
                    dve.wait_ge(s_bdp, 1)
                    dve.tensor_copy(bdT[:, :, :], psA[:, 0:256].rearrange("p (c n) -> p c n", c=KC)).then_inc(s_bd, 1)
                    dve.wait_ge(s_bdp, 2)
                    for c in range(KC):
                        dve.tensor_copy(Mx[:, c, :], B[4 + c][:, 0:D]).then_inc(s_bd, 1)

                def one_hots(b, q):
                    for u in range(U):
                        dve.wait_ge(s_mm[L], (q + b) * (U - 1) + max(u, 1))
                        dve.tensor_scalar(oh[:, u, :], iota[:, ds(b * P, P)], dstf[:, ds(q % NG * U + u, 1)], None, ALU.is_equal).then_inc(s_oh[L], 1)

                def mean(b):
                    g = L * NB + b
                    S = sums_of(L, b)
                    dve.wait_ge(s_sum, g + 1)
                    dve.tensor_scalar(rdeg[0:P, 0:1], S[:, D:D + 1], 1.0, None, ALU.max).then_inc(s_mean, 1)
                    dve.wait_ge(s_mean, g * 3 + 5)
                    dve.reciprocal(rdeg[0:P, 1:2], rdeg[0:P, 0:1]).then_inc(s_mean, 1)
                    dve.wait_ge(s_mean, g * 3 + 6)
                    dve.tensor_scalar(st[0:P, 1, :], S[:, 0:D], rdeg[0:P, 1:2], None, ALU.mult).then_inc(s_mean, 1)

                def follow(b):
                    if L == 0:
                        n = b * 6 + 1
                        heads = lambda t: t.rearrange("p (h e) -> p h e", h=8)
                        dve.wait_ge(s_qkv, b + 1)
                        dve.tensor_reduce(qst[:, 0, :], heads(psQK[0:P, 0:D]), AX.X, ALU.max).then_inc(s_mix0, 1)
                        dve.wait_ge(s_mix0, n + 1)
                        dve.tensor_tensor(heads(qsm[:, :]), heads(psQK[0:P, 0:D]), qst[:, 0, :].rearrange("p (h e) -> p h e", e=1).broadcast_to((P, 8, 32)), ALU.subtract).then_inc(s_mix0, 1)
                        dve.wait_ge(s_kvc, b * 2 + 3)
                        dve.tensor_tensor(rm[:, :], rm[:, :], blk(k_all, b), ALU.max).then_inc(s_mix0, 1)

                    if L == 2:
                        n = b * 12 + 1
                        dve.wait_ge(s_omx, b + 1)
                        n = ln_stats(rows_of(b)[:, D:2 * D], 0, n)
                        dve.wait_ge(s_lna, b * 2 + 1)
                        dve.reciprocal(lst[:, 0, 9:10], lst[:, 0, 8:9]).then_inc(s_ln, 1)
                        dve.wait_ge(s_ln, n + 1)
                        dve.tensor_scalar(ty[:, :], rows_of(b)[:, D:2 * D], lst[:, 0, 6:7], lst[:, 0, 9:10], ALU.subtract, ALU.mult).then_inc(s_ln, 1)
                        dve.wait_ge(s_ln, n + 2)
                        dve.tensor_tensor(ty[:, :], ty[:, :], gamma[:, :], ALU.mult).then_inc(s_ln, 1)
                        dve.wait_ge(s_ln, n + 3)
                        dve.wait_ge(s_xs, (b + 1) * 16)
                        dve.tensor_tensor(ty[:, :], ty[:, :], xs[:, :], ALU.add).then_inc(s_ln, 1)
                        dve.wait_ge(s_ln, n + 4)
                        dve.wait_ge(s_omm, L * NB + b + 1)
                        dve.tensor_tensor(x1s[:, :], ty[:, :], rows_of(b)[:, 0:D], ALU.add).then_inc(s_ln, 1)
                        dve.wait_ge(s_ln, n + 5)
                        n = ln_stats(x1s[:, :], 1, n + 5)
                        dve.wait_ge(s_lna, b * 2 + 2)
                        dve.reciprocal(lst[:, 1, 9:10], lst[:, 1, 8:9]).then_inc(s_ln, 1)
                        dve.wait_ge(s_ln, n + 1)
                        dve.wait_ge(s_xlT, b + 1)
                        dve.tensor_scalar(xls[:, :], x1s[:, :], lst[:, 1, 6:7], lst[:, 1, 9:10], ALU.subtract, ALU.mult).then_inc(s_ln, 1)
                        dve.wait_ge(s_ln, n + 2)
                        dve.tensor_tensor(blk(x1_all, b), x1s[:, :], xls[:, :], ALU.add).then_inc(s_ln, 1)

                heads = lambda t: t.rearrange("p (h e) -> p h e", h=8)

                def follow_q(b):
                    n = b * 6 + 1
                    dve.wait_ge(s_qx, b + 1)
                    dve.tensor_reduce(qst[:, 1, :], heads(qsm[:, :]), AX.X, ALU.add).then_inc(s_mix0, 1)
                    dve.wait_ge(s_mix0, n + 4)
                    dve.reciprocal(qst[:, 2, :], qst[:, 1, :]).then_inc(s_mix0, 1)
                    dve.wait_ge(s_mix0, n + 5)
                    dve.tensor_tensor(heads(blk(q_all, b)), heads(qsm[:, :]), qst[:, 2, :].rearrange("p (h e) -> p h e", e=1).broadcast_to((P, 8, 32)), ALU.mult).then_inc(s_mix0, 1)

                def body(b, sums, rows_, after, later):
                    if sums:
                        q0, q1 = group_range(dve, b)
                        one_hots(b, q0)
                    if rows_:
                        mean(b - 1)
                        if L == 1:
                            dve.wait_ge(s_ctx, b)
                            dve.tensor_tensor(ek[:, :], blk(k_all, b - 1), kmb[:, :], ALU.subtract).then_inc(s_ek, 1)
                    if after and L < 2:
                        follow(b - 2)
                    if sums:
                        with dve.If(q1 > q0 + 1):
                            with dve.Fori(q0 + 1, q1) as q:
                                one_hots(b, q)
                    if after and L == 0:
                        follow_q(b - 2)
                    if after and L == 2:
                        follow(b - 2)
                layer(dve, body)

            dve.wait_ge(s_wrow, NB)
            dve.wait_ge(s_id, 18)
            dve.memset(A8, 0.0).then_inc(s_a8, 1)
            dve.memset(cnt[:, :, :], 0.0).then_inc(s_wc, 1)
            for i in range(NB):
                dve.tensor_tensor_reduce(junk[:, P * i:P * i + P], wrow[:, P * i:P * i + P], ident[0:P, 0:P], 1.0, 0.0, ALU.mult, ALU.add, wcol[:, i:i + 1]).then_inc(s_wc, 1)
            dve.wait_ge(s_wc, NB + 1)
            for i in range(NB):
                lo, hi = P * i, P * i + P
                if i:
                    dve.wait_ge(s_rank, 4 * i - 1)
                    dve.tensor_scalar(junk[:, 0:lo], wrow[:, 0:lo], wcol[:, i:i + 1], 0.0, ALU.is_ge, ALU.add, accum_out=cnt[:, i, 0:1]).then_inc(s_rank, 1)
                if i < NB - 1:
                    dve.tensor_scalar(junk[:, hi:N], wrow[:, hi:N], wcol[:, i:i + 1], 0.0, ALU.is_gt, ALU.add, accum_out=cnt[:, i, 1:2]).then_inc(s_rank, 1)
                dve.scalar_tensor_tensor(out=junk[:, lo:hi], in0=wrow[:, lo:hi], scalar=wcol[:, i:i + 1], in1=tril[:, :], op0=ALU.is_ge, op1=ALU.mult, accum_out=cnt[:, i, 2:3]).then_inc(s_rank, 1)
                dve.scalar_tensor_tensor(out=junk2, in0=wrow[:, lo:hi], scalar=wcol[:, i:i + 1], in1=triu[:, :], op0=ALU.is_gt, op1=ALU.mult, accum_out=cnt[:, i, 3:4]).then_inc(s_rank, 1)
            nr = 4 * NB - 2
            dve.wait_ge(s_rank, nr)
            dve.tensor_reduce(sel[:, :], cnt[:, :, :], AX.X, ALU.add).then_inc(s_rank, 1)
            dve.wait_ge(s_rank, nr + 1)
            dve.tensor_scalar(sel[:, :], sel[:, :], float(CHOSEN), None, ALU.is_lt).then_inc(s_rank, 1)

            dve.wait_ge(s_pt, 2)
            for k, (to, bank) in enumerate(((WgT, 0), (WqT, 2))):
                dve.tensor_copy(to, B[bank][:, :].rearrange("p (c o) -> p c o", c=KC)).then_inc(s_pv, 1)
            groups = lambda t, n: t.rearrange("p (g e) -> p g e", g=n)
            dve.wait_ge(s_w5, 12 * 16)
            for k, (t, mean, n) in enumerate(((Wkv.rearrange("p c d -> p (c d)"), cmean, 32), (bkv, bmean, 16))):
                dve.tensor_reduce(mean, groups(t, n), AX.X, ALU.add).then_inc(s_pv, 1)
                dve.wait_ge(s_pv, 3 + 3 * k)
                dve.tensor_scalar(mean, mean, 1.0 / 32, None, ALU.mult).then_inc(s_pv, 1)
                dve.wait_ge(s_pv, 4 + 3 * k)
                dve.tensor_tensor(groups(t, n), groups(t, n), mean.rearrange("p (g e) -> p g e", e=1).broadcast_to((t.shape[0], n, 32)), ALU.subtract).then_inc(s_pv, 1)
            dve.wait_ge(s_pt, 3)
            dve.tensor_copy(Wg[:, :, D:D + 8], B[4][:, 0:16].rearrange("p (c h) -> p c h", c=KC)).then_inc(s_pv, 1)
            dve.tensor_copy(bqc, B[5][:, 0:KC]).then_inc(s_pv, 1)
            dve.wait_ge(s_yw, NB + TB)
            dve.wait_ge(s_rank, 4 * NB)
            def rows_in(b):
                n = b * 6
                if not isinstance(b, int):
                    dve.wait_ge(s_x2, n)
                dve.scalar_tensor_tensor(out=x1s[:, :], in0=blk(yw, b), scalar=sel[:, ds(b, 1)], in1=blk(x1_all, b), op0=ALU.mult, op1=ALU.add).then_inc(s_x2, 1)
                dve.wait_ge(s_x2, n + 1)
                dve.bn_stats(lst[:, 0, 0:6], x1s[:, :]).then_inc(s_x2, 1)
                dve.wait_ge(s_x2, n + 2)
                dve.nop(nofuse=True)
                dve.bn_aggr(lst[:, 0, 6:8], lst[:, 0, 0:6]).then_inc(s_x2, 1)
                dve.wait_ge(s_x2sd, b + 1)
                dve.reciprocal(lst[:, 0, 9:10], lst[:, 0, 8:9]).then_inc(s_x2, 1)
                dve.wait_ge(s_x2, n + 4)
                dve.wait_ge(s_x2T, b + 1)
                dve.tensor_scalar(xls[:, :], x1s[:, :], lst[:, 0, 6:7], lst[:, 0, 9:10], ALU.subtract, ALU.mult).then_inc(s_x2, 1)
                dve.wait_ge(s_x2, n + 5)
                dve.tensor_tensor(blk(x1_all, b), x1s[:, :], xls[:, :], ALU.add).then_inc(s_x2, 1)

            def normed(b):
                dve.wait_ge(s_kvsd, b * 2 + 1)
                dve.tensor_reduce(ss[:, 0:16], groups(sq, 16), AX.X, ALU.add).then_inc(s_kvn, 1)
                dve.wait_ge(s_kvsd, b * 2 + 2)
                dve.reciprocal(ss[:, 16:32], ss[:, 16:32]).then_inc(s_kvn, 1)
                dve.wait_ge(s_kvn, b * 3 + 6)
                dve.wait_ge(s_kva, b + 1)
                dve.tensor_tensor(groups(kvn, 16), groups(kv_of(b), 16), ss[:, 16:32].rearrange("p (g e) -> p g e", e=1).broadcast_to((P, 16, 32)), ALU.mult).then_inc(s_kvn, 1)
            rows_in(0)
            with dve.Fori(1, NB) as b:
                rows_in(b)
                normed(b - 1)
            normed(NB - 1)
            dve.wait_ge(s_kvd, 1)
            for c in range(KC):
                dve.scalar_tensor_tensor(out=bd[:, c, :], in0=psC[:, c * 128:c * 128 + 128], scalar=1.0 / N, in1=bdm[:, :], op0=ALU.mult, op1=ALU.mult).then_inc(s_k4, 1)
            dve.tensor_reduce(mx4, asd[:, :, 0:4].rearrange("p b h -> p h b"), AX.X, ALU.max).then_inc(s_k4, 1)
            dve.wait_ge(s_k4p, 1)
            dve.tensor_copy(WqpT, B[0][:, :].rearrange("p (c o) -> p c o", c=KC)).then_inc(s_k4, 1)
            dve.tensor_copy(bqp, B[5][:, 0:KC]).then_inc(s_k4, 1)
            dve.wait_ge(s_k4, 4)
            for c in range(KC):
                dve.tensor_tensor(WqpT[:, c, c * 128:c * 128 + 128], WqpT[:, c, c * 128:c * 128 + 128], ident[:, :], ALU.add).then_inc(s_k4, 1)
            dve.wait_ge(s_k4p, 2)
            dve.tensor_reduce(kx, B[7][0:4, 0:P], AX.X, ALU.max).then_inc(s_k4, 1)
            dve.wait_ge(s_k4, 8)
            dve.tensor_scalar(dg4, ident[0:4, 0:4], kx, None, ALU.mult).then_inc(s_k4, 1)
            dve.wait_ge(s_k4p, 3)
            dve.tensor_copy(Wpp, B[2][:, :].rearrange("p (c o) -> p c o", c=KC)).then_inc(s_k4, 1)
            dve.tensor_tensor(bpp, B[5][:, 4:4 + KC], b1m, ALU.add).then_inc(s_k4, 1)
            dve.wait_ge(s_k4p, 4)
            dve.tensor_copy(mx4, B[7][0:P, 128:132]).then_inc(s_k4, 1)
            dve.wait_ge(s_k4, 12)
            top = tab8[:, :, 4:8]
            dve.tensor_tensor(top, asd[:, :, 4:8], mx4.rearrange("p (b h) -> p b h", b=1).broadcast_to((P, NB, 4)), ALU.add).then_inc(s_k4, 1)
            dve.tensor_copy(tab8[:, :, 0:4], asd[:, :, 4:8]).then_inc(s_k4, 1)
            dve.tensor_tensor(wself, asd[:, :, 0:4], asd[:, :, 4:8], ALU.add).then_inc(s_k4, 1)
            dve.wait_ge(s_k4, 13)
            dve.scalar_tensor_tensor(out=top, in0=top, scalar=0.2, in1=top, op0=ALU.mult, op1=ALU.max).then_inc(s_k4, 1)
            dve.wait_ge(s_k4, 15)
            dve.scalar_tensor_tensor(out=wself, in0=wself, scalar=0.2, in1=wself, op0=ALU.mult, op1=ALU.max).then_inc(s_k4, 1)
            dve.wait_ge(s_k4, 17)
            dve.tensor_tensor(wself, wself, top, ALU.subtract).then_inc(s_k4, 1)
            dve.tensor_copy(identh[:, :], ident[:, :]).then_inc(s_k4, 1)
            for k in range(3):
                dve.tensor_copy(tabh[:, k, :, :], tab8 if k == 0 else tabr).then_inc(s_k4, 1)
                if k < 2:
                    dve.wait_ge(s_k4, 20 + 2 * k)
                    dve.tensor_tensor(tabr, tab8 if k == 0 else tabr, tabh[:, k, :, :], ALU.subtract).then_inc(s_k4, 1)
                    dve.wait_ge(s_k4, 21 + 2 * k)

            def mix(g, blocks):
                for k in range(blocks):
                    if k == 0:
                        dve.wait_ge(s_p2, g + 1)
                    dve.tensor_tensor(blk(x1_all, g * TB + k), blk(x1_all, g * TB + k), B[4 + k][0:P, 0:D], ALU.add).then_inc(s_p2x, 1)
            with dve.Fori(0, NB // TB) as g:
                mix(g, TB)
            mix(NB // TB, NB % TB)

            dve.sem_inc(s_gat, 11)
            dve.wait_ge(s_k4x, 1)
            dve.wait_ge(s_p2, NB // TB + 1)

            def one_hot(to, b, q):
                return dve.tensor_tensor(to[:, :, :], iota[:, ds(b * P, P)].rearrange("p (u n) -> p u n", u=1).broadcast_to((128, U, P)),
                                         dstf[:, ds(q % NG * U, U)].rearrange("p (u n) -> p u n", n=1).broadcast_to((128, U, P)), ALU.is_equal)

            def one_hots_to_sum(b, q, lo, hi):
                for u in range(lo, hi):
                    dve.wait_ge(s_mm[3], (q + b) * U + u + 1)
                    dve.tensor_scalar(oh[:, u, :], iota[:, ds(b * P, P)], dstf[:, ds(q % NG * U + u, 1)], None, ALU.is_equal).then_inc(s_oh[3], 1)

            def prepare(b, q):
                n = q + b
                if not (isinstance(n, int) and n == 0):
                    dve.wait_ge(s_ohT, n)
                one_hot(ohA, b, q).then_inc(s_ohA, 1)

            def weights(b, q, nb, nq):
                n = q + b
                if nb is not None:
                    prepare(nb, nq)
                rows4 = ds(q % RG * U, U)
                w = wh[:, ds(n % 2 * U, U), :]
                X = PS[:, ds(4 + n % 2, 1), 0:8 * U].rearrange("p a (u h) -> p (a u) h", u=U)
                dve.wait_ge(s_landed[3], q * U + U)
                dve.wait_ge(s_psx, n + 1)
                dve.tensor_tensor(ez[:, :, :], X[:, :, 0:4], G[:, rows4, D:GW], ALU.add).then_inc(s_z, 1)
                dve.wait_ge(s_z, n * 5 + 1)
                dve.scalar_tensor_tensor(out=ez[:, :, :], in0=ez[:, :, :], scalar=0.2, in1=ez[:, :, :], op0=ALU.mult, op1=ALU.max).then_inc(s_z, 1)
                dve.wait_ge(s_z, n * 5 + 2)
                dve.tensor_tensor(ez[:, :, :], ez[:, :, :], X[:, :, 4:8], ALU.subtract).then_inc(s_z, 1)
                dve.wait_ge(s_z, n * 5 + 3)
                dve.tensor_scalar(ez[:, :, :], ez[:, :, :], 0.0, None, ALU.min).then_inc(s_z, 1)
                one_hots_to_sum(b, q, 0, 2)
                dve.wait_ge(s_ew, n + 2)
                dve.tensor_tensor(w[:, :, 0:D].rearrange("p u (h f) -> p u h f", h=4), G[:, rows4, 0:D].rearrange("p u (h f) -> p u h f", h=4),
                                  w[:, :, D:GW].rearrange("p u (h f) -> p u h f", f=1).broadcast_to((128, U, 4, 64)), ALU.mult).then_inc(s_z, 1)
                one_hots_to_sum(b, q, 2, U)

            heads4 = lambda t: t.rearrange("p (h f) -> p h f", h=4)
            wide4 = lambda t: t.rearrange("p (h f) -> p h f", f=1).broadcast_to((P, 4, 64))

            def finish(b):
                n = b * 7 + 11
                dve.wait_ge(s_gat, n)
                ws = blk(wself, b)
                S = PS[0:P, ds(b % 2, 1), :].rearrange("p a n -> p (a n)")
                dve.wait_ge(s_hin, (3 * NB + b + 1) * 16)
                dve.tensor_tensor(heads4(ty[:, :]), heads4(st[0:P, 0, :]), wide4(ws), ALU.mult).then_inc(s_gat, 1)
                dve.wait_ge(s_sum, 3 * NB + b + 1)
                dve.tensor_tensor(rs8[:, 0:4], S[:, D:GW], ws, ALU.add).then_inc(s_gat, 1)
                dve.wait_ge(s_gat, n + 2)
                dve.reciprocal(rs8[:, 4:8], rs8[:, 0:4]).then_inc(s_gat, 1)
                dve.tensor_tensor(ty[:, :], ty[:, :], S[:, 0:D], ALU.add).then_inc(s_gat, 1)
                dve.wait_ge(s_gat, n + 4)
                dve.tensor_tensor(heads4(ty[:, :]), heads4(ty[:, :]), wide4(rs8[:, 4:8]), ALU.mult).then_inc(s_gat, 1)
                dve.wait_ge(s_gat, n + 5)
                dve.tensor_tensor(ty[:, :], ty[:, :], gbias, ALU.add).then_inc(s_gat, 1)
                dve.wait_ge(s_gat, n + 6)
                dve.scalar_tensor_tensor(out=blk(x1_all, b), in0=ty[:, :], scalar=0.0, in1=blk(x1_all, b), op0=ALU.max, op1=ALU.add).then_inc(s_gat, 1)
                dve.wait_ge(s_gat, n + 7)
                dve.bn_stats(st6[0:P, ds(b, 1), :].rearrange("p a k -> p (a k)"), blk(x1_all, b)).then_inc(s_m, 1)

            prepare(0, 0)
            stream(dve, lambda b: None, weights, lambda b: None, finish)

            dve.wait_ge(s_m, NB)
            for b in range(NB):
                dve.bn_aggr(mv[0:P, b, 0:2], st6[0:P, b, :]).then_inc(s_m, 1)
            dve.wait_ge(s_msd, 1)
            dve.reciprocal(mv[0:P, :, 2], mv[0:P, :, 2]).then_inc(s_m, 1)
            dve.wait_ge(s_m, 2 * NB + 1)
            with dve.Fori(0, NB) as b:
                dve.wait_ge(s_mxT, b + 1)
                dve.tensor_scalar(xls[:, :], blk(x1_all, b), mv[0:P, ds(b, 1), 0:1].rearrange("p a k -> p (a k)"), mv[0:P, ds(b, 1), 2:3].rearrange("p a k -> p (a k)"), ALU.subtract, ALU.mult).then_inc(s_m, 1)
            wide = lambda t: t.broadcast_to((P, NB, 4))
            dve.wait_ge(s_mge, NB + 1)
            dve.tensor_reduce(g1, gl, AX.X, ALU.max).then_inc(s_gx, 1)
            dve.wait_ge(s_gx, 1)
            dve.tensor_tensor(gx, gl, wide(g1), ALU.subtract).then_inc(s_gx, 1)
            dve.wait_ge(s_gxe, 1)
            dve.tensor_reduce(g1, gx, AX.X, ALU.add).then_inc(s_gx, 1)
            dve.wait_ge(s_gx, 3)
            dve.reciprocal(g1, g1).then_inc(s_gx, 1)
            dve.wait_ge(s_gx, 4)
            dve.tensor_tensor(gx, gx, wide(g1), ALU.mult).then_inc(s_gx, 1)
            dve.memset(gr2, 0.0).then_inc(s_gx, 1)
            dve.wait_ge(s_gx, 6)
            n = 6
            for i in range(4):
                for j in range(4):
                    if i != j:
                        op = ALU.is_ge if j < i else ALU.is_gt
                        dve.tensor_tensor(ga[:, :, 0:1], gx[:, :, j:j + 1], gx[:, :, i:i + 1], op).then_inc(s_gx, 1)
                        dve.wait_ge(s_gx, n + 1)
                        dve.tensor_tensor(gr2[:, :, i:i + 1], gr2[:, :, i:i + 1], ga[:, :, 0:1], ALU.add).then_inc(s_gx, 1)
                        n += 2
                        dve.wait_ge(s_gx, n)
            dve.tensor_reduce(g1, gx, AX.X, ALU.max).then_inc(s_gx, 1)
            dve.wait_ge(s_gx, n + 1)
            dve.tensor_tensor(gp, gx, wide(g1), ALU.subtract).then_inc(s_gx, 1)
            dve.wait_ge(s_gxe, 2)
            dve.scalar_tensor_tensor(out=gp, in0=gr2, scalar=2.0, in1=gp, op0=ALU.is_lt, op1=ALU.mult).then_inc(s_gx, 1)
            dve.wait_ge(s_gx, n + 3)
            dve.tensor_reduce(g1, gp, AX.X, ALU.add).then_inc(s_gx, 1)
            dve.wait_ge(s_gx, n + 4)
            dve.reciprocal(g1, g1).then_inc(s_gx, 1)
            dve.wait_ge(s_gx, n + 5)
            dve.tensor_tensor(gp, gp, wide(g1), ALU.mult).then_inc(s_gx, 1)
            dve.wait_ge(s_gx, n + 6)

            with dve.Fori(0, NB) as b:
                x = blk(x1_all, b)
                dve.tensor_tensor(x, x, b3[:, 0:D], ALU.add).then_inc(s_b3, 1)
                for k in range(4):
                    dve.wait_ge(s_b3, b * 5 + k + 1)
                    dve.scalar_tensor_tensor(out=x, in0=b3[:, (k + 1) * D:(k + 2) * D], scalar=gp[:, ds(b, 1), k:k + 1].rearrange("p a h -> p (a h)"), in1=x, op0=ALU.mult, op1=ALU.add).then_inc(s_b3, 1)
                dve.wait_ge(s_b3, b * 5 + 5)
                bank = lambda e: PS[0:P, ds(2 + b % 2 * 3 + e, 1), :].rearrange("p a n -> p (a n)")
                dve.wait_ge(s_tm, b + 1)
                dve.tensor_tensor(x, x, bank(2)[:, 0:D], ALU.add).then_inc(s_acc, 1)
                for k in range(4):
                    dve.wait_ge(s_acc, b * 5 + k + 7)
                    dve.scalar_tensor_tensor(out=x, in0=bank(k // 2)[:, k % 2 * D:k % 2 * D + D], scalar=gp[:, ds(b, 1), k:k + 1].rearrange("p a h -> p (a h)"), in1=x, op0=ALU.mult, op1=ALU.add).then_inc(s_acc, 1)

        @block.scalar
        def _(act):
            for g in range(5):
                act.wait_ge(s_mv, 5 * g + 5)
                act.wait_ge(s_id, 7)
                act.activation(mv[0:P, 5 * g:5 * g + 5, 2], mv[0:P, 5 * g:5 * g + 5, 1], ACT.Sqrt, bias=eps[0:P, :]).then_inc(s_sd, 1)
            for L in L4:
                if L == 0:
                    act.sem_inc(s_hfree, 1)
                    act.sem_inc(s_ho, 1)
                    act.sem_inc(s_kvc, 2)
                if L == 2:
                    act.sem_inc(s_qTe, 1)
                if L != 1:
                    act.activation(actw[:, :], eps[0:P, :], ACT.Exp if L == 0 else ACT.Sqrt).then_inc(s_actw, 1)
                def body(b, sums, rows_, after, later):
                    if rows_:
                        t = b - 1
                        if L == 2:
                            act.wait_ge(s_qTe, t + 1)
                            act.activation(qsm[:, :], blk(q_all, t), ACT.Copy).then_inc(s_qs, 1)
                        if L == 1:
                            act.wait_ge(s_ek, t + 1)
                            act.activation(ek[:, :], ek[:, :], ACT.Exp).then_inc(s_ekx, 1)
                        act.wait_ge(s_mT, L * NB + t + 1)
                        act.activation(rT[:, :, 0:KC * P], psHM[:, :].rearrange("p (a n) -> p a n", a=2)[:, :, 0:KC * P], ACT.Copy).then_inc(s_he, 1)
                        if L == 2:
                            act.wait_ge(s_qT, t + 1)
                            act.activation(qT[:, :], psV[:, 0:KC * P], ACT.Copy).then_inc(s_qTe, 1)
                    if later and L == 2:
                        t = b - 3
                        act.wait_ge(s_xlT, t + 2)
                        act.activation(xlT[:, :, ds(t * P, P)], psA[:, 0:KC * P].rearrange("p (c n) -> p c n", c=KC), ACT.Copy).then_inc(s_xlTe, 1)
                        act.wait_ge(s_rw, t + 1)
                        act.activation(wrow[:, ds(t * P, P)], psC[0:P, 0:P], ACT.Identity, bias=br[:, :]).then_inc(s_wrow, 1)
                    if after:
                        t = b - 2
                        if L == 0:
                            act.wait_ge(s_mix0, t * 6 + 3)
                            act.activation(qsm[:, :], qsm[:, :], ACT.Exp).then_inc(s_qx, 1)
                        if L == 2:
                            for k in range(2):
                                act.wait_ge(s_ln, t * 12 + 3 + 7 * k)
                                act.activation(lst[:, k, 8:9], lst[:, k, 7:8], ACT.Sqrt, bias=eps[0:P, :]).then_inc(s_lna, 1)
                    if rows_:
                        t = b - 1
                        if L < 2:
                            act.wait_ge(s_omm, L * NB + t + 1)
                            act.wait_ge(s_hfree, L * NB + t + 1)
                            act.activation(ho[0:P, :], psO[0:P, 0:D], ACT.Relu).then_inc(s_ho, 1)
                        if L == 0:
                            act.wait_ge(s_qkv, t + 1)
                            act.activation(blk(k_all, t), psV[0:P, 0:D], ACT.Copy).then_inc(s_kvc, 1)
                            act.activation(blk(v_all, t), psV[0:P, D:2 * D], ACT.Copy).then_inc(s_kvc, 1)
                layer(act, body)

            act.sem_inc(s_ge, 4)
            act.sem_inc(s_yw, TB)
            act.wait_ge(s_fw, 4 * 16)
            act.wait_ge(s_gdone, 3)

            def ffn(g, blocks):
                for m in range(HC):
                    act.wait_ge(s_st1, g * HC + m + 1)
                    act.activation(hT[:, m, 0:blocks * P], B[m % 4][:, 0:blocks * P], ACT.Gelu_apprx_tanh, bias=b1c[:, m:m + 1]).then_inc(s_ge, 1)
                act.wait_ge(s_wc, NB + 1)
                act.wait_ge(s_st2, g + 1)
                for k in range(blocks):
                    act.activation(blk(yw, g * TB + k), B[4 + k][0:P, 0:D], ACT.Identity, scale=wcol[:, ds(g * TB + k, 1)]).then_inc(s_yw, 1)
            with act.Fori(0, NB // TB) as g:
                ffn(g, TB)
            ffn(NB // TB, NB % TB)

            xT = lambda b: xlT[:, :, ds(b * P, P)]
            two = lambda t: t[:, 0:KC * P].rearrange("p (c n) -> p c n", c=KC)
            act.wait_ge(s_w5, 12 * 16)
            def rows_in(b):
                act.wait_ge(s_x2, b * 6 + 3)
                act.activation(lst[:, 0, 8:9], lst[:, 0, 7:8], ACT.Sqrt, bias=eps[0:P, :]).then_inc(s_x2sd, 1)
                act.wait_ge(s_x2T, b + 2)
                act.activation(rT[:, 0, 0:KC * P], psH[:, 0:KC * P], ACT.Copy).then_inc(s_x2Te, 1)
                act.activation(xT(b), two(psH), ACT.Copy).then_inc(s_x2Te, 1)

            def normed(b):
                act.wait_ge(s_hkv, b * 2 + 2)
                act.activation(sq, kv_of(b), ACT.Square).then_inc(s_kvsd, 1)
                act.wait_ge(s_kvn, b * 3 + 5)
                act.activation(ss[:, 16:32], ss[:, 0:16], ACT.Sqrt, scale=1.0 / 32, bias=eps[0:P, :]).then_inc(s_kvsd, 1)

            def table_rows(b):
                act.wait_ge(s_hkv, b * 2 + 1)
                act.wait_ge(s_hfree, 2 * NB + b + 1)
                act.activation(hs, psO[0:P, 0:D + 8], ACT.Copy).then_inc(s_hs, 1)
                act.activation(blk(asd, b), psO[0:P, D:D + 8], ACT.Copy).then_inc(s_hsa, 1)
            act.activation(actw[:, :], eps[0:P, :], ACT.Sqrt).then_inc(s_x2Te, 1)
            rows_in(0)
            table_rows(0)
            with act.Fori(1, NB) as b:
                rows_in(b)
                normed(b - 1)
                table_rows(b)
            normed(NB - 1)
            act.wait_ge(s_k4, 18)
            act.activation(wself, wself, ACT.Exp).then_inc(s_k4x, 1)

            def mix(g, blocks):
                for m in range(KC):
                    act.wait_ge(s_p1, g * KC + m + 1)
                    act.activation(gT[:, m, 0:blocks * P], B[m][:, 0:blocks * P], ACT.Gelu, bias=bpp[:, m:m + 1]).then_inc(s_p1e, 1)
            with act.Fori(0, NB // TB) as g:
                mix(g, TB)
            mix(NB // TB, NB % TB)

            def prepare(b, q):
                act.wait_ge(s_ohT, q + b + 1)
                act.activation(ohT[:, :], psT[0:P, :], ACT.Copy).then_inc(s_ohTe, 1)

            def weights(b, q, nb, nq):
                n = q + b
                act.wait_ge(s_z, n * 5 + 4)
                act.activation(wh[:, ds(n % 2 * U, U), D:GW], ez[:, :, :], ACT.Exp).then_inc(s_ew, 1)
                if nb is not None:
                    prepare(nb, nq)
                if nb is b:
                    act.wait_ge(s_z, n * 5 + 5)
                    act.sem_inc(s_free[3], 1)
            act.activation(actw[:, :], eps[0:P, :], ACT.Exp).then_inc(s_ew, 1)
            prepare(0, 0)
            stream(act, lambda b: None, weights, lambda b: None)

            act.wait_ge(s_m, 2 * NB)
            act.activation(mv[0:P, :, 2], mv[0:P, :, 1], ACT.Sqrt, bias=eps[0:P, :]).then_inc(s_msd, 1)

            def turned(b):
                act.wait_ge(s_mxT, b + 2)
                act.wait_ge(s_mg, b + 1)
                act.activation(rT[:, 0, 0:KC * P], psH[:, 0:KC * P], ACT.Copy).then_inc(s_mxTe, 1)
                act.activation(xT(b), two(psH), ACT.Copy).then_inc(s_mxTe, 1)

            def gates(b):
                act.wait_ge(s_mg, b + 2)
                act.activation(blk(gl, b), psO[0:P, 0:4], ACT.Copy).then_inc(s_mge, 1)
            turned(0)
            with act.Fori(1, NB) as b:
                gates(b - 1)
                turned(b)
            gates(NB - 1)
            for k, (t, n) in enumerate(((gx, 2), (gp, 32))):
                act.wait_ge(s_gx, n)
                act.activation(t, t, ACT.Exp).then_inc(s_gxe, 1)
            act.sem_inc(s_e2, 2)

            def experts(g, blocks):
                n = blocks * P
                bias = [sb1[:, 0:1], sb1[:, 1:2]] + [eb1[:, k:k + 1] for k in range(4)] + [sb2[:, 0:1]] + [eb2[0:64, k:k + 1] for k in range(4)]
                for k in range(11):
                    rows_ = 64 if k >= 7 else 128
                    act.wait_ge(s_e1, g * 11 + k + 1)
                    act.activation(ffh[k][0:rows_, 0:n], B[k % 2][0:rows_, 0:n], ACT.Relu, bias=bias[k]).then_inc(s_e2, 1)
            with act.Fori(0, NB // TB) as g:
                experts(g, TB)
            experts(NB // TB, NB % TB)

        @block.tensor
        def _(pe):
            pe.wait_ge(s_id, 14)
            pe.wait_ge(s_row, 1)
            for c in range(4):
                for a in range(2):
                    k = 2 * c + a
                    if k >= 4:
                        pe.wait_ge(s_ev, k - 3)
                    pe.transpose(B[k % 4][:, 0:chunk_rows[c]], rows[0:chunk_rows[c], a, c, :], ident[0:chunk_rows[c], 0:chunk_rows[c]]).then_inc(s_et, 1)
            pe.wait_ge(s_red, 8)
            for q in range(2):
                for c in range(4):
                    pe.transpose(B[4 + q][0:1, 128 * c:128 * c + 128], red[:, 8 + 4 * q + c:9 + 4 * q + c], ident[:, :]).then_inc(s_rt, 1)
            pe.wait_ge(s_w, 9 * 16)
            for k in range(6):
                if k >= 2:
                    pe.wait_ge(s_wv, k - 1)
                for cd in range(KC):
                    for co in range(KC):
                        last = pe.transpose(B[6 + k % 2][:, cd * D + co * 128:cd * D + co * 128 + 128], wst[:, k, co, cd * 128:cd * 128 + 128], ident[:, :])
                last.then_inc(s_wt, 1)
            pe.wait_ge(s_wv, 6)
            pe.wait_ge(s_qe, 2)
            for L in L4:
                pe.sem_inc(s_mm[L], U - 1)
                pe.sem_inc(s_free[L], RG)
                if L == 0:
                    pe.sem_inc(s_hT, 1)
                    pe.sem_inc(s_mean, 4)
                    pe.wait_ge(s_mixw, 5 * 16)
                if L == 1:
                    pe.wait_ge(s_mix0, 6 * NB + 1)
                    for c in range(KC):
                        m = pe.transpose(psA[:, c * P:c * P + P], rm[:, c * 128:c * 128 + 128], ident[0:P, 0:P])
                    m.then_inc(s_kmT, 1)
                    pe.wait_ge(s_km, 3)
                    pe.matmul(psA[0:P, 0:D], ones128[:, :], dg[:, :, :].rearrange("p c n -> p (c n)"), start=True, stop=True).then_inc(s_kmB, 1)
                    pe.matmul(psC[:, 0:D + KC], zrow[:, 0:128], zrow[:, 0:D + KC], start=True, stop=False, skip_group_check=True)
                if L == 2:
                    pe.matmul(psC[:, 0:D + KC], zrow[:, 0:128], zrow[:, 0:D + KC], start=False, stop=True, skip_group_check=True).then_inc(s_ctx, 1)
                    pe.wait_ge(s_bd, 4)
                    for c in range(KC):
                        m = pe.transpose(psA[:, c * 128:c * 128 + 128], bd[:, c, :], ident[:, :])
                    m.then_inc(s_bdp, 1)
                    pe.wait_ge(s_bd, 5)
                    for c in range(KC):
                        m = pe.matmul(B[4 + c][:, 0:D], bdT[:, c, :], Wout[:, c, :], start=True, stop=True)
                    m.then_inc(s_bdp, 1)

                def add(b, q, first):
                    for u in range(U):
                        pe.wait_ge(s_landed[L], q * U + u + 1)
                        pe.wait_ge(s_oh[L], (q + b) * U + u + 1)
                        m = pe.matmul(sums_of(L, b), oh[:, u, :], G[:, ring(q, u), 0:D + 1].rearrange("p a d -> p (a d)"),
                                      start=first and u == 0, stop=False, skip_group_check=True)
                        if u:
                            m.then_inc(s_mm[L], 1)
                        elif not first:
                            m.then_inc(s_free[L], 1)

                def to_features(to, src, signal):
                    for c in range(KC):
                        m = pe.transpose(to[:, c * P:c * P + P], src[:, c * 128:c * 128 + 128], ident[0:P, 0:P])
                    m.then_inc(signal, 1)

                def body(b, sums, rows_, after, later):
                    if sums:
                        q0, q1 = group_range(pe, b)
                        pe.wait_ge(s_mean, (L * NB + b) * 3 + 1)
                        add(b, q0, True)
                    if rows_:
                        g = L * NB + b - 1
                        pe.wait_ge(s_hin, (g + 1) * 16)
                        to_features(psHM[:, 0:D], st[0:P, 0, :], s_hT)
                        pe.wait_ge(s_mean, g * 3 + 7)
                        to_features(psHM[:, D:2 * D], st[0:P, 1, :], s_mT)
                        if L == 2:
                            pe.wait_ge(s_qs, b)
                            to_features(psV, qsm, s_qT)
                    if later and L == 2:
                        pe.wait_ge(s_ln, (b - 3) * 12 + 13)
                        to_features(psA, xls, s_xlT)
                        pe.wait_ge(s_xlTe, b - 2)
                        for c in range(KC):
                            m = pe.matmul(psC[0:P, 0:P], wrr[:, c, :], xlT[:, c, ds((b - 3) * P, P)], start=(c == 0), stop=(c == KC - 1))
                        m.then_inc(s_rw, 1)
                    if sums:
                        with pe.If(q1 > q0 + 1):
                            with pe.Fori(q0 + 1, q1) as q:
                                add(b, q, False)
                        pe.matmul(sums_of(L, b), zrow[:, 0:P], zrow[:, 0:D + 1], start=False, stop=True, skip_group_check=True).then_inc(s_sum, 1)
                    if rows_:
                        t = b - 1
                        pe.wait_ge(s_he, g + 1)
                        if L < 2:
                            pe.wait_ge(s_ho, g + 1)
                        elif not (isinstance(b, int) and b < 3):
                            pe.wait_ge(s_ln, (b - 2) * 12 + 1)
                        O = psO[0:P, 0:D] if L < 2 else rows_of(t)[:, 0:D]
                        for c in range(KC):
                            pe.matmul(O, rT[:, 0, c * P:c * P + P], WrT[:, L, c, :], start=(c == 0), stop=False)
                        pe.matmul(O, ones[:, :], bl[:, L, :], start=False, stop=False)
                        for c in range(KC):
                            m = pe.matmul(O, rT[:, 1, c * P:c * P + P], WlT[:, L, c, :], start=False, stop=(c == KC - 1))
                        m.then_inc(s_omm, 1)
                        if L == 0:
                            if not (isinstance(b, int) and b < 2):
                                pe.wait_ge(s_mix0, (b - 2) * 6 + 3)
                            pe.wait_ge(s_kvc, t * 2 + 2)
                            for c in range(KC):
                                pe.matmul(psQK[0:P, 0:D], rT[:, 0, c * P:c * P + P], Wqkv[:, c, 0:D], start=(c == 0), stop=(c == KC - 1))
                            for c in range(KC):
                                m = pe.matmul(psV[0:P, :], rT[:, 0, c * P:c * P + P], Wqkv[:, c, D:3 * D], start=(c == 0), stop=(c == KC - 1))
                            m.then_inc(s_qkv, 1)
                        if L == 1:
                            pe.wait_ge(s_ekx, t + 1)
                            for c in range(KC):
                                pe.matmul(psC[:, c * 128:c * 128 + 128], ek[:, c * 128:c * 128 + 128], v_all[:, ds(t, 1), c * 128:c * 128 + 128].rearrange("p a d -> p (a d)"),
                                          start=False, stop=False, skip_group_check=True)
                            for c in range(KC):
                                m = pe.matmul(psC[:, D + c:D + c + 1], ek[:, c * 128:c * 128 + 128], ones128[0:P, 0:1], start=False, stop=False, skip_group_check=True)
                            m.then_inc(s_ctx, 1)
                        if L == 2:
                            pe.wait_ge(s_qTe, t + 2)
                            for c in range(KC):
                                m = pe.matmul(rows_of(t)[:, D:2 * D], qT[:, c * P:c * P + P], Mx[:, c, :], start=(c == 0), stop=(c == KC - 1))
                            m.then_inc(s_omx, 1)
                if L == 1:
                    pe.sem_inc(s_ctx, 1)
                if L == 2:
                    pe.sem_inc(s_xlT, 1)
                    pe.wait_ge(s_bd, 7)
                layer(pe, body)

            pe.wait_ge(s_fw, 4 * 16)
            pe.wait_ge(s_wrow, NB)

            def ffn(g, blocks):
                n = blocks * P
                for m in range(HC):
                    pe.wait_ge(s_ge, g * HC + m + 1)
                    for c in range(KC):
                        x = pe.matmul(B[m % 4][:, 0:n], w1[:, c, m * 128:m * 128 + 128], xlT[:, c, ds(g * TOK, n)], start=(c == 0), stop=(c == KC - 1))
                    x.then_inc(s_st1, 1)
                for k in range(blocks):
                    pe.wait_ge(s_yw, g * TB + k + 1)
                    pe.matmul(B[4 + k][0:P, 0:D], ones[:, :], b2r[:, :], start=True, stop=False)
                for m in range(HC):
                    pe.wait_ge(s_ge, g * HC + m + 5)
                    for k in range(blocks):
                        x = pe.matmul(B[4 + k][0:P, 0:D], hT[:, m, k * P:k * P + P], w2[:, m, :], start=False, stop=(m == HC - 1))
                x.then_inc(s_st2, 1)
            with pe.Fori(0, NB // TB) as g:
                ffn(g, TB)
            ffn(NB // TB, NB % TB)

            pe.wait_ge(s_yw, NB + TB)
            pe.wait_ge(s_w4, 18 * 16)
            for k, (w, bank) in enumerate(((Wg, 0), (Wq, 2))):
                for i in range(KC):
                    for j in range(KC):
                        m = pe.transpose(B[bank][:, j * D + i * 128:j * D + i * 128 + 128], w[:, i, j * 128:j * 128 + 128], ident[:, :])
                m.then_inc(s_pt, 1)
            pe.wait_ge(s_pv, 1)
            pe.wait_ge(s_w5, 12 * 16)
            for i in range(KC):
                for j in range(KC):
                    pe.matmul(B[4][:, i * 8:i * 8 + 8], WgT[:, j, i * 128:i * 128 + 128], A8[:, j, :], start=(j == 0), stop=(j == KC - 1))
            for c in range(KC):
                m = pe.matmul(B[5][:, c:c + 1], bq[:, c * 128:c * 128 + 128], ones[:, 0:1], start=True, stop=True)
            m.then_inc(s_pt, 1)
            pe.wait_ge(s_pv, 10)
            pe.sem_inc(s_hsa, 1)
            pe.sem_inc(s_kva, 1)
            pe.matmul(psC[:, 0:D], zrow[:, 0:128], zrow[:, 0:D], start=True, stop=False, skip_group_check=True)
            pe.sem_inc(s_x2T, 1)
            pe.sem_inc(s_kvn, 4)

            def rows_in(b):
                pe.wait_ge(s_x2, b * 6 + 5)
                for c in range(KC):
                    m = pe.transpose(psH[:, c * P:c * P + P], xls[:, c * 128:c * 128 + 128], ident[0:P, 0:P])
                m.then_inc(s_x2T, 1)
                pe.wait_ge(s_x2Te, b * 2 + 3)
                pe.wait_ge(s_hsa, b + 1)
                for c in range(KC):
                    m = pe.matmul(psO[0:P, 0:D + 8], rT[:, 0, c * P:c * P + P], Wg[:, c, :], start=(c == 0), stop=(c == KC - 1))
                m.then_inc(s_hkv, 1)
                pe.wait_ge(s_kvn, b * 3 + 1)
                for c in range(KC):
                    pe.matmul(kv_of(b), rT[:, 0, c * P:c * P + P], Wkv[:, c, :], start=(c == 0), stop=False)
                pe.matmul(kv_of(b), ones[:, :], bkv, start=False, stop=True).then_inc(s_hkv, 1)

            def kv_sum(b):
                pe.wait_ge(s_kvg, b * 2 + 2)
                for c in range(KC):
                    m = pe.matmul(psC[:, c * 128:c * 128 + 128], kvn[:, c * 128:c * 128 + 128], kvn[:, D + c * 128:D + c * 128 + 128], start=False, stop=False, skip_group_check=True)
                m.then_inc(s_kva, 1)
            rows_in(0)
            with pe.Fori(1, NB) as b:
                rows_in(b)
                kv_sum(b - 1)
            kv_sum(NB - 1)
            pe.matmul(psC[:, 0:D], zrow[:, 0:128], zrow[:, 0:D], start=False, stop=True, skip_group_check=True).then_inc(s_kvd, 1)
            pe.sem_inc(s_free[3], RG)
            pe.wait_ge(s_k4, 2)
            for c in range(KC):
                pe.matmul(B[0][:, c * D:c * D + D], bd[:, c, :], WqT[:, c, :], start=True, stop=True)
                m = pe.matmul(B[5][:, c:c + 1], bd[:, c, :], bqc[:, c:c + 1], start=True, stop=True)
            m.then_inc(s_k4p, 1)
            pe.wait_ge(s_k4, 3)
            pe.transpose(B[7][0:4, 0:P], mx4, ident[0:P, 0:P]).then_inc(s_k4p, 1)
            pe.wait_ge(s_k4, 7)
            for i in range(KC):
                for j in range(KC):
                    pe.matmul(B[2][:, i * D:i * D + D], WqpT[:, j, i * 128:i * 128 + 128], m1[:, j, :], start=(j == 0), stop=(j == KC - 1))
                for j in range(KC):
                    m = pe.matmul(B[5][:, 4 + i:5 + i], m1[:, j, i * 128:i * 128 + 128], bqp[:, j:j + 1], start=(j == 0), stop=(j == KC - 1))
            m.then_inc(s_k4p, 1)
            pe.wait_ge(s_k4, 9)
            pe.matmul(B[7][0:P, 128:132], ones128[0:4, 0:P], dg4, start=True, stop=True).then_inc(s_k4p, 1)

            pe.wait_ge(s_k4, 11)
            pe.sem_inc(s_p1e, 2)
            pe.sem_inc(s_p2x, TB)

            def mix(g, blocks):
                n = blocks * P
                for m in range(KC):
                    pe.wait_ge(s_p1e, g * KC + m + 1)
                    for c in range(KC):
                        x = pe.matmul(B[m][:, 0:n], Wpp[:, c, m * 128:m * 128 + 128], xlT[:, c, ds(g * TOK, n)], start=(c == 0), stop=(c == KC - 1))
                    x.then_inc(s_p1, 1)
                pe.wait_ge(s_p1e, g * KC + 4)
                for k in range(blocks):
                    pe.wait_ge(s_p2x, g * TB + k + 1)
                    pe.matmul(B[4 + k][0:P, 0:D], ones[:, :], b2m, start=True, stop=False)
                    for m in range(KC):
                        x = pe.matmul(B[4 + k][0:P, 0:D], gT[:, m, k * P:k * P + P], m2[:, m, :], start=False, stop=(m == KC - 1))
                x.then_inc(s_p2, 1)
            with pe.Fori(0, NB // TB) as g:
                mix(g, TB)
            mix(NB // TB, NB % TB)

            pe.sem_inc(s_mm[3], U)

            def prepare(b, q):
                n = q + b
                pe.wait_ge(s_ohA, n + 1)
                for u in range(U):
                    m = pe.transpose(psT[0:P, u * ET:u * ET + ET], ohA[:, u, :], identh[:, :])
                m.then_inc(s_ohT, 1)

            def spread(b, q):
                n = q + b
                pe.wait_ge(s_ohTe, n + 1)
                for u in range(U):
                    for k in range(3):
                        m = pe.matmul(PS[:, ds(4 + n % 2, 1), 8 * u:8 * u + 8].rearrange("p a h -> p (a h)"),
                                      ohT[:, u * ET:u * ET + ET], tabh[:, k, ds(b, 1), :].rearrange("p a h -> p (a h)"), start=(k == 0), stop=(k == 2))
                m.then_inc(s_psx, 1)

            def edges(b, q, nb, nq):
                n = q + b
                S = PS[0:P, ds(b % 2, 1), 0:GW].rearrange("p a n -> p (a n)")
                if nb is not None:
                    prepare(nb, nq)
                    spread(nb, nq)
                pe.wait_ge(s_z, n * 5 + 5)
                for u in range(U):
                    pe.wait_ge(s_oh[3], n * U + u + 1)
                    pe.matmul(S, oh[:, u, :], wh[:, ds(n % 2 * U + u, 1), :].rearrange("p a d -> p (a d)"), start=False, stop=False, skip_group_check=True).then_inc(s_mm[3], 1)

            def begin(b):
                pe.wait_ge(s_gat, b * 7 + 1)
                pe.matmul(PS[0:P, ds(b % 2, 1), 0:GW].rearrange("p a n -> p (a n)"), zrow[:, 0:P], zrow[:, 0:GW], start=True, stop=False, skip_group_check=True)

            def end(b):
                pe.matmul(PS[0:P, ds(b % 2, 1), 0:GW].rearrange("p a n -> p (a n)"), zrow[:, 0:P], zrow[:, 0:GW], start=False, stop=True, skip_group_check=True).then_inc(s_sum, 1)
            pe.wait_ge(s_k4, 24)
            prepare(0, 0)
            spread(0, 0)
            stream(pe, begin, edges, end)

            pe.wait_ge(s_w6, 14 * 16)
            pe.sem_inc(s_mxT, 1)
            pe.sem_inc(s_mge, 1)
            pe.sem_inc(s_mg, 1)
            pe.sem_inc(s_mxTe, 3)

            def turned(b):
                pe.wait_ge(s_m, 2 * NB + 2 + b)
                pe.wait_ge(s_mxTe, b * 2 + 3)
                for c in range(KC):
                    m = pe.transpose(psH[:, c * P:c * P + P], xls[:, c * 128:c * 128 + 128], ident[0:P, 0:P])
                m.then_inc(s_mxT, 1)

            def gates(b):
                pe.wait_ge(s_mxTe, b * 2 + 4)
                pe.wait_ge(s_mge, b + 1)
                for c in range(KC):
                    pe.matmul(psO[0:P, 0:4], rT[:, 0, c * P:c * P + P], gW[:, c, :], start=(c == 0), stop=False)
                pe.matmul(psO[0:P, 0:4], ones[:, :], gbr, start=False, stop=True).then_inc(s_mg, 1)
            turned(0)
            with pe.Fori(1, NB) as b:
                turned(b)
                gates(b - 1)
            gates(NB - 1)

            pe.wait_ge(s_mge, NB + 1)
            pe.sem_inc(s_acc, 6)

            def experts(g, blocks):
                n = blocks * P
                for k in range(11):
                    to = B[k % 2]
                    pe.wait_ge(s_e2, g * 11 + k + (k > 1) + (k < 2) * (2 - k))
                    if k < 6:
                        for c in range(KC):
                            w = sW1[:, c, k * 128:k * 128 + 128] if k < 2 else eW1[:, k - 2, c, :]
                            m = pe.matmul(to[:, 0:n], w, xlT[:, c, ds(g * TOK, n)], start=(c == 0), stop=(c == KC - 1))
                    elif k == 6:
                        for c in range(KC):
                            m = pe.matmul(to[:, 0:n], sW2[:, c, :], ffh[c][:, 0:n], start=(c == 0), stop=(c == KC - 1))
                    else:
                        m = pe.matmul(to[0:64, 0:n], eW2[:, k - 7, :], ffh[k - 5][:, 0:n], start=True, stop=True)
                    m.then_inc(s_e1, 1)
                pe.wait_ge(s_e2, g * 11 + 13)
                for k in range(blocks):
                    pe.wait_ge(s_acc, (g * TB + k) * 5 + 1)
                    bank = 2 + k % 2 * 3
                    for e in range(4):
                        pe.matmul(B[bank + e // 2][0:P, e % 2 * D:e % 2 * D + D], ffh[7 + e][0:64, k * P:k * P + P], eW3[0:64, e, :], start=True, stop=True)
                    pe.matmul(B[bank + 2][0:P, 0:D], ffh[6][:, k * P:k * P + P], sW3[:, 0, :], start=True, stop=True).then_inc(s_tm, 1)
            with pe.Fori(0, NB // TB) as g:
                experts(g, TB)
            experts(NB // TB, NB % TB)


_INS = (["x", "src", "dst"] + [f"L0_gnn_{n}" for k in (1, 2, 3) for n in (f"W{k}l", f"b{k}l", f"W{k}r")]
        + [f"L0_mix_{n}" for n in "Wqkv Wout gamma".split()] + [f"L0_ffn_{n}" for n in "wr br w1 b1 w2 b2".split()]
        + [f"L1_gnn_{n}" for n in "W att_src att_dst bias".split()]
        + [f"L1_mix_{n}" for n in "w_qkv b_qkv kln_g kln_b vln_g vln_b w1 b1 w2 b2".split()]
        + [f"L1_ffn_{n}" for n in "sW1 sb1 sW2 sb2 sW3 sb3 eW1 eb1 eW2 eb2 eW3 eb3 gW gb".split()])


def kernel(**inputs):
    import numpy as _np
    import concourse.bacc as _bacc
    from concourse import mybir as _mybir
    from concourse.bass_utils import run_bass_kernel_spmd as _run
    nc = _bacc.Bacc("TRN2", target_bir_lowering=False, num_devices=1)
    arrays, args = {}, {}
    for name in _INS:
        a = _np.ascontiguousarray(inputs[name])
        arrays[f"in_{name}_dram"] = a
        args[name] = nc.dram_tensor(f"in_{name}_dram", a.shape, _mybir.dt.from_np(a.dtype), kind="ExternalInput").ap()
    out = nc.dram_tensor("out_0_dram", (N, D), F32, kind="ExternalOutput").ap()
    build(nc, args, out)
    r = _run(nc, [arrays], core_ids=[0])
    return r.results[0]["out_0_dram"]
```

```python
from contextlib import ExitStack

import concourse.bass as bass
from concourse import mybir

F32 = mybir.dt.float32
I32 = mybir.dt.int32
BF16 = mybir.dt.bfloat16
ALU = mybir.AluOpType
ACT = mybir.ActivationFunctionType
AX = mybir.AxisListType

N, D, E = 3125, 256, 50000
P = 125
NB = N // P
KC = D // 128
ET = 128
NT = -(-E // ET)
U = 4
NG = -(-NT // U)
GS = 16
RG = GS // U
LAG = 4
GW = 260
EPS = 1e-5
H1 = 4 * D
HC = H1 // 128
TB = 4
TOK = TB * P
CHOSEN = max(1, N // 2) - 1
ds = bass.ds


def build(nc, I, out):
    with ExitStack() as ctx:
        def sb(name, shape, dt=F32):
            return ctx.enter_context(nc.sbuf_tensor(name, shape, dt))

        def sem(name):
            return ctx.enter_context(nc.semaphore(name))

        bigk = sb("bigk", [128, NB * D])
        bigv = sb("bigv", [128, NB * D])
        bigx = sb("bigx", [128, NB * D])
        bigq = sb("bigq", [128, NB * D])
        ho = sb("ho", [128, D])
        iota = sb("iota", [128, N])
        G = sb("G", [128, GS, GW])
        oh = sb("oh", [128, U, P])
        ident = sb("ident", [128, 128])
        eps = sb("eps", [128, 1])
        ones = sb("ones", [1, P])
        zrow = sb("zrow", [1, 512], BF16)
        idx = sb("idx", [128, NG * U], I32)
        idxc = sb("idxc", [128, 16], I32)
        dstf = sb("dstf", [128, NG * U])
        qrun = sb("qrun", [1, 2, NB + 1], I32)
        st = sb("st", [128, 2, D])
        rT = sb("rT", [128, 2, KC * 128])
        st6 = sb("st6", [128, NB, 6])
        mv = sb("mv", [128, NB, 3])
        rdeg = sb("rdeg", [128, 2])
        gamma = sb("gamma", [P, D])
        rm = sb("rm", [P, D])
        kmb = sb("kmb", [P, D])
        kmx = sb("kmx", [128, KC])
        dg = sb("dg", [128, KC, 128])
        ones128 = sb("ones128", [128, P])
        bdm = sb("bdm", [128, 128])
        qst = sb("qst", [P, 3, 8])
        qsm = sb("qsm", [P, D])
        ek = sb("ek", [P, D])
        dn = sb("dn", [128, KC])
        bd = sb("bd", [128, KC, 128])
        bdT = sb("bdT", [128, KC, 128])
        qT = sb("qT", [128, KC * P])
        ty = sb("ty", [P, D])
        xs = sb("xs", [P, D])
        x1s = sb("x1s", [P, D])
        xls = sb("xls", [P, D])
        lst = sb("lst", [P, 2, 10])
        wr = sb("wr", [128, KC])
        wrr = sb("wrr", [128, KC, P])
        br = sb("br", [P, 1])
        b1c = sb("b1c", [128, HC])
        b2r = sb("b2r", [1, D])
        wcol = sb("wcol", [P, NB])
        cnt = sb("cnt", [P, NB, 4])
        sel = sb("sel", [P, NB])
        tril = sb("tril", [P, P])
        triu = sb("triu", [P, P])
        bl = sb("bl", [1, 3, D])
        ohT = sb("ohT", [P, U * ET], BF16)
        ez = sb("ez", [128, U, 4])
        rs8 = sb("rs8", [P, 8])
        actw = sb("actw", [P, 1])
        identh = sb("identh", [128, 128], BF16)
        tabh = sb("tabh", [P, 3, NB, 8], BF16)
        wA = sb("wA", [128, 11 * KC * D])
        wB = sb("wB", [128, 2 * KC * H1])
        PS = ctx.enter_context(nc.psum_tensor("PS", [128, 8, 512], F32))
        B = [PS[:, k, :] for k in range(8)]
        psH, psHM, psO = B[1:4]
        psQK, psV = B[4], B[5]
        psC, psA = B[6], B[7]
        psT = B[2][:, 0:U * ET // 2].bitcast(BF16)

        tab = [nc.dram_tensor(f"tab{k}", [N, D], F32, kind="Internal").ap() for k in range(3)]
        gtab = nc.dram_tensor("gtab", [N, GW], F32, kind="Internal").ap()
        tabb = [t.rearrange("(b p) d -> p b d", p=P) for t in tab]

        by_block = [t[0:P, :].rearrange("p (b d) -> p b d", b=NB) for t in (bigk, bigv, bigx, bigq)]
        k_all, v_all, x1_all, q_all = by_block
        xin, h = q_all, x1_all
        xlT = bigk[:, 0:KC * N].rearrange("p (c n) -> p c n", c=KC)

        def blk(t, b):
            return t[:, ds(b, 1), :].rearrange("p a d -> p (a d)")

        wrow = bigv[0:P, 0:N]
        yw = q_all
        hT = G[:, :, :].rearrange("p s d -> p (s d)")[:, 0:HC * TOK].rearrange("p (m n) -> p m n", m=HC)
        junk = bigv[0:P, N:2 * N]
        junk2 = bigv[0:P, 2 * N:2 * N + P]

        def part(buf, at, *shape):
            n = 1
            for k in shape:
                n *= k
            v = buf[:, at:at + n]
            names = "abc"[:len(shape)]
            return v.rearrange(f"p ({' '.join(names)}) -> p {' '.join(names)}", **dict(zip(names, shape)))
        W1 = KC * D
        WlT, WrT = part(wA, 0, 3, KC, D), part(wA, 3 * W1, 3, KC, D)
        Wqkv = part(wA, 6 * W1, KC, 3 * D)
        Wout = part(wA, 9 * W1, KC, D)
        Mx = part(wA, 10 * W1, KC, D)
        w1, w2 = part(wB, 0, KC, H1), part(wB, KC * H1, HC, D)

        Wg = part(wA, 0, KC, D + 8)
        at = KC * (D + 8)
        Wkv = part(wA, at, KC, 2 * D)
        at += 2 * W1
        Wq, WqT, WqpT, m1, m2, Wpp, WgT = [part(wA, at + k * W1, KC, D) for k in range(7)]
        at += 7 * W1
        A8 = part(wA, at, KC, 8)
        bqc, bqp, b1m, bpp = [part(wA, at + 16 + KC * k, KC) for k in range(4)]
        cmean = wA[:, at + 24:at + 56]
        gbk = bigv[0:P, 0:4 * D].rearrange("p (a d) -> p a d", a=2)
        kvn = bigv[0:P, 1024:1536]
        sq = bigv[0:P, 1536:2048]
        hs = bigv[0:P, 2048:2048 + D + 8]
        gbias = bigv[0:P, 2320:2320 + D]
        bkv = bigv[0:1, 2576:2576 + 2 * D]
        bq = bigv[0:1, 3088:3088 + D]
        b2m = bigv[0:1, 3344:3344 + D]
        b3 = bigv[0:P, 3600:3600 + 5 * D]
        asd = bigv[0:P, 4880:4880 + 8 * NB].rearrange("p (b h) -> p b h", b=NB)
        tab8 = bigv[0:P, 5080:5080 + 8 * NB].rearrange("p (b h) -> p b h", b=NB)
        tabr = bigv[0:P, 6000:6000 + 8 * NB].rearrange("p (b h) -> p b h", b=NB)
        wself = bigv[0:P, 5280:5280 + 4 * NB].rearrange("p (b h) -> p b h", b=NB)
        ss = bigv[0:P, 5380:5412]
        mx4 = bigv[0:P, 5412:5416]
        kx = bigv[0:4, 5416:5417]
        dg4 = bigv[0:4, 5420:5424]
        bmean = bigv[0:1, 5424:5440]
        gbr = bigv[0:1, 5440:5444]
        gl, gx, gr2, ga, gp = [bigv[0:P, 5444 + k * 4 * NB:5444 + (k + 1) * 4 * NB].rearrange("p (b h) -> p b h", b=NB) for k in range(5)]
        g1 = bigv[0:P, 5944:5944 + NB].rearrange("p (b h) -> p b h", b=NB)
        at = 0
        def take(*shape):
            nonlocal at
            n = 1
            for k in shape:
                n *= k
            at += n
            return part(wB, at - n, *shape)
        sW1, sW2, sW3 = take(KC, D), take(KC, 128), take(1, D)
        eW1, eW2, eW3 = take(4, KC, 128), take(4, 64), take(4, D)
        gW, sb1, sb2, eb1, eb2 = take(KC, 4), take(KC), take(1), take(4), take(4)
        gT = bigq[:, 0:KC * TOK].rearrange("p (m n) -> p m n", m=KC)
        ffh = [bigq[:, k * TOK:(k + 1) * TOK] for k in range(11)]

        ohA = bigq[:, 0:U * P // 2].bitcast(BF16).rearrange("p (u n) -> p u n", u=U)
        wh = bigq[:, 512:512 + 2 * U * GW].rearrange("p (u d) -> p u d", u=2 * U)

        rows = bigk[:, 0:2 * 4 * ET].rearrange("p (a c e) -> p a c e", a=2, c=4)
        rowsi = bigk[:, 1024:2048].bitcast(I32).rearrange("p (a c e) -> p a c e", a=2, c=4)
        red = bigk[:, 2048:2048 + 40]
        redi = bigk[:, 2096:2104].bitcast(I32)
        wst = bigv[:, 3200:3200 + 6 * KC * D].rearrange("p (m c d) -> p m c d", m=6, c=KC)

        s_edges = sem("s_edges")
        s_x = [sem(f"s_xin{g}") for g in range(5)]
        s_sage_w = sem("s_sage_w")
        s_consts = sem("s_consts")
        s_pad = sem("s_pad")
        s_edge_rows = sem("s_edge_rows")
        s_edgeT = sem("s_edgeT")
        s_edgeT_out = sem("s_edgeT_out")
        s_wT = sem("s_wT")
        s_wT_out = sem("s_wT_out")
        s_tile_ends = sem("s_tile_ends")
        s_tile_endsT = sem("s_tile_endsT")
        s_runs_step = sem("s_runs_step")
        s_runs = sem("s_runs")
        s_stats = sem("s_stats")
        s_moments = sem("s_moments")
        s_rstd = sem("s_rstd")
        s_dev = sem("s_dev")
        s_normed = sem("s_normed")
        s_table0 = sem("s_table0")
        s_iota = sem("s_iota")
        LAYERS = range(3)
        s_gathered = [[sem(f"s_gathered{k}_{u}") for u in range(LAG)] for k in range(4)]
        s_idx = [sem(f"s_idx{k}") for k in range(4)]
        s_landed = [sem(f"s_landed{k}") for k in range(4)]
        s_free = [sem(f"s_free{k}") for k in range(4)]
        s_onehot = [sem(f"s_onehot{k}") for k in range(4)]
        s_summed = [sem(f"s_summed{k}") for k in range(4)]
        s_sum = sem("s_sum")
        s_mean = sem("s_mean")
        s_gat = sem("s_gat")
        s_own_in = sem("s_own_in")
        s_ownT = sem("s_ownT")
        s_features = sem("s_features")
        s_meanT = sem("s_meanT")
        s_rows = sem("s_rows")
        s_relu = sem("s_relu")
        s_out_free = sem("s_out_free")
        s_stored = sem("s_stored")
        s_mix_w = sem("s_mix_w")
        s_gathers_done = sem("s_gathers_done")
        s_out = sem("s_out")
        s_ffn_w = sem("s_ffn_w")
        s_wcol = sem("s_wcol")
        s_rank = sem("s_rank")
        s_gelu = sem("s_gelu")
        s_outer = sem("s_outer")
        s_scaled = sem("s_scaled")
        s_inner = sem("s_inner")
        s_gat_w = sem("s_gat_w")
        s_biases = sem("s_biases")
        s_moe_w = sem("s_moe_w")
        s_att_clear = sem("s_att_clear")
        s_ln2 = sem("s_ln2")
        s_ln2_dev = sem("s_ln2_dev")
        s_ln2_T = sem("s_ln2_T")
        s_ln2_T_out = sem("s_ln2_T_out")
        s_proj = sem("s_proj")
        s_table_row = sem("s_table_row")
        s_kv_dev = sem("s_kv_dev")
        s_att_out = sem("s_att_out")
        s_kv_affine = sem("s_kv_affine")
        s_kv_normed = sem("s_kv_normed")
        s_kv_added = sem("s_kv_added")
        s_gat_stored = sem("s_gat_stored")
        s_prepT = sem("s_prepT")
        s_prep = sem("s_prep")
        s_kv_sum = sem("s_kv_sum")
        s_fold = sem("s_fold")
        s_fold_mm = sem("s_fold_mm")
        s_self_w = sem("s_self_w")
        s_mix_in = sem("s_mix_in")
        s_mix_gelu = sem("s_mix_gelu")
        s_mix_out = sem("s_mix_out")
        s_mix_added = sem("s_mix_added")
        s_onehotT = sem("s_onehotT")
        s_onehotT_out = sem("s_onehotT_out")
        s_spread = sem("s_spread")
        s_edge_w = sem("s_edge_w")
        s_edge_exp = sem("s_edge_exp")
        s_onehot_in = sem("s_onehot_in")
        s_ln3 = sem("s_ln3")
        s_ln3_dev = sem("s_ln3_dev")
        s_ln3_T = sem("s_ln3_T")
        s_ln3_T_out = sem("s_ln3_T_out")
        s_gates = sem("s_gates")
        s_gates_out = sem("s_gates_out")
        s_top2 = sem("s_top2")
        s_top2_exp = sem("s_top2_exp")
        s_experts = sem("s_experts")
        s_experts_out = sem("s_experts_out")
        s_expert_rows = sem("s_expert_rows")
        s_added = sem("s_added")
        s_act_table = sem("s_act_table")
        s_last_bias = sem("s_last_bias")
        s_q_softmax = sem("s_q_softmax")
        s_qkv = sem("s_qkv")
        s_kv_out = sem("s_kv_out")
        s_q_exp = sem("s_q_exp")
        s_kmax = sem("s_kmax")
        s_kmaxT = sem("s_kmaxT")
        s_kmax_rows = sem("s_kmax_rows")
        s_k_shifted = sem("s_k_shifted")
        s_k_exp = sem("s_k_exp")
        s_context = sem("s_context")
        s_ctx_w = sem("s_ctx_w")
        s_ctx_w_mm = sem("s_ctx_w_mm")
        s_x_rows = sem("s_x_rows")
        s_q_rows = sem("s_q_rows")
        s_qT = sem("s_qT")
        s_qT_out = sem("s_qT_out")
        s_mixed = sem("s_mixed")
        s_ln1 = sem("s_ln1")
        s_ln1_dev = sem("s_ln1_dev")
        s_ln1_T = sem("s_ln1_T")
        s_ln1_T_out = sem("s_ln1_T_out")
        s_router = sem("s_router")
        s_router_out = sem("s_router_out")
        s_router_w = sem("s_router_w")

        block = ctx.enter_context(nc.Block())
        full = E // ET // 128
        rest = E // ET - full * 128
        tail = E - (E // ET) * ET
        chunk_rows = [128] * full + [rest + 1]

        def group_range(eng, b):
            return [eng.value_load(qrun[0:1, k, ds(b, 1)], min_val=k, max_val=NB * NG) for k in range(2)]

        def layer(eng, body):
            for b in range(3):
                body(b, True, b > 0, b > 1, False)
            with eng.Fori(3, NB) as b:
                body(b, True, True, True, True)
            for k in range(3):
                body(NB + k, False, k < 1, k < 2, True)

        def rows_of(b):
            return PS[0:P, ds(3 + b % 2, 1), :].rearrange("p a n -> p (a n)")

        def sums_of(L, b):
            return PS[0:P, ds((L * NB + b) % 2, 1), 0:D + 1].rearrange("p a n -> p (a n)")

        def kv_of(b):
            return PS[0:P, ds(4 + b % 2, 1), :].rearrange("p a n -> p (a n)")

        def stream(eng, begin, step, end, late=None):
            def body(b, first, last):
                q0, q1 = [eng.value_load(qrun[0:1, 0, ds(b + k, 1)], min_val=0, max_val=NB * NG) for k in range(2)]
                begin(b)
                with eng.If(q1 > q0):
                    with eng.Fori(q0, q1) as q:
                        step(b, q, b, q + 1)
                if late and not first:
                    late(b - 1)
                step(b, q1, None if last else b + 1, q1)
                end(b)
            body(0, True, False)
            with eng.Fori(1, NB - 1) as b:
                body(b, False, False)
            body(NB - 1, False, True)
            if late:
                late(NB - 1)

        def ring(q, u):
            return ds(q % RG * U + u, 1)

        @block.sync
        def _(sp):
            sp.wait_ge(s_pad, 2)
            for a, e in enumerate((I["src"], I["dst"])):
                sp.dma_start(rowsi[:, a, 0:full, :], e[0:full * 128 * ET].rearrange("(c p e) -> p c e", p=128, e=ET)).then_inc(s_edges, 16)
                sp.dma_start(rowsi[0:rest, a, full, :], e[full * 128 * ET:(E // ET) * ET].rearrange("(p e) -> p e", e=ET)).then_inc(s_edges, 16)
                sp.dma_start(rowsi[rest:rest + 1, a, full, 0:tail], e[(E // ET) * ET:E].rearrange("(p e) -> p e", p=1)).then_inc(s_edges, 16)
            for g in range(5):
                sp.dma_start(xin[0:P, 5 * g:5 * g + 5, :], I["x"].rearrange("(b p) d -> p b d", p=P)[:, 5 * g:5 * g + 5, :]).then_inc(s_x[g], 16)
            for k in range(3):
                sp.dma_start(wst[:, k, :, :], I[f"L0_gnn_W{k+1}l"].rearrange("(c p) d -> p c d", p=128)).then_inc(s_sage_w, 16)
                sp.dma_start(wst[:, 3 + k, :, :], I[f"L0_gnn_W{k+1}r"].rearrange("(c p) d -> p c d", p=128)).then_inc(s_sage_w, 16)
                sp.dma_start(bl[:, k, :], I[f"L0_gnn_b{k+1}l"].rearrange("(a d) -> a d", a=1)).then_inc(s_sage_w, 16)
            sp.dma_start(Wqkv[:, :, :], I["L0_mix_Wqkv"].rearrange("(c p) d -> p c d", p=128)).then_inc(s_mix_w, 16)
            sp.dma_start(Wout[:, :, :], I["L0_mix_Wout"].rearrange("(c p) d -> p c d", p=128)).then_inc(s_mix_w, 16)
            sp.dma_start(gamma[:, :], I["L0_mix_gamma"].rearrange("(a d) -> a d", a=1).broadcast_to((P, D))).then_inc(s_mix_w, 16)
            sp.dma_start(wr[:, :], I["L0_ffn_wr"].rearrange("(c p) o -> p (c o)", p=128), allow_slow_non_contiguous=True).then_inc(s_mix_w, 16)
            sp.dma_start(br[:, :], I["L0_ffn_br"].rearrange("(a d) -> a d", a=1).broadcast_to((P, 1))).then_inc(s_mix_w, 16)
            sp.dma_start(w1[:, :, :], I["L0_ffn_w1"].rearrange("(c p) d -> p c d", p=128)).then_inc(s_ffn_w, 16)
            sp.dma_start(w2[:, :, :], I["L0_ffn_w2"].rearrange("(c p) d -> p c d", p=128)).then_inc(s_ffn_w, 16)
            sp.dma_start(b1c[:, :], I["L0_ffn_b1"].rearrange("(c p) -> p c", p=128), allow_slow_non_contiguous=True).then_inc(s_ffn_w, 16)
            sp.dma_start(b2r[:, :], I["L0_ffn_b2"].rearrange("(a d) -> a d", a=1)).then_inc(s_ffn_w, 16)
            for g in range(5):
                sp.wait_ge(s_normed, 5 * g + 5)
                sp.dma_start(tabb[0][:, 5 * g:5 * g + 5, :], h[0:P, 5 * g:5 * g + 5, :]).then_inc(s_table0, 16)
            for L in LAYERS:
                if L == 0:
                    sp.wait_ge(s_table0, 5 * 16)
                else:
                    sp.wait_ge(s_stored, L * NB * 16)
                def own_rows(b):
                    sp.wait_ge(s_ownT, L * NB + b + 1)
                    sp.dma_start(st[0:P, 0, :], tab[L][ds(b * P, P), :]).then_inc(s_own_in, 16)

                def results(b):
                    if L < 2:
                        sp.wait_ge(s_relu, L * NB + b + 2)
                        sp.dma_start(tab[L + 1][ds(b * P, P), :], ho[0:P, :]).then_inc(s_stored, 16)
                        sp.wait_ge(s_stored, (L * NB + b + 1) * 16)
                        sp.sem_inc(s_out_free, 1)
                    else:
                        sp.wait_ge(s_ln1, b * 12 + 1)
                        sp.dma_start(xs[:, :], I["x"][ds(b * P, P), :]).then_inc(s_x_rows, 16)
                own_rows(0)
                with sp.Fori(0, NB - 1) as b:
                    own_rows(b + 1)
                    results(b)
                results(NB - 1)
            row = lambda t: t.rearrange("(a d) -> a d", a=1)
            sp.wait_ge(s_router, NB)
            sp.wait_ge(s_att_clear, 1)
            sp.dma_start(Wg[:, :, 0:D], I["L1_gnn_W"].rearrange("(c p) d -> p c d", p=128)).then_inc(s_gat_w, 16)
            for a, w in enumerate((I["L1_gnn_att_src"], I["L1_gnn_att_dst"])):
                for k in range(4):
                    lo = 64 * (k % 2)
                    sp.dma_start(A8[lo:lo + 64, k // 2, 4 * a + k:4 * a + k + 1], w[k:k + 1, :].rearrange("a f -> f a"), allow_slow_non_contiguous=True).then_inc(s_gat_w, 16)
            wq = I["L1_mix_w_qkv"].rearrange("(c p) (h t e) -> c t p h e", p=128, t=3, e=32)
            for c in range(KC):
                for t in range(3):
                    to = Wq[:, c, :] if t == 0 else Wkv[:, c, (t - 1) * D:t * D]
                    sp.dma_start(to.rearrange("p (h e) -> p h e", h=8), wq[c, t]).then_inc(s_gat_w, 16)
            sp.dma_start(m1[:, :, :], I["L1_mix_w1"].rearrange("(c p) d -> p c d", p=128)).then_inc(s_gat_w, 16)
            sp.dma_start(m2[:, :, :], I["L1_mix_w2"].rearrange("(c p) d -> p c d", p=128)).then_inc(s_gat_w, 16)
            sp.dma_start(b1m[:, :], I["L1_mix_b1"].rearrange("(c p) -> p c", p=128), allow_slow_non_contiguous=True).then_inc(s_gat_w, 16)
            sp.wait_ge(s_rank, 4 * NB)
            for a, n in enumerate(("g", "b")):
                for k, t in enumerate(("kln", "vln")):
                    sp.dma_start(gbk[:, a, k * D:(k + 1) * D].rearrange("p (h e) -> p h e", h=8),
                                 I[f"L1_mix_{t}_{n}"].rearrange("(a b e) -> a b e", a=1, b=1).broadcast_to((P, 8, 32))).then_inc(s_biases, 16)
            bs = I["L1_mix_b_qkv"].rearrange("(a h t e) -> t a h e", a=1, t=3, e=32)
            for t in range(3):
                to = bq if t == 0 else bkv[:, (t - 1) * D:t * D]
                sp.dma_start(to.rearrange("p (h e) -> p h e", h=8), bs[t]).then_inc(s_biases, 16)
            sp.dma_start(gbias, row(I["L1_gnn_bias"]).broadcast_to((P, D))).then_inc(s_biases, 16)
            sp.dma_start(b2m, row(I["L1_mix_b2"])).then_inc(s_biases, 16)
            sp.dma_start(b3[:, 0:D], row(I["L1_ffn_sb3"]).broadcast_to((P, D))).then_inc(s_biases, 16)
            sp.dma_start(b3[:, D:5 * D], I["L1_ffn_eb3"].rearrange("(a e) d -> a (e d)", a=1).broadcast_to((P, 4 * D))).then_inc(s_biases, 16)
            sp.dma_start(gbr, row(I["L1_ffn_gb"])).then_inc(s_biases, 16)
            sp.wait_ge(s_outer, NB // TB + 1)
            sp.dma_start(sW1, I["L1_ffn_sW1"].rearrange("(c p) d -> p c d", p=128)).then_inc(s_moe_w, 16)
            sp.dma_start(sW2, I["L1_ffn_sW2"].rearrange("(c p) d -> p c d", p=128)).then_inc(s_moe_w, 16)
            sp.dma_start(sW3[:, 0, :], I["L1_ffn_sW3"]).then_inc(s_moe_w, 16)
            for k in range(4):
                sp.dma_start(eW1[:, k, :, :], I["L1_ffn_eW1"][k].rearrange("(c p) d -> p c d", p=128)).then_inc(s_moe_w, 16)
            sp.dma_start(eW2, I["L1_ffn_eW2"].rearrange("k p d -> p k d")).then_inc(s_moe_w, 16)
            sp.dma_start(eW3[0:64, :, :], I["L1_ffn_eW3"].rearrange("k p d -> p k d")).then_inc(s_moe_w, 16)
            sp.dma_start(gW, I["L1_ffn_gW"].rearrange("(c p) d -> p c d", p=128), allow_slow_non_contiguous=True).then_inc(s_moe_w, 16)
            sp.dma_start(sb1, I["L1_ffn_sb1"].rearrange("(c p) -> p c", p=128), allow_slow_non_contiguous=True).then_inc(s_moe_w, 16)
            sp.dma_start(sb2, I["L1_ffn_sb2"].rearrange("(p c) -> p c", c=1), allow_slow_non_contiguous=True).then_inc(s_moe_w, 16)
            sp.dma_start(eb1, I["L1_ffn_eb1"].rearrange("k p -> p k"), allow_slow_non_contiguous=True).then_inc(s_moe_w, 16)
            sp.dma_start(eb2[0:64, :], I["L1_ffn_eb2"].rearrange("k p -> p k"), allow_slow_non_contiguous=True).then_inc(s_moe_w, 16)
            with sp.Fori(0, NB) as b:
                sp.wait_ge(s_table_row, b + 1)
                sp.dma_start(gtab[ds(b * P, P), :], hs[:, 0:GW]).then_inc(s_gat_stored, 16)
                sp.wait_ge(s_gat_stored, (b + 1) * 16)
                sp.sem_inc(s_out_free, 1)
            sp.wait_ge(s_gat_stored, NB * 16)
            with sp.Fori(0, NB) as b:
                sp.wait_ge(s_gat, b * 7 + 5)
                sp.dma_start(st[0:P, 0, :], gtab[ds(b * P, P), 0:D]).then_inc(s_own_in, 16)
            with sp.Fori(0, NB) as b:
                sp.wait_ge(s_added, b * 5 + 11)
                sp.dma_start(out[ds(b * P, P), :], blk(x1_all, b)).then_inc(s_out, 16)
            sp.wait_ge(s_out, NB * 16)

        @block.gpsimd
        def _(pool):
            pool.memset(ident[:, :], 1.0).then_inc(s_consts, 1)
            pool.memset(G[:, :, D:GW], 1.0).then_inc(s_consts, 1)
            pool.memset(idx[:, :], 0).then_inc(s_consts, 1)
            pool.iota(bigv[:, 0:N].bitcast(I32), pattern=[[1, N]], base=0, channel_multiplier=0).then_inc(s_consts, 1)
            pool.wait_ge(s_consts, 4)
            pool.affine_select(out=ident[:, :], in_=ident[:, :], compare_op=ALU.is_equal, fill=0.0,
                               base=0, pattern=[[-1, 128]], channel_multiplier=1).then_inc(s_consts, 1)
            pool.memset(ones[:, :], 1.0).then_inc(s_consts, 1)
            pool.memset(eps[:, :], EPS).then_inc(s_consts, 1)
            pool.memset(zrow[:, :], 0.0).then_inc(s_consts, 1)
            pool.memset(ones128[:, :], 1.0).then_inc(s_consts, 1)
            pool.memset(bdm[:, :], 0.0).then_inc(s_consts, 1)
            pool.wait_ge(s_consts, 10)
            for q in range(4):
                pool.memset(bdm[32 * q:32 * q + 32, 32 * q:32 * q + 32], 1.0).then_inc(s_consts, 1)
            pool.wait_ge(s_consts, 14)
            pool.memset(tril[:, :], 1.0).then_inc(s_consts, 1)
            pool.memset(triu[:, :], 1.0).then_inc(s_consts, 1)
            pool.wait_ge(s_consts, 16)
            pool.affine_select(out=tril[:, :], in_=tril[:, :], compare_op=ALU.is_gt, fill=0.0,
                               base=0, pattern=[[-1, P]], channel_multiplier=1).then_inc(s_consts, 1)
            pool.affine_select(out=triu[:, :], in_=triu[:, :], compare_op=ALU.is_gt, fill=0.0,
                               base=0, pattern=[[1, P]], channel_multiplier=-1).then_inc(s_consts, 1)
            pool.wait_ge(s_runs, 2)
            for L in range(4):
                if L == 3:
                    pool.wait_ge(s_biases, 12 * 16)
                    with pool.Fori(0, NB) as b:
                        pool.wait_ge(s_kv_normed, b * 3 + 7)
                        pool.tensor_tensor(kvn, kvn, gbk[:, 0, :], ALU.mult).then_inc(s_kv_affine, 1)
                        pool.wait_ge(s_kv_affine, b * 2 + 1)
                        pool.tensor_tensor(kvn, kvn, gbk[:, 1, :], ALU.add).then_inc(s_kv_affine, 1)
                if L == 0:
                    pool.wait_ge(s_table0, 5 * 16)
                elif L == 3:
                    pool.wait_ge(s_gat_stored, NB * 16)
                else:
                    pool.wait_ge(s_stored, L * NB * 16)
                groups = pool.value_load(qrun[0:1, 1, NB - 1:NB], min_val=1, max_val=NB * NG)

                def gathers(q, slot):
                    pool.tensor_copy(idxc[:, slot:slot + U], idx[:, ds(q % NG * U, U)]).then_inc(s_idx[L], 1)
                    pool.wait_ge(s_idx[L], q + 1)
                    pool.wait_ge(s_free[L], q + 1)
                    for u in range(U):
                        if not isinstance(q, int):
                            pool.wait_ge(s_gathered[L][u], q * 16)
                            pool.sem_inc(s_landed[L], 1)
                        pool.indirect_dma_start(out=G[:, slot + u, 0:D if L < 3 else GW], out_offset=None, in_=tab[L][:, :] if L < 3 else gtab[:, :],
                                                in_offset=bass.IndirectOffsetOnAxis(ap=idxc[:, slot + u:slot + u + 1], axis=0)).then_inc(s_gathered[L][u], 16)

                gathers(0, 0)
                with pool.Fori(1, groups, RG) as q:
                    for k in range(RG):
                        gathers(q + k, (k + 1) % RG * U)
                for u in range(LAG):
                    pool.wait_ge(s_gathered[L][u], ((groups + (RG - 2)) // RG * RG + 1) * 16)
                    pool.sem_inc(s_landed[L], 1)
                pool.sem_inc(s_gathers_done, 1)

        @block.vector
        def _(dve):
            dve.memset(rowsi[:, 0, :, :], 0).then_inc(s_pad, 1)
            dve.memset(rowsi[:, 1, :, :], N).then_inc(s_pad, 1)
            dve.wait_ge(s_consts, 4)
            dve.tensor_copy(iota[:, :], bigv[:, 0:N].bitcast(I32)).then_inc(s_iota, 1)
            dve.memset(dstf[:, :], float(N)).then_inc(s_iota, 1)
            dve.wait_ge(s_edges, 96)
            dve.tensor_copy(rows[:, :, :, :], rowsi[:, :, :, :]).then_inc(s_edge_rows, 1)
            dve.wait_ge(s_edge_rows, 1)
            c1 = red[:, 0:4]
            c2 = red[:, 4:8]
            dve.tensor_reduce(c1, rows[:, 1, :, :], AX.X, ALU.min).then_inc(s_tile_ends, 1)
            dve.tensor_scalar(bigk[:, 4096:4096 + 512].rearrange("p (c e) -> p c e", c=4), rows[:, 1, :, :], float(N - 1), None, ALU.min).then_inc(s_tile_ends, 1)
            dve.wait_ge(s_tile_ends, 2)
            dve.tensor_reduce(c2, bigk[:, 4096:4096 + 512].rearrange("p (c e) -> p c e", c=4), AX.X, ALU.max).then_inc(s_tile_ends, 1)
            dve.wait_ge(s_tile_ends, 3)
            dve.tensor_scalar(red[:, 16:24], red[:, 0:8], 0.5, 1.0 / P, ALU.add, ALU.mult).then_inc(s_tile_ends, 1)
            dve.wait_ge(s_tile_ends, 4)
            dve.tensor_copy(redi, red[:, 16:24]).then_inc(s_tile_ends, 1)
            dve.wait_ge(s_tile_ends, 5)
            dve.tensor_copy(red[:, 24:32], redi).then_inc(s_tile_ends, 1)
            dve.wait_ge(s_tile_ends, 6)
            dve.tensor_tensor(red[:, 32:40], red[:, 24:32], red[:, 16:24], ALU.is_gt).then_inc(s_tile_ends, 1)
            dve.wait_ge(s_tile_ends, 7)
            dve.tensor_tensor(red[:, 8:16], red[:, 24:32], red[:, 32:40], ALU.subtract).then_inc(s_tile_ends, 1)
            for c in range(4):
                for a in range(2):
                    k = 2 * c + a
                    dve.wait_ge(s_edgeT, k + 1)
                    src_ps = B[k % 4][:, 0:chunk_rows[c]]
                    dst_sb = (idx if a == 0 else dstf)[:, 128 * c:128 * c + chunk_rows[c]]
                    dve.tensor_copy(dst_sb, src_ps).then_inc(s_edgeT_out, 1)
            gr = bigk[0:1, 3000:3000 + 4 * NG]
            gmin, gmax, gt = gr[:, 0:NG], gr[:, NG:2 * NG], gr[:, 2 * NG:3 * NG]
            fl = bigk[0:1, 3400:3404]
            qs, qg = bigk[0:1, 3410:3410 + NB], bigk[0:1, 3440:3440 + NB]
            le = bigk[0:1, 3470:3470 + NB * NG].rearrange("p (b g) -> p b g", b=NB)
            dve.wait_ge(s_tile_endsT, 8)
            dve.tensor_reduce(gmin, B[4][0:1, 0:NG * U].rearrange("p (g u) -> p g u", u=U), AX.X, ALU.min).then_inc(s_runs_step, 1)
            dve.tensor_reduce(gmax, B[5][0:1, 0:NG * U].rearrange("p (g u) -> p g u", u=U), AX.X, ALU.max).then_inc(s_runs_step, 1)
            dve.wait_ge(s_runs_step, 2)
            dve.tensor_tensor(gt[:, 0:NG - 1], gmin[:, 1:NG], gmax[:, 0:NG - 1], ALU.is_lt).then_inc(s_runs_step, 1)
            dve.wait_ge(s_runs_step, 3)
            dve.tensor_reduce(fl[:, 0:1], gt[:, 0:NG - 1], AX.X, ALU.max).then_inc(s_runs_step, 1)
            dve.tensor_tensor(le, gmin.rearrange("p (b g) -> p b g", b=1).broadcast_to((1, NB, NG)), iota[0:1, 0:NB].rearrange("p (b g) -> p b g", g=1).broadcast_to((1, NB, NG)), ALU.is_le).then_inc(s_runs_step, 1)
            dve.wait_ge(s_runs_step, 5)
            dve.tensor_reduce(qs, le, AX.X, ALU.add).then_inc(s_runs_step, 1)
            dve.tensor_scalar(qg, iota[0:1, 0:NB], float(NG - 1), float(NG), ALU.mult, ALU.add).then_inc(s_runs_step, 1)
            dve.wait_ge(s_runs_step, 7)
            dve.tensor_scalar(qs, qs, 1.0, None, ALU.max).then_inc(s_runs_step, 1)
            dve.wait_ge(s_runs_step, 8)
            dve.tensor_tensor(qg, qg, qs, ALU.subtract).then_inc(s_runs_step, 1)
            dve.wait_ge(s_runs_step, 9)
            dve.scalar_tensor_tensor(out=qs, in0=qg, scalar=fl[:, 0:1], in1=qs, op0=ALU.mult, op1=ALU.add).then_inc(s_runs_step, 1)
            dve.memset(qrun[:, 0, 0:1], 0).then_inc(s_runs_step, 1)
            dve.wait_ge(s_runs_step, 11)
            dve.tensor_copy(qrun[:, 1, 0:NB], qs).then_inc(s_runs, 1)
            dve.tensor_scalar(qg, qs, -1.0, None, ALU.add).then_inc(s_runs_step, 1)
            dve.wait_ge(s_runs_step, 12)
            dve.tensor_copy(qrun[:, 0, 1:NB + 1], qg).then_inc(s_runs, 1)

            for g in range(5):
                dve.wait_ge(s_x[g], 16)
                for b in range(5 * g, 5 * g + 5):
                    dve.bn_stats(st6[0:P, b, :], xin[0:P, b, :]).then_inc(s_stats, 1)
                for b in range(5 * g, 5 * g + 5):
                    dve.wait_ge(s_stats, b + 1)
                    dve.bn_aggr(mv[0:P, b, 0:2], st6[0:P, b, :]).then_inc(s_moments, 1)
            for g in range(5):
                dve.wait_ge(s_dev, g + 1)
                dve.reciprocal(mv[0:P, 5 * g:5 * g + 5, 2], mv[0:P, 5 * g:5 * g + 5, 2]).then_inc(s_rstd, 1)
                dve.wait_ge(s_rstd, g + 1)
                for b in range(5 * g, 5 * g + 5):
                    dve.tensor_scalar(h[0:P, b, :], xin[0:P, b, :], mv[0:P, b, 0:1], mv[0:P, b, 2:3], ALU.subtract, ALU.mult).then_inc(s_normed, 1)
            for k in range(6):
                dve.wait_ge(s_wT, k + 1)
                W = (WlT if k < 3 else WrT)[:, k % 3, :, :]
                dve.tensor_copy(W, B[6 + k % 2][:, :].rearrange("p (c o) -> p c o", c=KC)).then_inc(s_wT_out, 1)

            dve.memset(rm[:, :], -3.0e38).then_inc(s_q_softmax, 1)
            dve.sem_inc(s_ln1, 1)
            dve.wait_ge(s_mix_w, 5 * 16)
            for c in range(KC):
                dve.tensor_copy(wrr[:, c, :], wr[:, c:c + 1].broadcast_to((128, P))).then_inc(s_router_w, 1)

            def ln_stats(src, k, n):
                dve.bn_stats(lst[:, k, 0:6], src).then_inc(s_ln1, 1)
                dve.wait_ge(s_ln1, n + 1)
                dve.nop(nofuse=True)
                dve.bn_aggr(lst[:, k, 6:8], lst[:, k, 0:6]).then_inc(s_ln1, 1)
                return n + 2

            for L in LAYERS:
                if L == 1:
                    dve.wait_ge(s_kmaxT, 1)
                    dve.tensor_reduce(kmx[:, :], psA[:, 0:KC * P].rearrange("p (c n) -> p c n", c=KC), AX.X, ALU.max).then_inc(s_kmax, 1)
                    dve.wait_ge(s_kmax, 1)
                    for c in range(KC):
                        dve.tensor_scalar(dg[:, c, :], ident[:, :], kmx[:, c:c + 1], None, ALU.mult).then_inc(s_kmax, 1)
                    dve.wait_ge(s_kmax_rows, 1)
                    dve.tensor_copy(kmb[:, :], psA[0:P, 0:D]).then_inc(s_kmax, 1)
                    dve.wait_ge(s_kmax, 4)
                if L == 2:
                    dve.wait_ge(s_context, NB + 2)
                    dve.reciprocal(dn[:, :], psC[:, D:D + KC]).then_inc(s_ctx_w, 1)
                    dve.wait_ge(s_ctx_w, 1)
                    dve.tensor_scalar(dn[:, :], dn[:, :], 32.0 ** -0.5, None, ALU.mult).then_inc(s_ctx_w, 1)
                    dve.wait_ge(s_ctx_w, 2)
                    for c in range(KC):
                        dve.scalar_tensor_tensor(out=bd[:, c, :], in0=psC[:, c * 128:c * 128 + 128], scalar=dn[:, c:c + 1], in1=bdm[:, :], op0=ALU.mult, op1=ALU.mult).then_inc(s_ctx_w, 1)
                    dve.wait_ge(s_ctx_w_mm, 1)
                    dve.tensor_copy(bdT[:, :, :], psA[:, 0:256].rearrange("p (c n) -> p c n", c=KC)).then_inc(s_ctx_w, 1)
                    dve.wait_ge(s_ctx_w_mm, 2)
                    for c in range(KC):
                        dve.tensor_copy(Mx[:, c, :], B[4 + c][:, 0:D]).then_inc(s_ctx_w, 1)

                def one_hots(b, q):
                    for u in range(U):
                        dve.wait_ge(s_summed[L], (q + b) * (U - 1) + max(u, 1))
                        dve.tensor_scalar(oh[:, u, :], iota[:, ds(b * P, P)], dstf[:, ds(q % NG * U + u, 1)], None, ALU.is_equal).then_inc(s_onehot[L], 1)

                def mean(b):
                    g = L * NB + b
                    S = sums_of(L, b)
                    dve.wait_ge(s_sum, g + 1)
                    dve.tensor_scalar(rdeg[0:P, 0:1], S[:, D:D + 1], 1.0, None, ALU.max).then_inc(s_mean, 1)
                    dve.wait_ge(s_mean, g * 3 + 5)
                    dve.reciprocal(rdeg[0:P, 1:2], rdeg[0:P, 0:1]).then_inc(s_mean, 1)
                    dve.wait_ge(s_mean, g * 3 + 6)
                    dve.tensor_scalar(st[0:P, 1, :], S[:, 0:D], rdeg[0:P, 1:2], None, ALU.mult).then_inc(s_mean, 1)

                def follow(b):
                    if L == 0:
                        n = b * 6 + 1
                        heads = lambda t: t.rearrange("p (h e) -> p h e", h=8)
                        dve.wait_ge(s_qkv, b + 1)
                        dve.tensor_reduce(qst[:, 0, :], heads(psQK[0:P, 0:D]), AX.X, ALU.max).then_inc(s_q_softmax, 1)
                        dve.wait_ge(s_q_softmax, n + 1)
                        dve.tensor_tensor(heads(qsm[:, :]), heads(psQK[0:P, 0:D]), qst[:, 0, :].rearrange("p (h e) -> p h e", e=1).broadcast_to((P, 8, 32)), ALU.subtract).then_inc(s_q_softmax, 1)
                        dve.wait_ge(s_kv_out, b * 2 + 3)
                        dve.tensor_tensor(rm[:, :], rm[:, :], blk(k_all, b), ALU.max).then_inc(s_q_softmax, 1)

                    if L == 2:
                        n = b * 12 + 1
                        dve.wait_ge(s_mixed, b + 1)
                        n = ln_stats(rows_of(b)[:, D:2 * D], 0, n)
                        dve.wait_ge(s_ln1_dev, b * 2 + 1)
                        dve.reciprocal(lst[:, 0, 9:10], lst[:, 0, 8:9]).then_inc(s_ln1, 1)
                        dve.wait_ge(s_ln1, n + 1)
                        dve.tensor_scalar(ty[:, :], rows_of(b)[:, D:2 * D], lst[:, 0, 6:7], lst[:, 0, 9:10], ALU.subtract, ALU.mult).then_inc(s_ln1, 1)
                        dve.wait_ge(s_ln1, n + 2)
                        dve.tensor_tensor(ty[:, :], ty[:, :], gamma[:, :], ALU.mult).then_inc(s_ln1, 1)
                        dve.wait_ge(s_ln1, n + 3)
                        dve.wait_ge(s_x_rows, (b + 1) * 16)
                        dve.tensor_tensor(ty[:, :], ty[:, :], xs[:, :], ALU.add).then_inc(s_ln1, 1)
                        dve.wait_ge(s_ln1, n + 4)
                        dve.wait_ge(s_rows, L * NB + b + 1)
                        dve.tensor_tensor(x1s[:, :], ty[:, :], rows_of(b)[:, 0:D], ALU.add).then_inc(s_ln1, 1)
                        dve.wait_ge(s_ln1, n + 5)
                        n = ln_stats(x1s[:, :], 1, n + 5)
                        dve.wait_ge(s_ln1_dev, b * 2 + 2)
                        dve.reciprocal(lst[:, 1, 9:10], lst[:, 1, 8:9]).then_inc(s_ln1, 1)
                        dve.wait_ge(s_ln1, n + 1)
                        dve.wait_ge(s_ln1_T, b + 1)
                        dve.tensor_scalar(xls[:, :], x1s[:, :], lst[:, 1, 6:7], lst[:, 1, 9:10], ALU.subtract, ALU.mult).then_inc(s_ln1, 1)
                        dve.wait_ge(s_ln1, n + 2)
                        dve.tensor_tensor(blk(x1_all, b), x1s[:, :], xls[:, :], ALU.add).then_inc(s_ln1, 1)

                heads = lambda t: t.rearrange("p (h e) -> p h e", h=8)

                def follow_q(b):
                    n = b * 6 + 1
                    dve.wait_ge(s_q_exp, b + 1)
                    dve.tensor_reduce(qst[:, 1, :], heads(qsm[:, :]), AX.X, ALU.add).then_inc(s_q_softmax, 1)
                    dve.wait_ge(s_q_softmax, n + 4)
                    dve.reciprocal(qst[:, 2, :], qst[:, 1, :]).then_inc(s_q_softmax, 1)
                    dve.wait_ge(s_q_softmax, n + 5)
                    dve.tensor_tensor(heads(blk(q_all, b)), heads(qsm[:, :]), qst[:, 2, :].rearrange("p (h e) -> p h e", e=1).broadcast_to((P, 8, 32)), ALU.mult).then_inc(s_q_softmax, 1)

                def body(b, sums, rows_, after, later):
                    if sums:
                        q0, q1 = group_range(dve, b)
                        one_hots(b, q0)
                    if rows_:
                        mean(b - 1)
                        if L == 1:
                            dve.wait_ge(s_context, b)
                            dve.tensor_tensor(ek[:, :], blk(k_all, b - 1), kmb[:, :], ALU.subtract).then_inc(s_k_shifted, 1)
                    if after and L < 2:
                        follow(b - 2)
                    if sums:
                        with dve.If(q1 > q0 + 1):
                            with dve.Fori(q0 + 1, q1) as q:
                                one_hots(b, q)
                    if after and L == 0:
                        follow_q(b - 2)
                    if after and L == 2:
                        follow(b - 2)
                layer(dve, body)

            dve.wait_ge(s_router_out, NB)
            dve.wait_ge(s_consts, 18)
            dve.memset(A8, 0.0).then_inc(s_att_clear, 1)
            dve.memset(cnt[:, :, :], 0.0).then_inc(s_wcol, 1)
            for i in range(NB):
                dve.tensor_tensor_reduce(junk[:, P * i:P * i + P], wrow[:, P * i:P * i + P], ident[0:P, 0:P], 1.0, 0.0, ALU.mult, ALU.add, wcol[:, i:i + 1]).then_inc(s_wcol, 1)
            dve.wait_ge(s_wcol, NB + 1)
            for i in range(NB):
                lo, hi = P * i, P * i + P
                if i:
                    dve.wait_ge(s_rank, 4 * i - 1)
                    dve.tensor_scalar(junk[:, 0:lo], wrow[:, 0:lo], wcol[:, i:i + 1], 0.0, ALU.is_ge, ALU.add, accum_out=cnt[:, i, 0:1]).then_inc(s_rank, 1)
                if i < NB - 1:
                    dve.tensor_scalar(junk[:, hi:N], wrow[:, hi:N], wcol[:, i:i + 1], 0.0, ALU.is_gt, ALU.add, accum_out=cnt[:, i, 1:2]).then_inc(s_rank, 1)
                dve.scalar_tensor_tensor(out=junk[:, lo:hi], in0=wrow[:, lo:hi], scalar=wcol[:, i:i + 1], in1=tril[:, :], op0=ALU.is_ge, op1=ALU.mult, accum_out=cnt[:, i, 2:3]).then_inc(s_rank, 1)
                dve.scalar_tensor_tensor(out=junk2, in0=wrow[:, lo:hi], scalar=wcol[:, i:i + 1], in1=triu[:, :], op0=ALU.is_gt, op1=ALU.mult, accum_out=cnt[:, i, 3:4]).then_inc(s_rank, 1)
            nr = 4 * NB - 2
            dve.wait_ge(s_rank, nr)
            dve.tensor_reduce(sel[:, :], cnt[:, :, :], AX.X, ALU.add).then_inc(s_rank, 1)
            dve.wait_ge(s_rank, nr + 1)
            dve.tensor_scalar(sel[:, :], sel[:, :], float(CHOSEN), None, ALU.is_lt).then_inc(s_rank, 1)

            dve.wait_ge(s_prepT, 2)
            for k, (to, bank) in enumerate(((WgT, 0), (WqT, 2))):
                dve.tensor_copy(to, B[bank][:, :].rearrange("p (c o) -> p c o", c=KC)).then_inc(s_prep, 1)
            groups = lambda t, n: t.rearrange("p (g e) -> p g e", g=n)
            dve.wait_ge(s_biases, 12 * 16)
            for k, (t, mean, n) in enumerate(((Wkv.rearrange("p c d -> p (c d)"), cmean, 32), (bkv, bmean, 16))):
                dve.tensor_reduce(mean, groups(t, n), AX.X, ALU.add).then_inc(s_prep, 1)
                dve.wait_ge(s_prep, 3 + 3 * k)
                dve.tensor_scalar(mean, mean, 1.0 / 32, None, ALU.mult).then_inc(s_prep, 1)
                dve.wait_ge(s_prep, 4 + 3 * k)
                dve.tensor_tensor(groups(t, n), groups(t, n), mean.rearrange("p (g e) -> p g e", e=1).broadcast_to((t.shape[0], n, 32)), ALU.subtract).then_inc(s_prep, 1)
            dve.wait_ge(s_prepT, 3)
            dve.tensor_copy(Wg[:, :, D:D + 8], B[4][:, 0:16].rearrange("p (c h) -> p c h", c=KC)).then_inc(s_prep, 1)
            dve.tensor_copy(bqc, B[5][:, 0:KC]).then_inc(s_prep, 1)
            dve.wait_ge(s_scaled, NB + TB)
            dve.wait_ge(s_rank, 4 * NB)
            def rows_in(b):
                n = b * 6
                if not isinstance(b, int):
                    dve.wait_ge(s_ln2, n)
                dve.scalar_tensor_tensor(out=x1s[:, :], in0=blk(yw, b), scalar=sel[:, ds(b, 1)], in1=blk(x1_all, b), op0=ALU.mult, op1=ALU.add).then_inc(s_ln2, 1)
                dve.wait_ge(s_ln2, n + 1)
                dve.bn_stats(lst[:, 0, 0:6], x1s[:, :]).then_inc(s_ln2, 1)
                dve.wait_ge(s_ln2, n + 2)
                dve.nop(nofuse=True)
                dve.bn_aggr(lst[:, 0, 6:8], lst[:, 0, 0:6]).then_inc(s_ln2, 1)
                dve.wait_ge(s_ln2_dev, b + 1)
                dve.reciprocal(lst[:, 0, 9:10], lst[:, 0, 8:9]).then_inc(s_ln2, 1)
                dve.wait_ge(s_ln2, n + 4)
                dve.wait_ge(s_ln2_T, b + 1)
                dve.tensor_scalar(xls[:, :], x1s[:, :], lst[:, 0, 6:7], lst[:, 0, 9:10], ALU.subtract, ALU.mult).then_inc(s_ln2, 1)
                dve.wait_ge(s_ln2, n + 5)
                dve.tensor_tensor(blk(x1_all, b), x1s[:, :], xls[:, :], ALU.add).then_inc(s_ln2, 1)

            def normed(b):
                dve.wait_ge(s_kv_dev, b * 2 + 1)
                dve.tensor_reduce(ss[:, 0:16], groups(sq, 16), AX.X, ALU.add).then_inc(s_kv_normed, 1)
                dve.wait_ge(s_kv_dev, b * 2 + 2)
                dve.reciprocal(ss[:, 16:32], ss[:, 16:32]).then_inc(s_kv_normed, 1)
                dve.wait_ge(s_kv_normed, b * 3 + 6)
                dve.wait_ge(s_kv_added, b + 1)
                dve.tensor_tensor(groups(kvn, 16), groups(kv_of(b), 16), ss[:, 16:32].rearrange("p (g e) -> p g e", e=1).broadcast_to((P, 16, 32)), ALU.mult).then_inc(s_kv_normed, 1)
            rows_in(0)
            with dve.Fori(1, NB) as b:
                rows_in(b)
                normed(b - 1)
            normed(NB - 1)
            dve.wait_ge(s_kv_sum, 1)
            for c in range(KC):
                dve.scalar_tensor_tensor(out=bd[:, c, :], in0=psC[:, c * 128:c * 128 + 128], scalar=1.0 / N, in1=bdm[:, :], op0=ALU.mult, op1=ALU.mult).then_inc(s_fold, 1)
            dve.tensor_reduce(mx4, asd[:, :, 0:4].rearrange("p b h -> p h b"), AX.X, ALU.max).then_inc(s_fold, 1)
            dve.wait_ge(s_fold_mm, 1)
            dve.tensor_copy(WqpT, B[0][:, :].rearrange("p (c o) -> p c o", c=KC)).then_inc(s_fold, 1)
            dve.tensor_copy(bqp, B[5][:, 0:KC]).then_inc(s_fold, 1)
            dve.wait_ge(s_fold, 4)
            for c in range(KC):
                dve.tensor_tensor(WqpT[:, c, c * 128:c * 128 + 128], WqpT[:, c, c * 128:c * 128 + 128], ident[:, :], ALU.add).then_inc(s_fold, 1)
            dve.wait_ge(s_fold_mm, 2)
            dve.tensor_reduce(kx, B[7][0:4, 0:P], AX.X, ALU.max).then_inc(s_fold, 1)
            dve.wait_ge(s_fold, 8)
            dve.tensor_scalar(dg4, ident[0:4, 0:4], kx, None, ALU.mult).then_inc(s_fold, 1)
            dve.wait_ge(s_fold_mm, 3)
            dve.tensor_copy(Wpp, B[2][:, :].rearrange("p (c o) -> p c o", c=KC)).then_inc(s_fold, 1)
            dve.tensor_tensor(bpp, B[5][:, 4:4 + KC], b1m, ALU.add).then_inc(s_fold, 1)
            dve.wait_ge(s_fold_mm, 4)
            dve.tensor_copy(mx4, B[7][0:P, 128:132]).then_inc(s_fold, 1)
            dve.wait_ge(s_fold, 12)
            top = tab8[:, :, 4:8]
            dve.tensor_tensor(top, asd[:, :, 4:8], mx4.rearrange("p (b h) -> p b h", b=1).broadcast_to((P, NB, 4)), ALU.add).then_inc(s_fold, 1)
            dve.tensor_copy(tab8[:, :, 0:4], asd[:, :, 4:8]).then_inc(s_fold, 1)
            dve.tensor_tensor(wself, asd[:, :, 0:4], asd[:, :, 4:8], ALU.add).then_inc(s_fold, 1)
            dve.wait_ge(s_fold, 13)
            dve.scalar_tensor_tensor(out=top, in0=top, scalar=0.2, in1=top, op0=ALU.mult, op1=ALU.max).then_inc(s_fold, 1)
            dve.wait_ge(s_fold, 15)
            dve.scalar_tensor_tensor(out=wself, in0=wself, scalar=0.2, in1=wself, op0=ALU.mult, op1=ALU.max).then_inc(s_fold, 1)
            dve.wait_ge(s_fold, 17)
            dve.tensor_tensor(wself, wself, top, ALU.subtract).then_inc(s_fold, 1)
            dve.tensor_copy(identh[:, :], ident[:, :]).then_inc(s_fold, 1)
            for k in range(3):
                dve.tensor_copy(tabh[:, k, :, :], tab8 if k == 0 else tabr).then_inc(s_fold, 1)
                if k < 2:
                    dve.wait_ge(s_fold, 20 + 2 * k)
                    dve.tensor_tensor(tabr, tab8 if k == 0 else tabr, tabh[:, k, :, :], ALU.subtract).then_inc(s_fold, 1)
                    dve.wait_ge(s_fold, 21 + 2 * k)

            def mix(g, blocks):
                for k in range(blocks):
                    if k == 0:
                        dve.wait_ge(s_mix_out, g + 1)
                    dve.tensor_tensor(blk(x1_all, g * TB + k), blk(x1_all, g * TB + k), B[4 + k][0:P, 0:D], ALU.add).then_inc(s_mix_added, 1)
            with dve.Fori(0, NB // TB) as g:
                mix(g, TB)
            mix(NB // TB, NB % TB)

            dve.sem_inc(s_gat, 11)
            dve.wait_ge(s_self_w, 1)
            dve.wait_ge(s_mix_out, NB // TB + 1)

            def one_hot(to, b, q):
                return dve.tensor_tensor(to[:, :, :], iota[:, ds(b * P, P)].rearrange("p (u n) -> p u n", u=1).broadcast_to((128, U, P)),
                                         dstf[:, ds(q % NG * U, U)].rearrange("p (u n) -> p u n", n=1).broadcast_to((128, U, P)), ALU.is_equal)

            def one_hots_to_sum(b, q, lo, hi):
                for u in range(lo, hi):
                    dve.wait_ge(s_summed[3], (q + b) * U + u + 1)
                    dve.tensor_scalar(oh[:, u, :], iota[:, ds(b * P, P)], dstf[:, ds(q % NG * U + u, 1)], None, ALU.is_equal).then_inc(s_onehot[3], 1)

            def prepare(b, q):
                n = q + b
                if not (isinstance(n, int) and n == 0):
                    dve.wait_ge(s_onehotT, n)
                one_hot(ohA, b, q).then_inc(s_onehot_in, 1)

            def weights(b, q, nb, nq):
                n = q + b
                if nb is not None:
                    prepare(nb, nq)
                rows4 = ds(q % RG * U, U)
                w = wh[:, ds(n % 2 * U, U), :]
                X = PS[:, ds(4 + n % 2, 1), 0:8 * U].rearrange("p a (u h) -> p (a u) h", u=U)
                dve.wait_ge(s_landed[3], q * U + U)
                dve.wait_ge(s_spread, n + 1)
                dve.tensor_tensor(ez[:, :, :], X[:, :, 0:4], G[:, rows4, D:GW], ALU.add).then_inc(s_edge_w, 1)
                dve.wait_ge(s_edge_w, n * 5 + 1)
                dve.scalar_tensor_tensor(out=ez[:, :, :], in0=ez[:, :, :], scalar=0.2, in1=ez[:, :, :], op0=ALU.mult, op1=ALU.max).then_inc(s_edge_w, 1)
                dve.wait_ge(s_edge_w, n * 5 + 2)
                dve.tensor_tensor(ez[:, :, :], ez[:, :, :], X[:, :, 4:8], ALU.subtract).then_inc(s_edge_w, 1)
                dve.wait_ge(s_edge_w, n * 5 + 3)
                dve.tensor_scalar(ez[:, :, :], ez[:, :, :], 0.0, None, ALU.min).then_inc(s_edge_w, 1)
                one_hots_to_sum(b, q, 0, 2)
                dve.wait_ge(s_edge_exp, n + 2)
                dve.tensor_tensor(w[:, :, 0:D].rearrange("p u (h f) -> p u h f", h=4), G[:, rows4, 0:D].rearrange("p u (h f) -> p u h f", h=4),
                                  w[:, :, D:GW].rearrange("p u (h f) -> p u h f", f=1).broadcast_to((128, U, 4, 64)), ALU.mult).then_inc(s_edge_w, 1)
                one_hots_to_sum(b, q, 2, U)

            heads4 = lambda t: t.rearrange("p (h f) -> p h f", h=4)
            wide4 = lambda t: t.rearrange("p (h f) -> p h f", f=1).broadcast_to((P, 4, 64))

            def finish(b):
                n = b * 7 + 11
                dve.wait_ge(s_gat, n)
                ws = blk(wself, b)
                S = PS[0:P, ds(b % 2, 1), :].rearrange("p a n -> p (a n)")
                dve.wait_ge(s_own_in, (3 * NB + b + 1) * 16)
                dve.tensor_tensor(heads4(ty[:, :]), heads4(st[0:P, 0, :]), wide4(ws), ALU.mult).then_inc(s_gat, 1)
                dve.wait_ge(s_sum, 3 * NB + b + 1)
                dve.tensor_tensor(rs8[:, 0:4], S[:, D:GW], ws, ALU.add).then_inc(s_gat, 1)
                dve.wait_ge(s_gat, n + 2)
                dve.reciprocal(rs8[:, 4:8], rs8[:, 0:4]).then_inc(s_gat, 1)
                dve.tensor_tensor(ty[:, :], ty[:, :], S[:, 0:D], ALU.add).then_inc(s_gat, 1)
                dve.wait_ge(s_gat, n + 4)
                dve.tensor_tensor(heads4(ty[:, :]), heads4(ty[:, :]), wide4(rs8[:, 4:8]), ALU.mult).then_inc(s_gat, 1)
                dve.wait_ge(s_gat, n + 5)
                dve.tensor_tensor(ty[:, :], ty[:, :], gbias, ALU.add).then_inc(s_gat, 1)
                dve.wait_ge(s_gat, n + 6)
                dve.scalar_tensor_tensor(out=blk(x1_all, b), in0=ty[:, :], scalar=0.0, in1=blk(x1_all, b), op0=ALU.max, op1=ALU.add).then_inc(s_gat, 1)
                dve.wait_ge(s_gat, n + 7)
                dve.bn_stats(st6[0:P, ds(b, 1), :].rearrange("p a k -> p (a k)"), blk(x1_all, b)).then_inc(s_ln3, 1)

            prepare(0, 0)
            stream(dve, lambda b: None, weights, lambda b: None, finish)

            dve.wait_ge(s_ln3, NB)
            for b in range(NB):
                dve.bn_aggr(mv[0:P, b, 0:2], st6[0:P, b, :]).then_inc(s_ln3, 1)
            dve.wait_ge(s_ln3_dev, 1)
            dve.reciprocal(mv[0:P, :, 2], mv[0:P, :, 2]).then_inc(s_ln3, 1)
            dve.wait_ge(s_ln3, 2 * NB + 1)
            with dve.Fori(0, NB) as b:
                dve.wait_ge(s_ln3_T, b + 1)
                dve.tensor_scalar(xls[:, :], blk(x1_all, b), mv[0:P, ds(b, 1), 0:1].rearrange("p a k -> p (a k)"), mv[0:P, ds(b, 1), 2:3].rearrange("p a k -> p (a k)"), ALU.subtract, ALU.mult).then_inc(s_ln3, 1)
            wide = lambda t: t.broadcast_to((P, NB, 4))
            dve.wait_ge(s_gates_out, NB + 1)
            dve.tensor_reduce(g1, gl, AX.X, ALU.max).then_inc(s_top2, 1)
            dve.wait_ge(s_top2, 1)
            dve.tensor_tensor(gx, gl, wide(g1), ALU.subtract).then_inc(s_top2, 1)
            dve.wait_ge(s_top2_exp, 1)
            dve.tensor_reduce(g1, gx, AX.X, ALU.add).then_inc(s_top2, 1)
            dve.wait_ge(s_top2, 3)
            dve.reciprocal(g1, g1).then_inc(s_top2, 1)
            dve.wait_ge(s_top2, 4)
            dve.tensor_tensor(gx, gx, wide(g1), ALU.mult).then_inc(s_top2, 1)
            dve.memset(gr2, 0.0).then_inc(s_top2, 1)
            dve.wait_ge(s_top2, 6)
            n = 6
            for i in range(4):
                for j in range(4):
                    if i != j:
                        op = ALU.is_ge if j < i else ALU.is_gt
                        dve.tensor_tensor(ga[:, :, 0:1], gx[:, :, j:j + 1], gx[:, :, i:i + 1], op).then_inc(s_top2, 1)
                        dve.wait_ge(s_top2, n + 1)
                        dve.tensor_tensor(gr2[:, :, i:i + 1], gr2[:, :, i:i + 1], ga[:, :, 0:1], ALU.add).then_inc(s_top2, 1)
                        n += 2
                        dve.wait_ge(s_top2, n)
            dve.tensor_reduce(g1, gx, AX.X, ALU.max).then_inc(s_top2, 1)
            dve.wait_ge(s_top2, n + 1)
            dve.tensor_tensor(gp, gx, wide(g1), ALU.subtract).then_inc(s_top2, 1)
            dve.wait_ge(s_top2_exp, 2)
            dve.scalar_tensor_tensor(out=gp, in0=gr2, scalar=2.0, in1=gp, op0=ALU.is_lt, op1=ALU.mult).then_inc(s_top2, 1)
            dve.wait_ge(s_top2, n + 3)
            dve.tensor_reduce(g1, gp, AX.X, ALU.add).then_inc(s_top2, 1)
            dve.wait_ge(s_top2, n + 4)
            dve.reciprocal(g1, g1).then_inc(s_top2, 1)
            dve.wait_ge(s_top2, n + 5)
            dve.tensor_tensor(gp, gp, wide(g1), ALU.mult).then_inc(s_top2, 1)
            dve.wait_ge(s_top2, n + 6)

            with dve.Fori(0, NB) as b:
                x = blk(x1_all, b)
                dve.tensor_tensor(x, x, b3[:, 0:D], ALU.add).then_inc(s_last_bias, 1)
                for k in range(4):
                    dve.wait_ge(s_last_bias, b * 5 + k + 1)
                    dve.scalar_tensor_tensor(out=x, in0=b3[:, (k + 1) * D:(k + 2) * D], scalar=gp[:, ds(b, 1), k:k + 1].rearrange("p a h -> p (a h)"), in1=x, op0=ALU.mult, op1=ALU.add).then_inc(s_last_bias, 1)
                dve.wait_ge(s_last_bias, b * 5 + 5)
                bank = lambda e: PS[0:P, ds(2 + b % 2 * 3 + e, 1), :].rearrange("p a n -> p (a n)")
                dve.wait_ge(s_expert_rows, b + 1)
                dve.tensor_tensor(x, x, bank(2)[:, 0:D], ALU.add).then_inc(s_added, 1)
                for k in range(4):
                    dve.wait_ge(s_added, b * 5 + k + 7)
                    dve.scalar_tensor_tensor(out=x, in0=bank(k // 2)[:, k % 2 * D:k % 2 * D + D], scalar=gp[:, ds(b, 1), k:k + 1].rearrange("p a h -> p (a h)"), in1=x, op0=ALU.mult, op1=ALU.add).then_inc(s_added, 1)

        @block.scalar
        def _(act):
            for g in range(5):
                act.wait_ge(s_moments, 5 * g + 5)
                act.wait_ge(s_consts, 7)
                act.activation(mv[0:P, 5 * g:5 * g + 5, 2], mv[0:P, 5 * g:5 * g + 5, 1], ACT.Sqrt, bias=eps[0:P, :]).then_inc(s_dev, 1)
            for L in LAYERS:
                if L == 0:
                    act.sem_inc(s_out_free, 1)
                    act.sem_inc(s_relu, 1)
                    act.sem_inc(s_kv_out, 2)
                if L == 2:
                    act.sem_inc(s_qT_out, 1)
                if L != 1:
                    act.activation(actw[:, :], eps[0:P, :], ACT.Exp if L == 0 else ACT.Sqrt).then_inc(s_act_table, 1)
                def body(b, sums, rows_, after, later):
                    if rows_:
                        t = b - 1
                        if L == 2:
                            act.wait_ge(s_qT_out, t + 1)
                            act.activation(qsm[:, :], blk(q_all, t), ACT.Copy).then_inc(s_q_rows, 1)
                        if L == 1:
                            act.wait_ge(s_k_shifted, t + 1)
                            act.activation(ek[:, :], ek[:, :], ACT.Exp).then_inc(s_k_exp, 1)
                        act.wait_ge(s_meanT, L * NB + t + 1)
                        act.activation(rT[:, :, 0:KC * P], psHM[:, :].rearrange("p (a n) -> p a n", a=2)[:, :, 0:KC * P], ACT.Copy).then_inc(s_features, 1)
                        if L == 2:
                            act.wait_ge(s_qT, t + 1)
                            act.activation(qT[:, :], psV[:, 0:KC * P], ACT.Copy).then_inc(s_qT_out, 1)
                    if later and L == 2:
                        t = b - 3
                        act.wait_ge(s_ln1_T, t + 2)
                        act.activation(xlT[:, :, ds(t * P, P)], psA[:, 0:KC * P].rearrange("p (c n) -> p c n", c=KC), ACT.Copy).then_inc(s_ln1_T_out, 1)
                        act.wait_ge(s_router, t + 1)
                        act.activation(wrow[:, ds(t * P, P)], psC[0:P, 0:P], ACT.Identity, bias=br[:, :]).then_inc(s_router_out, 1)
                    if after:
                        t = b - 2
                        if L == 0:
                            act.wait_ge(s_q_softmax, t * 6 + 3)
                            act.activation(qsm[:, :], qsm[:, :], ACT.Exp).then_inc(s_q_exp, 1)
                        if L == 2:
                            for k in range(2):
                                act.wait_ge(s_ln1, t * 12 + 3 + 7 * k)
                                act.activation(lst[:, k, 8:9], lst[:, k, 7:8], ACT.Sqrt, bias=eps[0:P, :]).then_inc(s_ln1_dev, 1)
                    if rows_:
                        t = b - 1
                        if L < 2:
                            act.wait_ge(s_rows, L * NB + t + 1)
                            act.wait_ge(s_out_free, L * NB + t + 1)
                            act.activation(ho[0:P, :], psO[0:P, 0:D], ACT.Relu).then_inc(s_relu, 1)
                        if L == 0:
                            act.wait_ge(s_qkv, t + 1)
                            act.activation(blk(k_all, t), psV[0:P, 0:D], ACT.Copy).then_inc(s_kv_out, 1)
                            act.activation(blk(v_all, t), psV[0:P, D:2 * D], ACT.Copy).then_inc(s_kv_out, 1)
                layer(act, body)

            act.sem_inc(s_gelu, 4)
            act.sem_inc(s_scaled, TB)
            act.wait_ge(s_ffn_w, 4 * 16)
            act.wait_ge(s_gathers_done, 3)

            def ffn(g, blocks):
                for m in range(HC):
                    act.wait_ge(s_inner, g * HC + m + 1)
                    act.activation(hT[:, m, 0:blocks * P], B[m % 4][:, 0:blocks * P], ACT.Gelu_apprx_tanh, bias=b1c[:, m:m + 1]).then_inc(s_gelu, 1)
                act.wait_ge(s_wcol, NB + 1)
                act.wait_ge(s_outer, g + 1)
                for k in range(blocks):
                    act.activation(blk(yw, g * TB + k), B[4 + k][0:P, 0:D], ACT.Identity, scale=wcol[:, ds(g * TB + k, 1)]).then_inc(s_scaled, 1)
            with act.Fori(0, NB // TB) as g:
                ffn(g, TB)
            ffn(NB // TB, NB % TB)

            xT = lambda b: xlT[:, :, ds(b * P, P)]
            two = lambda t: t[:, 0:KC * P].rearrange("p (c n) -> p c n", c=KC)
            act.wait_ge(s_biases, 12 * 16)
            def rows_in(b):
                act.wait_ge(s_ln2, b * 6 + 3)
                act.activation(lst[:, 0, 8:9], lst[:, 0, 7:8], ACT.Sqrt, bias=eps[0:P, :]).then_inc(s_ln2_dev, 1)
                act.wait_ge(s_ln2_T, b + 2)
                act.activation(rT[:, 0, 0:KC * P], psH[:, 0:KC * P], ACT.Copy).then_inc(s_ln2_T_out, 1)
                act.activation(xT(b), two(psH), ACT.Copy).then_inc(s_ln2_T_out, 1)

            def normed(b):
                act.wait_ge(s_proj, b * 2 + 2)
                act.activation(sq, kv_of(b), ACT.Square).then_inc(s_kv_dev, 1)
                act.wait_ge(s_kv_normed, b * 3 + 5)
                act.activation(ss[:, 16:32], ss[:, 0:16], ACT.Sqrt, scale=1.0 / 32, bias=eps[0:P, :]).then_inc(s_kv_dev, 1)

            def table_rows(b):
                act.wait_ge(s_proj, b * 2 + 1)
                act.wait_ge(s_out_free, 2 * NB + b + 1)
                act.activation(hs, psO[0:P, 0:D + 8], ACT.Copy).then_inc(s_table_row, 1)
                act.activation(blk(asd, b), psO[0:P, D:D + 8], ACT.Copy).then_inc(s_att_out, 1)
            act.activation(actw[:, :], eps[0:P, :], ACT.Sqrt).then_inc(s_ln2_T_out, 1)
            rows_in(0)
            table_rows(0)
            with act.Fori(1, NB) as b:
                rows_in(b)
                normed(b - 1)
                table_rows(b)
            normed(NB - 1)
            act.wait_ge(s_fold, 18)
            act.activation(wself, wself, ACT.Exp).then_inc(s_self_w, 1)

            def mix(g, blocks):
                for m in range(KC):
                    act.wait_ge(s_mix_in, g * KC + m + 1)
                    act.activation(gT[:, m, 0:blocks * P], B[m][:, 0:blocks * P], ACT.Gelu, bias=bpp[:, m:m + 1]).then_inc(s_mix_gelu, 1)
            with act.Fori(0, NB // TB) as g:
                mix(g, TB)
            mix(NB // TB, NB % TB)

            def prepare(b, q):
                act.wait_ge(s_onehotT, q + b + 1)
                act.activation(ohT[:, :], psT[0:P, :], ACT.Copy).then_inc(s_onehotT_out, 1)

            def weights(b, q, nb, nq):
                n = q + b
                act.wait_ge(s_edge_w, n * 5 + 4)
                act.activation(wh[:, ds(n % 2 * U, U), D:GW], ez[:, :, :], ACT.Exp).then_inc(s_edge_exp, 1)
                if nb is not None:
                    prepare(nb, nq)
                if nb is b:
                    act.wait_ge(s_edge_w, n * 5 + 5)
                    act.sem_inc(s_free[3], 1)
            act.activation(actw[:, :], eps[0:P, :], ACT.Exp).then_inc(s_edge_exp, 1)
            prepare(0, 0)
            stream(act, lambda b: None, weights, lambda b: None)

            act.wait_ge(s_ln3, 2 * NB)
            act.activation(mv[0:P, :, 2], mv[0:P, :, 1], ACT.Sqrt, bias=eps[0:P, :]).then_inc(s_ln3_dev, 1)

            def turned(b):
                act.wait_ge(s_ln3_T, b + 2)
                act.wait_ge(s_gates, b + 1)
                act.activation(rT[:, 0, 0:KC * P], psH[:, 0:KC * P], ACT.Copy).then_inc(s_ln3_T_out, 1)
                act.activation(xT(b), two(psH), ACT.Copy).then_inc(s_ln3_T_out, 1)

            def gates(b):
                act.wait_ge(s_gates, b + 2)
                act.activation(blk(gl, b), psO[0:P, 0:4], ACT.Copy).then_inc(s_gates_out, 1)
            turned(0)
            with act.Fori(1, NB) as b:
                turned(b)
                gates(b - 1)
            gates(NB - 1)
            for k, (t, n) in enumerate(((gx, 2), (gp, 32))):
                act.wait_ge(s_top2, n)
                act.activation(t, t, ACT.Exp).then_inc(s_top2_exp, 1)
            act.sem_inc(s_experts_out, 2)

            def experts(g, blocks):
                n = blocks * P
                bias = [sb1[:, 0:1], sb1[:, 1:2]] + [eb1[:, k:k + 1] for k in range(4)] + [sb2[:, 0:1]] + [eb2[0:64, k:k + 1] for k in range(4)]
                for k in range(11):
                    rows_ = 64 if k >= 7 else 128
                    act.wait_ge(s_experts, g * 11 + k + 1)
                    act.activation(ffh[k][0:rows_, 0:n], B[k % 2][0:rows_, 0:n], ACT.Relu, bias=bias[k]).then_inc(s_experts_out, 1)
            with act.Fori(0, NB // TB) as g:
                experts(g, TB)
            experts(NB // TB, NB % TB)

        @block.tensor
        def _(pe):
            pe.wait_ge(s_consts, 14)
            pe.wait_ge(s_edge_rows, 1)
            for c in range(4):
                for a in range(2):
                    k = 2 * c + a
                    if k >= 4:
                        pe.wait_ge(s_edgeT_out, k - 3)
                    pe.transpose(B[k % 4][:, 0:chunk_rows[c]], rows[0:chunk_rows[c], a, c, :], ident[0:chunk_rows[c], 0:chunk_rows[c]]).then_inc(s_edgeT, 1)
            pe.wait_ge(s_tile_ends, 8)
            for q in range(2):
                for c in range(4):
                    pe.transpose(B[4 + q][0:1, 128 * c:128 * c + 128], red[:, 8 + 4 * q + c:9 + 4 * q + c], ident[:, :]).then_inc(s_tile_endsT, 1)
            pe.wait_ge(s_sage_w, 9 * 16)
            for k in range(6):
                if k >= 2:
                    pe.wait_ge(s_wT_out, k - 1)
                for cd in range(KC):
                    for co in range(KC):
                        last = pe.transpose(B[6 + k % 2][:, cd * D + co * 128:cd * D + co * 128 + 128], wst[:, k, co, cd * 128:cd * 128 + 128], ident[:, :])
                last.then_inc(s_wT, 1)
            pe.wait_ge(s_wT_out, 6)
            pe.wait_ge(s_runs, 2)
            for L in LAYERS:
                pe.sem_inc(s_summed[L], U - 1)
                pe.sem_inc(s_free[L], RG)
                if L == 0:
                    pe.sem_inc(s_ownT, 1)
                    pe.sem_inc(s_mean, 4)
                    pe.wait_ge(s_mix_w, 5 * 16)
                if L == 1:
                    pe.wait_ge(s_q_softmax, 6 * NB + 1)
                    for c in range(KC):
                        m = pe.transpose(psA[:, c * P:c * P + P], rm[:, c * 128:c * 128 + 128], ident[0:P, 0:P])
                    m.then_inc(s_kmaxT, 1)
                    pe.wait_ge(s_kmax, 3)
                    pe.matmul(psA[0:P, 0:D], ones128[:, :], dg[:, :, :].rearrange("p c n -> p (c n)"), start=True, stop=True).then_inc(s_kmax_rows, 1)
                    pe.matmul(psC[:, 0:D + KC], zrow[:, 0:128], zrow[:, 0:D + KC], start=True, stop=False, skip_group_check=True)
                if L == 2:
                    pe.matmul(psC[:, 0:D + KC], zrow[:, 0:128], zrow[:, 0:D + KC], start=False, stop=True, skip_group_check=True).then_inc(s_context, 1)
                    pe.wait_ge(s_ctx_w, 4)
                    for c in range(KC):
                        m = pe.transpose(psA[:, c * 128:c * 128 + 128], bd[:, c, :], ident[:, :])
                    m.then_inc(s_ctx_w_mm, 1)
                    pe.wait_ge(s_ctx_w, 5)
                    for c in range(KC):
                        m = pe.matmul(B[4 + c][:, 0:D], bdT[:, c, :], Wout[:, c, :], start=True, stop=True)
                    m.then_inc(s_ctx_w_mm, 1)

                def add(b, q, first):
                    for u in range(U):
                        pe.wait_ge(s_landed[L], q * U + u + 1)
                        pe.wait_ge(s_onehot[L], (q + b) * U + u + 1)
                        m = pe.matmul(sums_of(L, b), oh[:, u, :], G[:, ring(q, u), 0:D + 1].rearrange("p a d -> p (a d)"),
                                      start=first and u == 0, stop=False, skip_group_check=True)
                        if u:
                            m.then_inc(s_summed[L], 1)
                        elif not first:
                            m.then_inc(s_free[L], 1)

                def to_features(to, src, signal):
                    for c in range(KC):
                        m = pe.transpose(to[:, c * P:c * P + P], src[:, c * 128:c * 128 + 128], ident[0:P, 0:P])
                    m.then_inc(signal, 1)

                def body(b, sums, rows_, after, later):
                    if sums:
                        q0, q1 = group_range(pe, b)
                        pe.wait_ge(s_mean, (L * NB + b) * 3 + 1)
                        add(b, q0, True)
                    if rows_:
                        g = L * NB + b - 1
                        pe.wait_ge(s_own_in, (g + 1) * 16)
                        to_features(psHM[:, 0:D], st[0:P, 0, :], s_ownT)
                        pe.wait_ge(s_mean, g * 3 + 7)
                        to_features(psHM[:, D:2 * D], st[0:P, 1, :], s_meanT)
                        if L == 2:
                            pe.wait_ge(s_q_rows, b)
                            to_features(psV, qsm, s_qT)
                    if later and L == 2:
                        pe.wait_ge(s_ln1, (b - 3) * 12 + 13)
                        to_features(psA, xls, s_ln1_T)
                        pe.wait_ge(s_ln1_T_out, b - 2)
                        for c in range(KC):
                            m = pe.matmul(psC[0:P, 0:P], wrr[:, c, :], xlT[:, c, ds((b - 3) * P, P)], start=(c == 0), stop=(c == KC - 1))
                        m.then_inc(s_router, 1)
                    if sums:
                        with pe.If(q1 > q0 + 1):
                            with pe.Fori(q0 + 1, q1) as q:
                                add(b, q, False)
                        pe.matmul(sums_of(L, b), zrow[:, 0:P], zrow[:, 0:D + 1], start=False, stop=True, skip_group_check=True).then_inc(s_sum, 1)
                    if rows_:
                        t = b - 1
                        pe.wait_ge(s_features, g + 1)
                        if L < 2:
                            pe.wait_ge(s_relu, g + 1)
                        elif not (isinstance(b, int) and b < 3):
                            pe.wait_ge(s_ln1, (b - 2) * 12 + 1)
                        O = psO[0:P, 0:D] if L < 2 else rows_of(t)[:, 0:D]
                        for c in range(KC):
                            pe.matmul(O, rT[:, 0, c * P:c * P + P], WrT[:, L, c, :], start=(c == 0), stop=False)
                        pe.matmul(O, ones[:, :], bl[:, L, :], start=False, stop=False)
                        for c in range(KC):
                            m = pe.matmul(O, rT[:, 1, c * P:c * P + P], WlT[:, L, c, :], start=False, stop=(c == KC - 1))
                        m.then_inc(s_rows, 1)
                        if L == 0:
                            if not (isinstance(b, int) and b < 2):
                                pe.wait_ge(s_q_softmax, (b - 2) * 6 + 3)
                            pe.wait_ge(s_kv_out, t * 2 + 2)
                            for c in range(KC):
                                pe.matmul(psQK[0:P, 0:D], rT[:, 0, c * P:c * P + P], Wqkv[:, c, 0:D], start=(c == 0), stop=(c == KC - 1))
                            for c in range(KC):
                                m = pe.matmul(psV[0:P, :], rT[:, 0, c * P:c * P + P], Wqkv[:, c, D:3 * D], start=(c == 0), stop=(c == KC - 1))
                            m.then_inc(s_qkv, 1)
                        if L == 1:
                            pe.wait_ge(s_k_exp, t + 1)
                            for c in range(KC):
                                pe.matmul(psC[:, c * 128:c * 128 + 128], ek[:, c * 128:c * 128 + 128], v_all[:, ds(t, 1), c * 128:c * 128 + 128].rearrange("p a d -> p (a d)"),
                                          start=False, stop=False, skip_group_check=True)
                            for c in range(KC):
                                m = pe.matmul(psC[:, D + c:D + c + 1], ek[:, c * 128:c * 128 + 128], ones128[0:P, 0:1], start=False, stop=False, skip_group_check=True)
                            m.then_inc(s_context, 1)
                        if L == 2:
                            pe.wait_ge(s_qT_out, t + 2)
                            for c in range(KC):
                                m = pe.matmul(rows_of(t)[:, D:2 * D], qT[:, c * P:c * P + P], Mx[:, c, :], start=(c == 0), stop=(c == KC - 1))
                            m.then_inc(s_mixed, 1)
                if L == 1:
                    pe.sem_inc(s_context, 1)
                if L == 2:
                    pe.sem_inc(s_ln1_T, 1)
                    pe.wait_ge(s_ctx_w, 7)
                layer(pe, body)

            pe.wait_ge(s_ffn_w, 4 * 16)
            pe.wait_ge(s_router_out, NB)

            def ffn(g, blocks):
                n = blocks * P
                for m in range(HC):
                    pe.wait_ge(s_gelu, g * HC + m + 1)
                    for c in range(KC):
                        x = pe.matmul(B[m % 4][:, 0:n], w1[:, c, m * 128:m * 128 + 128], xlT[:, c, ds(g * TOK, n)], start=(c == 0), stop=(c == KC - 1))
                    x.then_inc(s_inner, 1)
                for k in range(blocks):
                    pe.wait_ge(s_scaled, g * TB + k + 1)
                    pe.matmul(B[4 + k][0:P, 0:D], ones[:, :], b2r[:, :], start=True, stop=False)
                for m in range(HC):
                    pe.wait_ge(s_gelu, g * HC + m + 5)
                    for k in range(blocks):
                        x = pe.matmul(B[4 + k][0:P, 0:D], hT[:, m, k * P:k * P + P], w2[:, m, :], start=False, stop=(m == HC - 1))
                x.then_inc(s_outer, 1)
            with pe.Fori(0, NB // TB) as g:
                ffn(g, TB)
            ffn(NB // TB, NB % TB)

            pe.wait_ge(s_scaled, NB + TB)
            pe.wait_ge(s_gat_w, 18 * 16)
            for k, (w, bank) in enumerate(((Wg, 0), (Wq, 2))):
                for i in range(KC):
                    for j in range(KC):
                        m = pe.transpose(B[bank][:, j * D + i * 128:j * D + i * 128 + 128], w[:, i, j * 128:j * 128 + 128], ident[:, :])
                m.then_inc(s_prepT, 1)
            pe.wait_ge(s_prep, 1)
            pe.wait_ge(s_biases, 12 * 16)
            for i in range(KC):
                for j in range(KC):
                    pe.matmul(B[4][:, i * 8:i * 8 + 8], WgT[:, j, i * 128:i * 128 + 128], A8[:, j, :], start=(j == 0), stop=(j == KC - 1))
            for c in range(KC):
                m = pe.matmul(B[5][:, c:c + 1], bq[:, c * 128:c * 128 + 128], ones[:, 0:1], start=True, stop=True)
            m.then_inc(s_prepT, 1)
            pe.wait_ge(s_prep, 10)
            pe.sem_inc(s_att_out, 1)
            pe.sem_inc(s_kv_added, 1)
            pe.matmul(psC[:, 0:D], zrow[:, 0:128], zrow[:, 0:D], start=True, stop=False, skip_group_check=True)
            pe.sem_inc(s_ln2_T, 1)
            pe.sem_inc(s_kv_normed, 4)

            def rows_in(b):
                pe.wait_ge(s_ln2, b * 6 + 5)
                for c in range(KC):
                    m = pe.transpose(psH[:, c * P:c * P + P], xls[:, c * 128:c * 128 + 128], ident[0:P, 0:P])
                m.then_inc(s_ln2_T, 1)

            def project(b):
                pe.wait_ge(s_ln2_T_out, b * 2 + 3)
                pe.wait_ge(s_att_out, b + 1)
                for c in range(KC):
                    m = pe.matmul(psO[0:P, 0:D + 8], rT[:, 0, c * P:c * P + P], Wg[:, c, :], start=(c == 0), stop=(c == KC - 1))
                m.then_inc(s_proj, 1)
                pe.wait_ge(s_kv_normed, b * 3 + 1)
                for c in range(KC):
                    pe.matmul(kv_of(b), rT[:, 0, c * P:c * P + P], Wkv[:, c, :], start=(c == 0), stop=False)
                pe.matmul(kv_of(b), ones[:, :], bkv, start=False, stop=True).then_inc(s_proj, 1)

            def kv_sum(b):
                pe.wait_ge(s_kv_affine, b * 2 + 2)
                for c in range(KC):
                    m = pe.matmul(psC[:, c * 128:c * 128 + 128], kvn[:, c * 128:c * 128 + 128], kvn[:, D + c * 128:D + c * 128 + 128], start=False, stop=False, skip_group_check=True)
                m.then_inc(s_kv_added, 1)
            for b in range(2):
                rows_in(b)
                project(b)
            with pe.Fori(2, NB) as b:
                rows_in(b)
                kv_sum(b - 2)
                project(b)
            kv_sum(NB - 2)
            kv_sum(NB - 1)
            pe.matmul(psC[:, 0:D], zrow[:, 0:128], zrow[:, 0:D], start=False, stop=True, skip_group_check=True).then_inc(s_kv_sum, 1)
            pe.sem_inc(s_free[3], RG)
            pe.wait_ge(s_fold, 2)
            for c in range(KC):
                pe.matmul(B[0][:, c * D:c * D + D], bd[:, c, :], WqT[:, c, :], start=True, stop=True)
                m = pe.matmul(B[5][:, c:c + 1], bd[:, c, :], bqc[:, c:c + 1], start=True, stop=True)
            m.then_inc(s_fold_mm, 1)
            pe.wait_ge(s_fold, 3)
            pe.transpose(B[7][0:4, 0:P], mx4, ident[0:P, 0:P]).then_inc(s_fold_mm, 1)
            pe.wait_ge(s_fold, 7)
            for i in range(KC):
                for j in range(KC):
                    pe.matmul(B[2][:, i * D:i * D + D], WqpT[:, j, i * 128:i * 128 + 128], m1[:, j, :], start=(j == 0), stop=(j == KC - 1))
                for j in range(KC):
                    m = pe.matmul(B[5][:, 4 + i:5 + i], m1[:, j, i * 128:i * 128 + 128], bqp[:, j:j + 1], start=(j == 0), stop=(j == KC - 1))
            m.then_inc(s_fold_mm, 1)
            pe.wait_ge(s_fold, 9)
            pe.matmul(B[7][0:P, 128:132], ones128[0:4, 0:P], dg4, start=True, stop=True).then_inc(s_fold_mm, 1)

            pe.wait_ge(s_fold, 11)
            pe.sem_inc(s_mix_gelu, 2)
            pe.sem_inc(s_mix_added, TB)

            def mix(g, blocks):
                n = blocks * P
                for m in range(KC):
                    pe.wait_ge(s_mix_gelu, g * KC + m + 1)
                    for c in range(KC):
                        x = pe.matmul(B[m][:, 0:n], Wpp[:, c, m * 128:m * 128 + 128], xlT[:, c, ds(g * TOK, n)], start=(c == 0), stop=(c == KC - 1))
                    x.then_inc(s_mix_in, 1)
                pe.wait_ge(s_mix_gelu, g * KC + 4)
                for k in range(blocks):
                    pe.wait_ge(s_mix_added, g * TB + k + 1)
                    pe.matmul(B[4 + k][0:P, 0:D], ones[:, :], b2m, start=True, stop=False)
                    for m in range(KC):
                        x = pe.matmul(B[4 + k][0:P, 0:D], gT[:, m, k * P:k * P + P], m2[:, m, :], start=False, stop=(m == KC - 1))
                x.then_inc(s_mix_out, 1)
            with pe.Fori(0, NB // TB) as g:
                mix(g, TB)
            mix(NB // TB, NB % TB)

            pe.sem_inc(s_summed[3], U)

            def prepare(b, q):
                n = q + b
                pe.wait_ge(s_onehot_in, n + 1)
                for u in range(U):
                    m = pe.transpose(psT[0:P, u * ET:u * ET + ET], ohA[:, u, :], identh[:, :])
                m.then_inc(s_onehotT, 1)

            def spread(b, q):
                n = q + b
                pe.wait_ge(s_onehotT_out, n + 1)
                for u in range(U):
                    for k in range(3):
                        m = pe.matmul(PS[:, ds(4 + n % 2, 1), 8 * u:8 * u + 8].rearrange("p a h -> p (a h)"),
                                      ohT[:, u * ET:u * ET + ET], tabh[:, k, ds(b, 1), :].rearrange("p a h -> p (a h)"), start=(k == 0), stop=(k == 2))
                m.then_inc(s_spread, 1)

            def edges(b, q, nb, nq):
                n = q + b
                S = PS[0:P, ds(b % 2, 1), 0:GW].rearrange("p a n -> p (a n)")
                if nb is not None:
                    prepare(nb, nq)
                    spread(nb, nq)
                pe.wait_ge(s_edge_w, n * 5 + 5)
                for u in range(U):
                    pe.wait_ge(s_onehot[3], n * U + u + 1)
                    pe.matmul(S, oh[:, u, :], wh[:, ds(n % 2 * U + u, 1), :].rearrange("p a d -> p (a d)"), start=False, stop=False, skip_group_check=True).then_inc(s_summed[3], 1)

            def begin(b):
                pe.wait_ge(s_gat, b * 7 + 1)
                pe.matmul(PS[0:P, ds(b % 2, 1), 0:GW].rearrange("p a n -> p (a n)"), zrow[:, 0:P], zrow[:, 0:GW], start=True, stop=False, skip_group_check=True)

            def end(b):
                pe.matmul(PS[0:P, ds(b % 2, 1), 0:GW].rearrange("p a n -> p (a n)"), zrow[:, 0:P], zrow[:, 0:GW], start=False, stop=True, skip_group_check=True).then_inc(s_sum, 1)
            pe.wait_ge(s_fold, 24)
            prepare(0, 0)
            spread(0, 0)
            stream(pe, begin, edges, end)

            pe.wait_ge(s_moe_w, 14 * 16)
            pe.sem_inc(s_ln3_T, 1)
            pe.sem_inc(s_gates_out, 1)
            pe.sem_inc(s_gates, 1)
            pe.sem_inc(s_ln3_T_out, 3)

            def turned(b):
                pe.wait_ge(s_ln3, 2 * NB + 2 + b)
                pe.wait_ge(s_ln3_T_out, b * 2 + 3)
                for c in range(KC):
                    m = pe.transpose(psH[:, c * P:c * P + P], xls[:, c * 128:c * 128 + 128], ident[0:P, 0:P])
                m.then_inc(s_ln3_T, 1)

            def gates(b):
                pe.wait_ge(s_ln3_T_out, b * 2 + 4)
                pe.wait_ge(s_gates_out, b + 1)
                for c in range(KC):
                    pe.matmul(psO[0:P, 0:4], rT[:, 0, c * P:c * P + P], gW[:, c, :], start=(c == 0), stop=False)
                pe.matmul(psO[0:P, 0:4], ones[:, :], gbr, start=False, stop=True).then_inc(s_gates, 1)
            turned(0)
            with pe.Fori(1, NB) as b:
                turned(b)
                gates(b - 1)
            gates(NB - 1)

            pe.wait_ge(s_gates_out, NB + 1)
            pe.sem_inc(s_added, 6)

            def experts(g, blocks):
                n = blocks * P
                for k in range(11):
                    to = B[k % 2]
                    pe.wait_ge(s_experts_out, g * 11 + k + (k > 1) + (k < 2) * (2 - k))
                    if k < 6:
                        for c in range(KC):
                            w = sW1[:, c, k * 128:k * 128 + 128] if k < 2 else eW1[:, k - 2, c, :]
                            m = pe.matmul(to[:, 0:n], w, xlT[:, c, ds(g * TOK, n)], start=(c == 0), stop=(c == KC - 1))
                    elif k == 6:
                        for c in range(KC):
                            m = pe.matmul(to[:, 0:n], sW2[:, c, :], ffh[c][:, 0:n], start=(c == 0), stop=(c == KC - 1))
                    else:
                        m = pe.matmul(to[0:64, 0:n], eW2[:, k - 7, :], ffh[k - 5][:, 0:n], start=True, stop=True)
                    m.then_inc(s_experts, 1)
                pe.wait_ge(s_experts_out, g * 11 + 13)
                for k in range(blocks):
                    pe.wait_ge(s_added, (g * TB + k) * 5 + 1)
                    bank = 2 + k % 2 * 3
                    for e in range(4):
                        pe.matmul(B[bank + e // 2][0:P, e % 2 * D:e % 2 * D + D], ffh[7 + e][0:64, k * P:k * P + P], eW3[0:64, e, :], start=True, stop=True)
                    pe.matmul(B[bank + 2][0:P, 0:D], ffh[6][:, k * P:k * P + P], sW3[:, 0, :], start=True, stop=True).then_inc(s_expert_rows, 1)
            with pe.Fori(0, NB // TB) as g:
                experts(g, TB)
            experts(NB // TB, NB % TB)


_INS = (["x", "src", "dst"] + [f"L0_gnn_{n}" for k in (1, 2, 3) for n in (f"W{k}l", f"b{k}l", f"W{k}r")]
        + [f"L0_mix_{n}" for n in "Wqkv Wout gamma".split()] + [f"L0_ffn_{n}" for n in "wr br w1 b1 w2 b2".split()]
        + [f"L1_gnn_{n}" for n in "W att_src att_dst bias".split()]
        + [f"L1_mix_{n}" for n in "w_qkv b_qkv kln_g kln_b vln_g vln_b w1 b1 w2 b2".split()]
        + [f"L1_ffn_{n}" for n in "sW1 sb1 sW2 sb2 sW3 sb3 eW1 eb1 eW2 eb2 eW3 eb3 gW gb".split()])


def kernel(**inputs):
    import numpy as _np
    import concourse.bacc as _bacc
    from concourse import mybir as _mybir
    from concourse.bass_utils import run_bass_kernel_spmd as _run
    nc = _bacc.Bacc("TRN2", target_bir_lowering=False, num_devices=1)
    arrays, args = {}, {}
    for name in _INS:
        a = _np.ascontiguousarray(inputs[name])
        arrays[f"in_{name}_dram"] = a
        args[name] = nc.dram_tensor(f"in_{name}_dram", a.shape, _mybir.dt.from_np(a.dtype), kind="ExternalInput").ap()
    out = nc.dram_tensor("out_0_dram", (N, D), F32, kind="ExternalOutput").ap()
    build(nc, args, out)
    r = _run(nc, [arrays], core_ids=[0])
    return r.results[0]["out_0_dram"]
```
